# Optimizing a Trainium2 kernel written in Bass

```python
import numpy as np
import jax
import jax.numpy as jnp

def _softmax(x, axis=-1):
    return jax.nn.softmax(x, axis=axis)

def _gelu(x):
    return jax.nn.gelu(x, approximate=True)

def _silu(x):
    return jax.nn.silu(x)

def _sigmoid(x):
    return jax.nn.sigmoid(x)

def _layernorm(x, axis=-1, eps=1e-05):
    m = jnp.mean(x, axis=axis, keepdims=True)
    v = jnp.var(x, axis=axis, keepdims=True)
    return (x - m) / jnp.sqrt(v + eps)

def _scatter_add(tgt, idx, src, axis=0):
    return tgt.at[idx].add(src)

def _segment_sum(src, seg, n):
    return jax.ops.segment_sum(src, seg, n)
kernel_name = 'mk_decoder_postln_d1_seqx_r8_016e7c'

def setup_inputs(seed: int=0):
    np.random.seed(seed)
    _w = jnp.asarray

    def _rec_inputs():
        import jax
        import jax.numpy as jnp
        _rk = jax.random.key(seed)
        x = 0.0003765 + 1 * jax.random.normal(jax.random.fold_in(_rk, 1), (16, 128, 256), jnp.float32)
        _lenS = 128 - jax.random.randint(jax.random.fold_in(_rk, 7), (16,), 0, max(1, 128 // 4) + 1, jnp.int32)
        _lenS2 = 128 - jax.random.randint(jax.random.fold_in(_rk, 8), (16,), 0, max(1, 128 // 4) + 1, jnp.int32)
        _ctx_2048P = jax.random.normal(jax.random.fold_in(_rk, 11), (16, 16, 256), jnp.float32)
        _ctx_2048c = jax.random.dirichlet(jax.random.fold_in(_rk, 511), 0.3 * jnp.ones((16,), jnp.float32), (16, 128))
        _ctx_2048t = jnp.einsum('bsk,bkd->bsd', _ctx_2048c, _ctx_2048P)
        _ctx_2048t = _ctx_2048t * jax.lax.rsqrt(jnp.mean(jnp.square(_ctx_2048t)) + 1e-12) * 0.953939
        ctx_2048 = -0.000292821 + 1.00034 * (_ctx_2048t + 0.3 * jax.random.normal(jax.random.fold_in(_rk, 611), (16, 128, 256), jnp.float32))
        return (x, ctx_2048)
    x, ctx_2048 = _rec_inputs()

    def _L0_attn_setup():
        import jax, jax.numpy as jnp
        import numpy as np
        B, S, HID = (1, 128, 256)
        H, DQK, DV = (16, 128, 128)
        K = 4
        SCALE = DQK ** (-0.5)

        def _dwconv_causal(x_btc, wk, bk, seq):
            y = jax.lax.conv_general_dilated(x_btc.transpose(0, 2, 1), wk, (1,), [(K - 1, K - 1)], dimension_numbers=('NCH', 'OIH', 'NCH'), feature_group_count=wk.shape[0])
            return (y[:, :, :seq] + bk[None, :, None]).transpose(0, 2, 1)

        def _kda_forward(x, Wq, Wk, Wv, Wa, ba, Wb, bb, Wg, Wo, qc_w, qc_b, kc_w, kc_b, vc_w, vc_b, ln_g, ln_b):
            Bb, Ss, _ = x.shape
            q = x @ Wq.T
            k = x @ Wk.T
            v = x @ Wv.T
            q = jax.nn.silu(_dwconv_causal(q, qc_w, qc_b, Ss))
            k = jax.nn.silu(_dwconv_causal(k, kc_w, kc_b, Ss))
            v = jax.nn.silu(_dwconv_causal(v, vc_w, vc_b, Ss))
            q = q.reshape(Bb, Ss, H, DQK)
            k = k.reshape(Bb, Ss, H, DQK) * SCALE
            v = v.reshape(Bb, Ss, H, DV)
            a = jax.nn.sigmoid(x @ Wa.T + ba).reshape(Bb, Ss, H, DV)
            beta = jax.nn.sigmoid(x @ Wb.T + bb)

            def step(St, inp):
                kt, qt, vt, at, bt = inp
                Sk = jnp.einsum('bhij,bhj->bhi', St, kt)
                err = Sk - vt
                Sn = at[..., None] * St - (bt[..., None] * err)[..., None] * kt[:, :, None, :]
                ot = jnp.einsum('bhij,bhj->bhi', Sn, qt)
                return (Sn, ot)
            tfirst = lambda u: u.transpose(1, 0, 2, 3)
            S0 = jnp.zeros((Bb, H, DV, DQK), x.dtype)
            _, outs = jax.lax.scan(step, S0, (tfirst(k), tfirst(q), tfirst(v), tfirst(a), beta.transpose(1, 0, 2)))
            out = outs.transpose(1, 0, 2, 3)
            mu = out.mean(-1, keepdims=True)
            var = out.var(-1, keepdims=True)
            o = (out - mu) * jax.lax.rsqrt(var + 1e-05) * ln_g + ln_b
            g = jax.nn.sigmoid(x @ Wg.T).reshape(Bb, Ss, H, DV)
            o = (o * g).reshape(Bb, Ss, H * DV)
            return o @ Wo.T
        key = jax.random.key(seed)
        ks = jax.random.split(key, 12)
        w = lambda i, shape, sc=0.02: jax.random.normal(ks[i], shape, jnp.float32) * sc
        return dict(x=jax.random.normal(ks[0], (B, S, HID), jnp.float32), Wq=w(1, (H * DQK, HID)), Wk=w(2, (H * DQK, HID)), Wv=w(3, (H * DV, HID)), Wa=w(4, (H * DV, HID)), ba=jnp.zeros((H * DV,), jnp.float32), Wb=w(5, (H, HID)), bb=jnp.zeros((H,), jnp.float32), Wg=w(6, (H * DV, HID)), Wo=w(7, (HID, H * DV)), qc_w=w(8, (H * DQK, 1, K), 0.2), qc_b=jnp.zeros((H * DQK,), jnp.float32), kc_w=w(9, (H * DQK, 1, K), 0.2), kc_b=jnp.zeros((H * DQK,), jnp.float32), vc_w=w(10, (H * DV, 1, K), 0.2), vc_b=jnp.zeros((H * DV,), jnp.float32), ln_g=jnp.ones((DV,), jnp.float32), ln_b=jnp.zeros((DV,), jnp.float32))
    _L0_attn_all = _L0_attn_setup()
    _L0_attn_in = {k: v for k, v in _L0_attn_all.items() if k in ('Wq', 'Wk', 'Wv', 'Wa', 'ba', 'Wb', 'bb', 'Wg', 'Wo', 'qc_w', 'qc_b', 'kc_w', 'kc_b', 'vc_w', 'vc_b', 'ln_g', 'ln_b')}
    del _L0_attn_all

    def _L0_xattn_setup():
        import jax, jax.numpy as jnp
        import numpy as np
        key = jax.random.key(seed)
        k1, k2, k3, k4, k5 = jax.random.split(key, 5)
        B, D_MODEL, L = (2, 128, 256)
        HEAD_DIM = 8
        H = D_MODEL // HEAD_DIM
        return {'k': jax.random.normal(k1, (B, D_MODEL, L), dtype=jnp.float32), 'v': jax.random.normal(k2, (B, D_MODEL, L), dtype=jnp.float32), 'q': jax.random.normal(k3, (B, D_MODEL, L), dtype=jnp.float32), 'ssm_kernel': jax.random.normal(k4, (H, L), dtype=jnp.float32), 'D': jax.random.normal(k5, (H,), dtype=jnp.float32), 'head_dim': HEAD_DIM}
    _L0_xattn_all = _L0_xattn_setup()
    _L0_xattn_in = {k: v for k, v in _L0_xattn_all.items() if k in ('ssm_kernel', 'D')}
    del _L0_xattn_all

    def _L0_ffn_setup():
        import jax, jax.numpy as jnp
        import numpy as np
        TOP_K = 6
        N_GROUP = 8
        TOPK_GROUP = 3
        CAPACITY = 96
        RSF = 1.0
        key = jax.random.key(seed)
        ks = jax.random.split(key, 8)
        B, S, H = (1, 512, 256)
        E, M = (64, 176)
        MS = 352
        sc = 0.02
        return {'hidden_states': jax.random.normal(ks[0], (B, S, H), jnp.float32), 'gate_weight': jax.random.normal(ks[1], (E, H), jnp.float32) * sc, 'Wg': jax.random.normal(ks[2], (E, M, H), jnp.float32) * sc, 'Wu': jax.random.normal(ks[3], (E, M, H), jnp.float32) * sc, 'Wd': jax.random.normal(ks[4], (E, H, M), jnp.float32) * sc, 'Sg': jax.random.normal(ks[5], (MS, H), jnp.float32) * sc, 'Su': jax.random.normal(ks[6], (MS, H), jnp.float32) * sc, 'Sd': jax.random.normal(ks[7], (H, MS), jnp.float32) * sc}
    _L0_ffn_all = _L0_ffn_setup()
    _L0_ffn_in = {k: v for k, v in _L0_ffn_all.items() if k in ('gate_weight', 'Wg', 'Wu', 'Wd', 'Sg', 'Su', 'Sd')}
    del _L0_ffn_all
    return {'x': x, 'ctx_2048': ctx_2048, 'L0_attn_Wq': _L0_attn_in['Wq'], 'L0_attn_Wk': _L0_attn_in['Wk'], 'L0_attn_Wv': _L0_attn_in['Wv'], 'L0_attn_Wa': _L0_attn_in['Wa'], 'L0_attn_ba': _L0_attn_in['ba'], 'L0_attn_Wb': _L0_attn_in['Wb'], 'L0_attn_bb': _L0_attn_in['bb'], 'L0_attn_Wg': _L0_attn_in['Wg'], 'L0_attn_Wo': _L0_attn_in['Wo'], 'L0_attn_qc_w': _L0_attn_in['qc_w'], 'L0_attn_qc_b': _L0_attn_in['qc_b'], 'L0_attn_kc_w': _L0_attn_in['kc_w'], 'L0_attn_kc_b': _L0_attn_in['kc_b'], 'L0_attn_vc_w': _L0_attn_in['vc_w'], 'L0_attn_vc_b': _L0_attn_in['vc_b'], 'L0_attn_ln_g': _L0_attn_in['ln_g'], 'L0_attn_ln_b': _L0_attn_in['ln_b'], 'L0_xattn_ssm_kernel': _L0_xattn_in['ssm_kernel'], 'L0_xattn_D': _L0_xattn_in['D'], 'L0_ffn_gate_weight': _L0_ffn_in['gate_weight'], 'L0_ffn_Wg': _L0_ffn_in['Wg'], 'L0_ffn_Wu': _L0_ffn_in['Wu'], 'L0_ffn_Wd': _L0_ffn_in['Wd'], 'L0_ffn_Sg': _L0_ffn_in['Sg'], 'L0_ffn_Su': _L0_ffn_in['Su'], 'L0_ffn_Sd': _L0_ffn_in['Sd']}

def reference(x, ctx_2048, L0_attn_Wq, L0_attn_Wk, L0_attn_Wv, L0_attn_Wa, L0_attn_ba, L0_attn_Wb, L0_attn_bb, L0_attn_Wg, L0_attn_Wo, L0_attn_qc_w, L0_attn_qc_b, L0_attn_kc_w, L0_attn_kc_b, L0_attn_vc_w, L0_attn_vc_b, L0_attn_ln_g, L0_attn_ln_b, L0_xattn_ssm_kernel, L0_xattn_D, L0_ffn_gate_weight, L0_ffn_Wg, L0_ffn_Wu, L0_ffn_Wd, L0_ffn_Sg, L0_ffn_Su, L0_ffn_Sd):
    import jax
    import jax.numpy as jnp

    def _L0_attn_ref(x, Wq, Wk, Wv, Wa, ba, Wb, bb, Wg, Wo, qc_w, qc_b, kc_w, kc_b, vc_w, vc_b, ln_g, ln_b):
        import jax, jax.numpy as jnp
        import numpy as np
        B, S, HID = (1, 128, 256)
        H, DQK, DV = (16, 128, 128)
        K = 4
        SCALE = DQK ** (-0.5)

        def _dwconv_causal(x_btc, wk, bk, seq):
            y = jax.lax.conv_general_dilated(x_btc.transpose(0, 2, 1), wk, (1,), [(K - 1, K - 1)], dimension_numbers=('NCH', 'OIH', 'NCH'), feature_group_count=wk.shape[0])
            return (y[:, :, :seq] + bk[None, :, None]).transpose(0, 2, 1)

        def _kda_forward(x, Wq, Wk, Wv, Wa, ba, Wb, bb, Wg, Wo, qc_w, qc_b, kc_w, kc_b, vc_w, vc_b, ln_g, ln_b):
            Bb, Ss, _ = x.shape
            q = x @ Wq.T
            k = x @ Wk.T
            v = x @ Wv.T
            q = jax.nn.silu(_dwconv_causal(q, qc_w, qc_b, Ss))
            k = jax.nn.silu(_dwconv_causal(k, kc_w, kc_b, Ss))
            v = jax.nn.silu(_dwconv_causal(v, vc_w, vc_b, Ss))
            q = q.reshape(Bb, Ss, H, DQK)
            k = k.reshape(Bb, Ss, H, DQK) * SCALE
            v = v.reshape(Bb, Ss, H, DV)
            a = jax.nn.sigmoid(x @ Wa.T + ba).reshape(Bb, Ss, H, DV)
            beta = jax.nn.sigmoid(x @ Wb.T + bb)

            def step(St, inp):
                kt, qt, vt, at, bt = inp
                Sk = jnp.einsum('bhij,bhj->bhi', St, kt)
                err = Sk - vt
                Sn = at[..., None] * St - (bt[..., None] * err)[..., None] * kt[:, :, None, :]
                ot = jnp.einsum('bhij,bhj->bhi', Sn, qt)
                return (Sn, ot)
            tfirst = lambda u: u.transpose(1, 0, 2, 3)
            S0 = jnp.zeros((Bb, H, DV, DQK), x.dtype)
            _, outs = jax.lax.scan(step, S0, (tfirst(k), tfirst(q), tfirst(v), tfirst(a), beta.transpose(1, 0, 2)))
            out = outs.transpose(1, 0, 2, 3)
            mu = out.mean(-1, keepdims=True)
            var = out.var(-1, keepdims=True)
            o = (out - mu) * jax.lax.rsqrt(var + 1e-05) * ln_g + ln_b
            g = jax.nn.sigmoid(x @ Wg.T).reshape(Bb, Ss, H, DV)
            o = (o * g).reshape(Bb, Ss, H * DV)
            return o @ Wo.T
        return _kda_forward(x, Wq, Wk, Wv, Wa, ba, Wb, bb, Wg, Wo, qc_w, qc_b, kc_w, kc_b, vc_w, vc_b, ln_g, ln_b)

    def _L0_xattn_ref(k, v, q, ssm_kernel, D, head_dim):
        import jax, jax.numpy as jnp
        import numpy as np
        B, HD, L = k.shape
        H = HD // head_dim
        fft_size = 2 * L
        k_ = k.reshape(B, H, head_dim, L)
        v_ = v.reshape(B, H, head_dim, L)
        q_ = q.reshape(B, H, head_dim, L)
        kv = jnp.einsum('bhil,bhjl->bijhl', k_, v_)
        kv_f = jnp.fft.rfft(kv, n=fft_size)
        kernel_f = jnp.fft.rfft(ssm_kernel, n=fft_size)
        y = jnp.fft.irfft(kv_f * kernel_f, n=fft_size)[..., :L]
        out = y + kv * D[None, None, None, :, None]
        out = jnp.einsum('bijhl,bhil->bjhl', out, q_)
        out = jnp.transpose(out, (0, 2, 1, 3)).reshape(B, H * head_dim, L)
        return out.astype(k.dtype)

    def _L0_ffn_ref(hidden_states, gate_weight, Wg, Wu, Wd, Sg, Su, Sd):
        import jax, jax.numpy as jnp
        import numpy as np
        TOP_K = 6
        N_GROUP = 8
        TOPK_GROUP = 3
        CAPACITY = 96
        RSF = 1.0
        B, S, H = hidden_states.shape
        E, M, _ = Wg.shape
        K, NG, TG, C = (TOP_K, N_GROUP, TOPK_GROUP, CAPACITY)
        x = hidden_states.reshape(-1, H)
        T = x.shape[0]
        logits = x.astype(jnp.float32) @ gate_weight.astype(jnp.float32).T
        scores = jax.nn.softmax(logits, axis=-1)
        group_scores = scores.reshape(T, NG, E // NG).max(axis=-1)
        _, gidx = jax.lax.top_k(group_scores, TG)
        gmask = jnp.zeros((T, NG), scores.dtype).at[jnp.arange(T)[:, None], gidx].set(1.0)
        smask = jnp.repeat(gmask, E // NG, axis=1)
        tmp_scores = jnp.where(smask > 0, scores, 0.0)
        topk_w, topk_i = jax.lax.top_k(tmp_scores, K)
        topk_w = topk_w * RSF
        flat = topk_i.reshape(-1)
        oh = jax.nn.one_hot(flat, E, dtype=jnp.int32)
        pos = jnp.sum(jnp.cumsum(oh, axis=0) * oh, axis=-1) - 1
        slot = flat * C + jnp.minimum(pos, C - 1)
        tok = jnp.arange(T * K) // K
        buf = jnp.zeros((E * C, H), x.dtype).at[slot].set(x[tok]).reshape(E, C, H)
        g = jnp.einsum('ech,emh->ecm', buf, Wg)
        u = jnp.einsum('ech,emh->ecm', buf, Wu)
        out = jnp.einsum('ecm,ehm->ech', jax.nn.silu(g) * u, Wd).reshape(E * C, H)
        yk = out[slot].reshape(T, K, H)
        y = jnp.sum(yk * topk_w[..., None].astype(yk.dtype), axis=1)
        shared = jax.nn.silu(x @ Sg.T) * (x @ Su.T) @ Sd.T
        return (y + shared).reshape(B, S, H)
    x = _layernorm(x + _L0_attn_ref(x, L0_attn_Wq, L0_attn_Wk, L0_attn_Wv, L0_attn_Wa, L0_attn_ba, L0_attn_Wb, L0_attn_bb, L0_attn_Wg, L0_attn_Wo, L0_attn_qc_w, L0_attn_qc_b, L0_attn_kc_w, L0_attn_kc_b, L0_attn_vc_w, L0_attn_vc_b, L0_attn_ln_g, L0_attn_ln_b), axis=-1)
    x = _layernorm(x + _L0_xattn_ref(ctx_2048, ctx_2048, x, L0_xattn_ssm_kernel, L0_xattn_D, 8), axis=-1)
    x = _layernorm(x + _L0_ffn_ref(x, L0_ffn_gate_weight, L0_ffn_Wg, L0_ffn_Wu, L0_ffn_Wd, L0_ffn_Sg, L0_ffn_Su, L0_ffn_Sd), axis=-1)
    return x

_drawn_inputs = setup_inputs


def setup_inputs(seed=0):
    import zlib

    import numpy as np

    out = dict(_drawn_inputs(seed))
    spreads = {'L0_attn_ba': (0.0, 0.8),
     'L0_attn_bb': (0.0, 0.8),
     'L0_attn_qc_b': (0.0, 0.1),
     'L0_attn_kc_b': (0.0, 0.1),
     'L0_attn_vc_b': (0.0, 0.1),
     'L0_attn_ln_g': (1.0, 0.6),
     'L0_attn_ln_b': (0.0, 0.1)}
    factors = {'L0_attn_Wa': 8.0,
     'L0_attn_Wb': 6.697,
     'L0_attn_Wg': 4.806,
     'L0_ffn_gate_weight': 8.0,
     'L0_ffn_Wg': 8.0,
     'L0_ffn_Wu': 8.0,
     'L0_ffn_Wd': 8.0,
     'L0_ffn_Sg': 2.891,
     'L0_ffn_Su': 2.846,
     'L0_ffn_Sd': 2.855}
    for name, (base, spread) in spreads.items():
        noise = np.random.default_rng([zlib.crc32(name.encode()), seed]).standard_normal(out[name].shape)
        drawn = base * np.exp(spread * noise) if base else spread * noise
        out[name] = jnp.asarray(drawn.astype(out[name].dtype))
    for name, factor in factors.items():
        out[name] = (out[name] * factor).astype(out[name].dtype)
    return out
```

```python
from contextlib import ExitStack

import concourse.bass as bass
import numpy as np
from concourse import mybir

FP32 = mybir.dt.float32
INT32 = mybir.dt.int32
UINT32 = mybir.dt.uint32
ALU = mybir.AluOpType
ACT = mybir.ActivationFunctionType
AXIS_X = mybir.AxisListType.X

P = 128
B, T, D = 16, 128, 256
H, DH = 16, 128
KT = D // P
TOK = B * T
TAPS = 4
EPS = 1e-5
DMA = 16
C = 16
NCHUNK = T // C
HK, HD2 = 16, 8
E, M, TOPK, GROUPS, TOPG, CAP = 64, 176, 6, 8, 3, 96
MS = 352
SLOTS = E * CAP


class Pool:

    def __init__(self, nc, ctx):
        self.nc, self.ctx = nc, ctx

    def sb(self, name, shape, dt=FP32):
        return self.ctx.enter_context(self.nc.sbuf_tensor(name, shape, dt))

    def ps(self, name, shape):
        return self.ctx.enter_context(self.nc.psum_tensor(name, shape, FP32))

    def sem(self, name):
        return self.ctx.enter_context(self.nc.semaphore(name))


def projections(nc, xT, w_heads, ba, wbT, bb_col, bb_row, a_dram, bv_dram, gram_dram, beta_dram):
    QB = 4
    NQ = B // QB
    KINDS = 3
    UNITS = NQ * KINDS
    K_SCALE, Q_SCALE = 1.0 / DH, float(DH) ** -0.5
    with ExitStack() as ctx:
        m = Pool(nc, ctx)
        x_sb = m.sb("p1_x", [P, KT, TOK])
        head_sb = [m.sb(f"p1_w{i}", [P, KT * 4 * P + KINDS * (TAPS + 1)]) for i in range(2)]
        w_sb = [t[:, 0:KT * 4 * P].rearrange("p (k s c) -> p k s c", k=KT, s=4) for t in head_sb]
        par = [t[:, KT * 4 * P:].rearrange("p (s x) -> p s x", s=KINDS) for t in head_sb]
        ba_sb = m.sb("p1_ba", [1, H * P])
        wb_sb = m.sb("p1_wb", [P, KT, H])
        bbc_sb = m.sb("p1_bbc", [H, 1])
        bbr_sb = m.sb("p1_bbr", [1, H])
        ones = m.sb("p1_ones", [1, P])
        ident = m.sb("p1_ident", [P, P])
        beta_t = m.sb("p1_beta_t", [P, B, H])
        beta_h = m.sb("p1_beta_h", [H, TOK])
        y = [m.sb(f"p1_y{i}", [P, QB * T]) for i in range(4)]
        sig = [m.sb(f"p1_sig{i}", [P, QB * T]) for i in range(2)]
        kq = [m.sb(f"p1_kq{i}", [P, QB, 2, T]) for i in range(2)]
        v = [m.sb(f"p1_v{i}", [P, QB, T]) for i in range(2)]
        gram = [m.sb(f"p1_gram{i}", [P, QB, NCHUNK, 2, C]) for i in range(2)]
        bv = [m.sb(f"p1_bv{i}", [P, QB, P]) for i in range(2)]
        dec = [m.sb(f"p1_dec{i}", [P, QB, P]) for i in range(2)]
        ps_proj = [m.ps(f"p1_ps_proj{i}", [P, QB * T]) for i in range(4)]
        ps_gram = m.ps("p1_ps_gram", [P, QB, 2 * T])
        ps_v = m.ps("p1_ps_v", [P, QB, P])
        ps_a = m.ps("p1_ps_a", [P, QB, P])

        consts = m.sem("p1_consts")
        w_loaded = [m.sem(f"p1_w_loaded{i}") for i in range(2)]
        made = m.sem("p1_made")
        beta_mm = m.sem("p1_beta_mm")
        beta_sig = m.sem("p1_beta_sig")
        beta_out = m.sem("p1_beta_out")
        proj_done = m.sem("p1_proj_done")
        y_init = m.sem("p1_y_init")
        tap = m.sem("p1_tap")
        conv_done = m.sem("p1_conv_done")
        sig_done = m.sem("p1_sig_done")
        silu_done = m.sem("p1_silu_done")
        gram_done = m.sem("p1_gram_done")
        a_done = m.sem("p1_a_done")
        gram_k_cp, gram_q_cp = m.sem("p1_gram_k_cp"), m.sem("p1_gram_q_cp")
        bv_cp = m.sem("p1_bv_cp")
        a_cp = m.sem("p1_a_cp")
        gram_out, bv_out, a_out = ([m.sem(f"p1_{n}_out{i}") for i in range(2)] for n in ("gram", "bv", "a"))
        block = ctx.enter_context(nc.Block())

        @block.sync
        def _(sp):
            sp.dma_start(x_sb[:], xT.rearrange("(k p) t -> p k t", p=P)).then_inc(consts, DMA)
            sp.dma_start(wb_sb[:], wbT.rearrange("(k p) h -> p k h", p=P)).then_inc(consts, DMA)
            sp.dma_start(bbc_sb[:], bb_col).then_inc(consts, DMA)
            sp.dma_start(bbr_sb[:], bb_row).then_inc(consts, DMA)
            sp.dma_start(ba_sb[:], ba).then_inc(consts, DMA)
            sp.wait_ge(beta_sig, 2)
            sp.dma_start(beta_dram.rearrange("b h t -> h b t"),
                         beta_h[:].rearrange("h (b t) -> h b t", b=B)).then_inc(beta_out, DMA)
            with sp.Fori(0, H // 2) as hp:
                for j in range(2):
                    h = hp * 2 + j
                    for n in range(NQ):
                        i = n % 2
                        at = hp * (2 * NQ) + j * NQ + n + 1
                        b0 = n * QB
                        sp.wait_ge(a_cp, at)
                        sp.dma_start(a_dram[b0:b0 + QB, bass.ds(h, 1), :, :].rearrange("b h t i -> t (b h) i"),
                                     dec[i][:]).then_inc(a_out[i], DMA)
                        sp.wait_ge(bv_cp, at)
                        sp.dma_start(bv_dram[b0:b0 + QB, bass.ds(h, 1), :, :].rearrange("b h t i -> t (b h) i"),
                                     bv[i][:]).then_inc(bv_out[i], DMA)
                        sp.wait_ge(gram_k_cp, at)
                        sp.wait_ge(gram_q_cp, at)
                        sp.dma_start(gram_dram[b0:b0 + QB, bass.ds(h, 1), :, :].rearrange("b h t i -> t (b h) i"),
                                     gram[i][:].rearrange("p b c s e -> p b (c s e)")).then_inc(gram_out[i], DMA)
            sp.wait_ge(beta_out, DMA)
            for i in range(2):
                sp.wait_ge(a_out[i], DMA * H * NQ // 2)
            for i in range(2):
                sp.wait_ge(bv_out[i], DMA * H * NQ // 2)
            for i in range(2):
                sp.wait_ge(gram_out[i], DMA * H * NQ // 2)

        @block.gpsimd
        def _(pool):
            nc.gpsimd.memset(ones[:], 1.0).then_inc(made, 1)
            nc.gpsimd.memset(ident[:], 0.0).then_inc(made, 1)
            pool.wait_ge(made, 2)
            nc.gpsimd.affine_select(out=ident[:], in_=ident[:], compare_op=ALU.not_equal, fill=1.0, base=0,
                                    pattern=[[-1, P]], channel_multiplier=1).then_inc(made, 1)
            for j in range(2):
                pool.dma_start(head_sb[j][:], w_heads[j]).then_inc(w_loaded[j], DMA)
            with pool.Fori(0, H // 2) as hp:
                for j in range(2):
                    for u in range(UNITS):
                        n, kind = divmod(u, KINDS)
                        at = hp * (2 * UNITS) + j * UNITS + u + 1
                        pool.wait_ge(sig_done, at)
                        if j == 1 or n >= 2:
                            pool.wait_ge(gram_done, hp * (2 * NQ) + j * NQ + n - 1)
                        dst = v[n % 2][:].rearrange("p b t -> p b t") if kind == 2 else kq[n % 2][:, :, kind, :]
                        nc.gpsimd.tensor_tensor(out=dst, in0=y[u % 4][:].rearrange("p (b t) -> p b t", b=QB),
                                                in1=sig[u % 2][:].rearrange("p (b t) -> p b t", b=QB),
                                                op=ALU.mult).then_inc(silu_done, 1)
                    pool.wait_ge(a_done, hp * (2 * NQ) + (j + 1) * NQ)
                    pool.wait_ge(conv_done, hp * (2 * UNITS) + (j + 1) * UNITS)
                    pool.dma_start(head_sb[j][:], w_heads[bass.ds((hp * 2 + (j + 2)) % H, 1)]
                                   .rearrange("a p x -> p (a x)")).then_inc(w_loaded[j], DMA)
            for j in range(2):
                pool.wait_ge(w_loaded[j], DMA * (H // 2 + 1))

        @block.tensor
        def _(pe):
            pe.wait_ge(consts, DMA * 5)
            pe.wait_ge(made, 3)
            for q in range(NQ):
                for k in range(KT):
                    nc.tensor.matmul(ps_proj[q][0:H, :], wb_sb[:, k, :], x_sb[:, k, q * 512:(q + 1) * 512],
                                     start=(k == 0), stop=(k == KT - 1))
            for b in range(B):
                for k in range(KT):
                    nc.tensor.matmul(ps_gram[:, 0, b * H:(b + 1) * H],
                                     x_sb[:, k, b * T:(b + 1) * T], wb_sb[:, k, :], start=(k == 0), stop=False)
                last = nc.tensor.matmul(ps_gram[:, 0, b * H:(b + 1) * H], ones[:], bbr_sb[:], start=False, stop=True)
            last.then_inc(beta_mm, 1)
            pe.wait_ge(beta_sig, 2)

            def project(hp, j, n):
                for kind in range(KINDS):
                    u = n * KINDS + kind
                    if j == 1 or u >= 4:
                        pe.wait_ge(conv_done, hp * (2 * UNITS) + j * UNITS + u - 3)
                    else:
                        pe.wait_ge(conv_done, hp * (2 * UNITS))
                    for k in range(KT):
                        last = nc.tensor.matmul(ps_proj[u % 4][:], w_sb[j][:, k, kind, :],
                                                x_sb[:, k, n * 512:(n + 1) * 512], start=(k == 0), stop=(k == KT - 1))
                    last.then_inc(proj_done, 1)

            def decays(hp, j, n):
                h = hp * 2 + j
                pe.wait_ge(a_cp, hp * (2 * NQ) + j * NQ + n)
                for b in range(QB):
                    t0 = (n * QB + b) * T
                    for k in range(KT):
                        nc.tensor.matmul(ps_a[:, b, :], x_sb[:, k, t0:t0 + T], w_sb[j][:, k, 3, :],
                                         start=(k == 0), stop=False)
                    last = nc.tensor.matmul(ps_a[:, b, :], ones[:], ba_sb[:, bass.ds(h * P, P)], start=False, stop=True)
                last.then_inc(a_done, 1)

            def grams(hp, j, n):
                at = hp * (2 * NQ) + j * NQ + n
                pe.wait_ge(silu_done, hp * (2 * UNITS) + j * UNITS + (n + 1) * KINDS)
                pe.wait_ge(gram_k_cp, at)
                pe.wait_ge(gram_q_cp, at)
                pe.wait_ge(bv_cp, at)
                for b in range(QB):
                    nc.tensor.matmul(ps_gram[:, b, :], kq[n % 2][:, b, 0, :],
                                     kq[n % 2][:, b, :, :].rearrange("p s t -> p (s t)"), start=True, stop=True)
                for b in range(QB):
                    last = nc.tensor.transpose(ps_v[:, b, :], v[n % 2][:, b, :], ident[:])
                last.then_inc(gram_done, 1)

            with pe.Fori(0, H // 2) as hp:
                for j in range(2):
                    pe.wait_ge(w_loaded[j], hp * DMA + DMA)
                    project(hp, j, 0)
                    for n in range(NQ):
                        if n + 1 < NQ:
                            project(hp, j, n + 1)
                        decays(hp, j, n)
                        grams(hp, j, n)

        @block.scalar
        def _(act):
            act.wait_ge(beta_mm, 1)
            for q in range(NQ):
                last = nc.scalar.activation(beta_h[:, q * 512:(q + 1) * 512], ps_proj[q][0:H, :], ACT.Sigmoid,
                                            bias=bbc_sb[:, 0:1])
            last.then_inc(beta_sig, 1)
            nc.scalar.activation(beta_t[:].rearrange("p b h -> p (b h)"), ps_gram[:, 0, :], ACT.Sigmoid).then_inc(beta_sig, 1)

            def first_tap(hp, j, u):
                h = hp * 2 + j
                kind = u % KINDS
                at = hp * (2 * UNITS) + j * UNITS + u
                act.wait_ge(proj_done, at + 1)
                if j == 1 or u >= 4:
                    act.wait_ge(silu_done, at - 3)
                else:
                    act.wait_ge(silu_done, hp * (2 * UNITS))
                nc.scalar.activation(y[u % 4][:], ps_proj[u % 4][:], ACT.Identity,
                                     bias=par[j][:, kind, TAPS:TAPS + 1],
                                     scale=par[j][:, kind, TAPS - 1:TAPS]).then_inc(y_init, 1)

            def sigmoid(hp, j, u):
                at = hp * (2 * UNITS) + j * UNITS + u
                act.wait_ge(conv_done, at + 1)
                if j == 1 or u >= 2:
                    act.wait_ge(silu_done, at - 1)
                else:
                    act.wait_ge(silu_done, hp * (2 * UNITS))
                nc.scalar.activation(sig[u % 2][:], y[u % 4][:], ACT.Sigmoid).then_inc(sig_done, 1)

            def copies(hp, j, n):
                at = hp * (2 * NQ) + j * NQ + n
                i = n % 2
                act.wait_ge(a_out[i], hp * (NQ * DMA) + (j * NQ + n) // 2 * DMA)
                act.wait_ge(a_done, at + 1)
                nc.scalar.activation(dec[i][:], ps_a[:], ACT.Sigmoid).then_inc(a_cp, 1)
                act.wait_ge(gram_out[i], hp * (NQ * DMA) + (j * NQ + n) // 2 * DMA)
                act.wait_ge(gram_done, at + 1)
                for half, scale, done in ((0, K_SCALE, gram_k_cp), (1, Q_SCALE, gram_q_cp)):
                    nc.scalar.activation(gram[i][:, :, :, half, :],
                                         ps_gram[:, :, half * T:(half + 1) * T].rearrange("p b (c s) -> p b c s", c=NCHUNK),
                                         ACT.Copy, scale=scale).then_inc(done, 1)

            with act.Fori(0, H // 2) as hp:
                for j in range(2):
                    for u in range(KINDS):
                        first_tap(hp, j, u)
                    for n in range(NQ):
                        for kind in range(KINDS):
                            sigmoid(hp, j, n * KINDS + kind)
                            if n + 1 < NQ:
                                first_tap(hp, j, (n + 1) * KINDS + kind)
                        copies(hp, j, n)

        @block.vector
        def _(dve):
            dve.wait_ge(beta_sig, 2)
            with dve.Fori(0, H // 2) as hp:
                for j in range(2):
                    h = hp * 2 + j

                    def conv(u):
                        kind = u % KINDS
                        at = hp * (2 * UNITS) + j * UNITS + u
                        dve.wait_ge(y_init, at + 1)
                        yv = y[u % 4][:].rearrange("p (b t) -> p b t", b=QB)
                        pv = ps_proj[u % 4][:].rearrange("p (b t) -> p b t", b=QB)
                        for s in range(1, TAPS):
                            if s > 1:
                                dve.wait_ge(tap, at * 2 + s - 1)
                            nc.vector.scalar_tensor_tensor(
                                out=yv[:, :, s:], in0=pv[:, :, 0:T - s],
                                scalar=par[j][:, kind, TAPS - 1 - s:TAPS - s],
                                in1=yv[:, :, s:], op0=ALU.mult, op1=ALU.add).then_inc(
                                    tap if s < TAPS - 1 else conv_done, 1)

                    for u in range(KINDS):
                        conv(u)
                    for n in range(NQ):
                        for kind in range(KINDS):
                            if n + 1 < NQ:
                                conv((n + 1) * KINDS + kind)
                        at = hp * (2 * NQ) + j * NQ + n
                        dve.wait_ge(gram_done, at + 1)
                        dve.wait_ge(bv_out[n % 2], hp * (NQ * DMA) + (j * NQ + n) // 2 * DMA)
                        for b in range(QB):
                            last = nc.vector.tensor_scalar(
                                bv[n % 2][:, b, :], ps_v[:, b, :],
                                beta_t[:, n * QB + b, bass.ds(h, 1)], None, ALU.mult)
                        last.then_inc(bv_cp, 1)


def recurrence(nc, a_dram, bv_dram, gram_dram, beta_dram, hist_dram, o_dram):
    GR = 2
    BG = B // GR
    HU = H // 2
    UNITS = BG * 2
    OLD = T - 2 * C
    SPANS = ((0, 2, C), (2, 4, 3 * C), (4, NCHUNK - 1, OLD))
    with ExitStack() as ctx:
        m = Pool(nc, ctx)
        hist = [m.sb(f"p2_hist{g}", [P, OLD, DH]) for g in range(GR)]
        zo = [m.sb(f"p2_zo{g}", [P, 2, C, DH]) for g in range(GR)]
        dec = [m.sb(f"p2_dec{g}", [P, C, DH]) for g in range(GR)]
        bv = [m.sb(f"p2_bv{g}", [P, C, DH]) for g in range(GR)]
        gd = [m.sb(f"p2_gd{g}", [P, C, 2 * C]) for g in range(GR)]
        beta = [m.sb(f"p2_beta{g}", [P, C]) for g in range(GR)]
        w = [m.sb(f"p2_w{g}", [P, C + 1, DH]) for g in range(GR)]
        turned = [m.sb(f"p2_turned{i}", [C + OLD, HU, DH]) for i in range(2)]
        gcol = [m.sb(f"p2_gcol{i}", [C + OLD, HU, 2 * C]) for i in range(2)]
        z_turn = m.sb("p2_z_turn", [DH, P, 2 * C])
        ident = m.sb("p2_ident", [P, P])
        ps_z = [m.ps(f"p2_ps_z{i}", [DH, H, 2 * C]) for i in range(2)]
        ps_t = [m.ps(f"p2_ps_t{i}", [P, 4, DH]) for i in range(4)]

        zo_zero = m.sem("p2_zo_zero")
        cleared = m.sem("p2_cleared")
        leaf_in = [m.sem(f"p2_leaf_in{g}") for g in range(GR)]
        step_done = m.sem("p2_step_done")
        leaf_done = [m.sem(f"p2_leaf_done{g}") for g in range(GR)]
        o_out = [m.sem(f"p2_o_out{g}") for g in range(GR)]
        hist_done = [m.sem(f"p2_hist_done{g}") for g in range(GR)]
        kept = [m.sem(f"p2_kept{g}") for g in range(GR)]
        turned_in = [m.sem(f"p2_turned_in{i}") for i in range(2)]
        mm_done = m.sem("p2_mm_done")
        hist_saved = [m.sem(f"p2_hist_saved{g}") for g in range(GR)]
        z_cp = m.sem("p2_z_cp")
        t_done = m.sem("p2_t_done")
        t_cp = m.sem("p2_t_cp")
        zo_ready = [m.sem(f"p2_zo_ready{g}") for g in range(GR)]
        block = ctx.enter_context(nc.Block())
        NLOAD = 4
        TD = 3
        TB = 2 * C // 4
        STEPS = sum(1 + s for s in range(1, C)) + sum(2 + s for s in range(C)) + 2 * C

        def seq_rows(dram, g, c):
            return dram[g * BG:(g + 1) * BG, :, bass.ds(c * C, C), :].rearrange("b h t i -> (b h) t i")

        @block.vector
        def _(dve):
            for g in range(GR):
                nc.vector.memset(zo[g][:], 0.0).then_inc(zo_zero, 1)

            def chunk(c, g):
                base = c * (GR * STEPS) + g * STEPS
                count = [0]

                def done(ins):
                    count[0] += 1
                    ins.then_inc(step_done, 1)
                    return count[0]

                def after(n):
                    if n:
                        dve.wait_ge(step_done, base + n)

                dve.wait_ge(leaf_in[g], c * (NLOAD * DMA) + NLOAD * DMA)
                dve.wait_ge(zo_ready[g], c)
                dve.wait_ge(kept[g], c)
                dve.wait_ge(zo_zero, GR)
                w_at = z_at = o_at = u_at = 0
                for s in range(C + 1):
                    for r in range(-1, s):
                        if 0 < s < C:
                            after(max(z_at, w_at))
                            if r < 0:
                                z_at = done(nc.vector.tensor_tensor(out=zo[g][:, 0, s, :], in0=zo[g][:, 0, s, :],
                                                                    in1=w[g][:, 0, :], op=ALU.mult))
                            else:
                                z_at = done(nc.vector.scalar_tensor_tensor(
                                    out=zo[g][:, 0, s, :], in0=w[g][:, 1 + r, :], scalar=gd[g][:, r, s:s + 1],
                                    in1=zo[g][:, 0, s, :], op0=ALU.mult, op1=ALU.add))
                        if s > 0:
                            after(max(o_at, w_at, u_at))
                            if r < 0:
                                o_at = done(nc.vector.tensor_tensor(out=zo[g][:, 1, s - 1, :], in0=zo[g][:, 1, s - 1, :],
                                                                    in1=w[g][:, 0, :], op=ALU.mult))
                            else:
                                o_at = done(nc.vector.scalar_tensor_tensor(
                                    out=zo[g][:, 1, s - 1, :], in0=w[g][:, 1 + r, :],
                                    scalar=gd[g][:, r, C + s - 1:C + s], in1=zo[g][:, 1, s - 1, :],
                                    op0=ALU.mult, op1=ALU.add))
                    if s < C:
                        after(z_at)
                        u_at = done(nc.vector.scalar_tensor_tensor(
                            out=w[g][:, 1 + s, :], in0=zo[g][:, 0, s, :], scalar=beta[g][:, s:s + 1],
                            in1=bv[g][:, s, :], op0=ALU.mult, op1=ALU.subtract, reverse1=True))
                        after(max(z_at, o_at))
                        if s == 0:
                            w_at = done(nc.vector.tensor_copy(w[g][:, 0, :], dec[g][:, 0, :]))
                        else:
                            w_at = done(nc.vector.tensor_tensor(
                                out=w[g][:, 0:1 + s, :], in0=w[g][:, 0:1 + s, :],
                                in1=dec[g][:, s:s + 1, :].broadcast_to([P, 1 + s, DH]), op=ALU.mult))
                assert count[0] == STEPS
                after(count[0])
                dve.sem_inc(leaf_done[g], 1)

            with dve.Fori(0, NCHUNK) as c:
                for g in range(GR):
                    chunk(c, g)

        @block.gpsimd
        def _(pool):
            for g in range(GR):
                nc.gpsimd.memset(hist[g][:], 0.0).then_inc(cleared, 1)
            nc.gpsimd.memset(ident[:], 0.0).then_inc(cleared, 1)
            pool.wait_ge(cleared, GR + 1)
            nc.gpsimd.affine_select(out=ident[:], in_=ident[:], compare_op=ALU.not_equal, fill=1.0, base=0,
                                    pattern=[[-1, P]], channel_multiplier=1).then_inc(cleared, 1)

            def load(c, g):
                for dst, dram in ((dec[g], a_dram), (bv[g], bv_dram)):
                    pool.dma_start(dst[:], seq_rows(dram, g, c)).then_inc(leaf_in[g], DMA)
                pool.dma_start(gd[g][:], gram_dram[g * BG:(g + 1) * BG, :, bass.ds(c * C, C), bass.ds(c * (2 * C), 2 * C)]
                               .rearrange("b h t e -> (b h) t e")).then_inc(leaf_in[g], DMA)
                pool.dma_start(beta[g][:], beta_dram[g * BG:(g + 1) * BG, :, bass.ds(c * C, C)]
                               .rearrange("b h t -> (b h) t")).then_inc(leaf_in[g], DMA)

            def store(c, g):
                pool.dma_start(seq_rows(o_dram, g, c)[:, :, 0:DH], zo[g][:, 1]).then_inc(o_out[g], DMA)

            for g in range(GR):
                load(0, g)
            pool.wait_ge(cleared, GR + 2)
            for c0, c1, old in SPANS:
                with pool.Fori(c0, c1) as c:
                    for g in range(GR):
                        pool.wait_ge(leaf_done[g], c + 1)
                        store(c, g)
                        load(c + 1, g)
                        pool.wait_ge(kept[g], c)
                        nc.gpsimd.tensor_tensor(out=hist[g][:, 0:old], in0=hist[g][:, 0:old],
                                                in1=w[g][:, 0:1, :].broadcast_to([P, old, DH]),
                                                op=ALU.mult).then_inc(hist_done[g], 1)
            for g in range(GR):
                pool.wait_ge(leaf_done[g], NCHUNK)
                store(NCHUNK - 1, g)
            for g in range(GR):
                pool.wait_ge(o_out[g], DMA * NCHUNK)

        @block.sync
        def _(sp):
            for c0, c1, old in SPANS:
                with sp.Fori(c0, c1) as c:
                    row0, col0 = sp.snap(c * C), sp.snap((c + 1) * (2 * C))
                    for g in range(GR):
                        sp.wait_ge(leaf_done[g], c + 1)
                        sp.dma_start(hist_dram[g, :, 0:C, :], w[g][:, 1:, :]).then_inc(hist_saved[g], DMA)
                        sp.wait_ge(hist_done[g], c + 1)
                        sp.dma_start(hist_dram[g, :, C:C + old, :], hist[g][:, 0:old]).then_inc(hist_saved[g], DMA)
                        for u in range(UNITS):
                            n = g * UNITS + u
                            i = n % 2
                            b, h0 = u // 2, u % 2 * HU
                            sp.wait_ge(mm_done, c * (GR * UNITS) + max(n - 1, 0))
                            sp.dma_start(gcol[i][0:C], gram_dram[g * BG + b, h0:h0 + HU, bass.ds(row0, C), bass.ds(col0, 2 * C)]
                                         .rearrange("h r e -> r h e")).then_inc(turned_in[i], DMA)
                            sp.dma_start(gcol[i][C:C + old], gram_dram[g * BG + b, h0:h0 + HU, 0:old, bass.ds(col0, 2 * C)]
                                         .rearrange("h r e -> r h e")).then_inc(turned_in[i], DMA)
                            if u == 0:
                                sp.wait_ge(hist_saved[g], c * (2 * DMA) + 2 * DMA)
                            sp.dma_start(turned[i][0:C + old], hist_dram[g, u * HU:(u + 1) * HU, 0:C + old].rearrange("h r i -> r h i")).then_inc(turned_in[i], DMA)

        @block.tensor
        def _(pe):
            pe.wait_ge(cleared, GR + 2)
            for c0, c1, old in SPANS:
                with pe.Fori(c0, c1) as c:
                    for g in range(GR):
                        for u in range(UNITS):
                            n = g * UNITS + u
                            i = n % 2
                            k = g * BG + u // 2
                            pe.wait_ge(turned_in[i], c * (GR * UNITS // 2 * TD * DMA) + (n // 2 + 1) * TD * DMA)
                            pe.wait_ge(z_cp, c * (GR * BG) + k - 1 if k >= 2 else c * (GR * BG))
                            for h in range(HU):
                                last = nc.tensor.matmul(ps_z[k % 2][:, u % 2 * HU + h, :], turned[i][0:C + old, h, :],
                                                        gcol[i][0:C + old, h, :],
                                                        start=True, stop=True)
                            last.then_inc(mm_done, 1)
                        pe.wait_ge(z_cp, c * (GR * BG) + (g + 1) * BG)
                        for t in range(TB):
                            k = g * TB + t
                            pe.wait_ge(t_cp, c * (GR * TB) + k - 3 if k >= 4 else c * (GR * TB))
                            for e in range(4):
                                last = nc.tensor.transpose(ps_t[t % 4][:, e, :], z_turn[:, :, t * 4 + e], ident[:])
                            last.then_inc(t_done, 1)

        @block.scalar
        def _(act):
            for c0, c1, old in SPANS:
                with act.Fori(c0, c1) as c:
                    for g in range(GR):
                        for b in range(BG):
                            k = g * BG + b
                            act.wait_ge(mm_done, c * (GR * UNITS) + 2 * k + 2)
                            if b == 0:
                                act.wait_ge(t_done, c * (GR * TB) + g * TB)
                            nc.scalar.copy(z_turn[:, b * H:(b + 1) * H, :], ps_z[k % 2][:]).then_inc(z_cp, 1)
                        act.wait_ge(hist_saved[g], c * (2 * DMA) + 2 * DMA)
                        nc.scalar.copy(hist[g][:, bass.ds((c * C) % OLD, C), :], w[g][:, 1:, :]).then_inc(kept[g], 1)
                        act.wait_ge(o_out[g], c * DMA + DMA)
                        for t in range(TB):
                            act.wait_ge(t_done, c * (GR * TB) + g * TB + t + 1)
                            last = nc.scalar.copy(zo[g][:].rearrange("p f s i -> p (f s) i")[:, 4 * t:4 * t + 4, :],
                                                  ps_t[t % 4][:]).then_inc(t_cp, 1)
                        act.wait_ge(t_cp, c * (GR * TB) + (g + 1) * TB)
                        act.sem_inc(zo_ready[g], 1)


class Steps:

    def __init__(self, eng, sem, base):
        self.eng, self.sem, self.base, self.n = eng, sem, base, 0

    def done(self, ins):
        ins.then_inc(self.sem, 1)
        self.n += 1
        return self.n

    def after(self, n):
        self.eng.wait_ge(self.sem, self.base + n)


def moments(nc, st, stats, mean, var, tmp, width):
    me, ce, mo, co = (stats[:, :, i] for i in (1, 2, 4, 5))
    diff = st.done(nc.vector.tensor_tensor(out=tmp, in0=me, in1=mo, op=ALU.subtract))
    total = st.done(nc.vector.tensor_tensor(out=mean, in0=me, in1=mo, op=ALU.add))
    m2 = st.done(nc.vector.tensor_tensor(out=var, in0=ce, in1=co, op=ALU.add))
    st.after(diff)
    square = st.done(nc.vector.scalar_tensor_tensor(out=tmp, in0=tmp, scalar=0.25, in1=tmp, op0=ALU.mult, op1=ALU.mult))
    st.after(total)
    half = st.done(nc.vector.tensor_scalar(mean, mean, 0.5, None, ALU.mult))
    st.after(m2)
    scaled = st.done(nc.vector.tensor_scalar(var, var, 1.0 / width, EPS, ALU.mult, ALU.add))
    st.after(max(square, half, scaled))
    st.after(st.done(nc.vector.tensor_tensor(out=var, in0=var, in1=tmp, op=ALU.add)))


MOMENT_STEPS = 7


def attention_out(nc, x, xT, o_dram, wgT, woT, ln_g, ln_b, x1_dram, x1T_dram):
    PB = 2
    PAIRS = B // PB
    HEADS4 = H // 4
    with ExitStack() as ctx:
        m = Pool(nc, ctx)
        xT_sb = m.sb("p3_xT", [P, KT, TOK])
        wg = m.sb("p3_wg", [P, KT, H * DH])
        wo = m.sb("p3_wo", [DH, H, D])
        lg, lb = m.sb("p3_lg", [DH, 1]), m.sb("p3_lb", [DH, 1])
        ident = m.sb("p3_ident", [P, P])
        neg_half = m.sb("p3_neg_half", [P, H])
        o = [m.sb(f"p3_o{b}", [T, H, DH]) for b in range(PB)]
        xr = [m.sb(f"p3_x{b}", [T, D]) for b in range(PB)]
        on = [m.sb(f"p3_on{b}", [T, H, DH]) for b in range(PB)]
        stats = [m.sb(f"p3_stats{b}", [T, H, 6]) for b in range(PB)]
        hm = [m.sb(f"p3_hm{b}", [T, H]) for b in range(PB)]
        hr = [m.sb(f"p3_hr{b}", [T, H]) for b in range(PB)]
        ht = [m.sb(f"p3_ht{b}", [T, H]) for b in range(PB)]
        gate = m.sb("p3_gate", [DH, H, PB, T])
        y = [m.sb(f"p3_y{b}", [DH, H, T]) for b in range(PB)]
        res = [m.sb(f"p3_res{b}", [T, D]) for b in range(PB)]
        x1 = [m.sb(f"p3_x1{b}", [T, D]) for b in range(PB)]
        x1t = [m.sb(f"p3_x1t{b}", [P, KT, T]) for b in range(PB)]
        rstats = m.sb("p3_rstats", [T, PB, 6])
        rm, rr, rt = (m.sb(f"p3_r{n}", [T, PB]) for n in "mrt")
        ps_g = [m.ps(f"p3_ps_g{i}", [DH, 2, PB * T]) for i in range(2)]
        ps_t = [m.ps(f"p3_ps_t{i}", [DH, 4, T]) for i in range(2)]
        ps_o = [m.ps(f"p3_ps_o{b}", [T, 2 * D]) for b in range(PB)]
        ps_x = [m.ps(f"p3_ps_x{b}", [P, 4, T]) for b in range(PB)]

        consts = m.sem("p3_consts")
        made = m.sem("p3_made")
        row_in = [m.sem(f"p3_row_in{b}") for b in range(PB)]
        gate_mm, gate_sig = m.sem("p3_gate_mm"), m.sem("p3_gate_sig")
        steps = m.sem("p3_steps")
        head_var, head_rstd = m.sem("p3_head_var"), m.sem("p3_head_rstd")
        row_var, row_rstd = m.sem("p3_row_var"), m.sem("p3_row_rstd")
        normed = m.sem("p3_normed")
        turned, affine = m.sem("p3_turned"), m.sem("p3_affine")
        gated = m.sem("p3_gated")
        out_mm = m.sem("p3_out_mm")
        x1_ready = m.sem("p3_x1_ready")
        x1_turned, x1t_cp = m.sem("p3_x1_turned"), m.sem("p3_x1t_cp")
        x1_out = [m.sem(f"p3_x1_out{b}") for b in range(PB)]
        x1t_out = [m.sem(f"p3_x1t_out{b}") for b in range(PB)]
        block = ctx.enter_context(nc.Block())
        STEPS = PB * (H + MOMENT_STEPS + H - 1) + PB * 2 + MOMENT_STEPS

        @block.sync
        def _(sp):
            sp.dma_start(xT_sb[:], xT.rearrange("(k p) t -> p k t", p=P)).then_inc(consts, DMA)
            sp.dma_start(wg[:], wgT.rearrange("(k p) c -> p k c", p=P)).then_inc(consts, DMA)
            sp.dma_start(wo[:], woT.rearrange("(h i) n -> i h n", i=DH)).then_inc(consts, DMA)
            sp.dma_start(lg[:], ln_g).then_inc(consts, DMA)
            sp.dma_start(lb[:], ln_b).then_inc(consts, DMA)
            with sp.Fori(0, PAIRS) as p:
                row = sp.snap(p * PB)
                for b in range(PB):
                    sp.wait_ge(normed, p * PB)
                    sp.dma_start(o[b][:], o_dram[bass.ds(row + b, 1), :, :, 0:DH].rearrange("a h t i -> t (a h) i")).then_inc(row_in[b], DMA)
                for b in range(PB):
                    sp.wait_ge(x1_ready, p * PB)
                    sp.dma_start(xr[b][:], x[bass.ds(row + b, 1)].rearrange("a t n -> (a t) n")).then_inc(row_in[b], DMA)
            for b in range(PB):
                sp.wait_ge(x1_out[b], DMA * PAIRS)
                sp.wait_ge(x1t_out[b], DMA * PAIRS)

        @block.gpsimd
        def _(pool):
            nc.gpsimd.memset(ident[:], 0.0).then_inc(made, 1)
            nc.gpsimd.memset(neg_half[:], -0.5).then_inc(made, 1)
            pool.wait_ge(made, 2)
            nc.gpsimd.affine_select(out=ident[:], in_=ident[:], compare_op=ALU.not_equal, fill=1.0, base=0,
                                    pattern=[[-1, P]], channel_multiplier=1).then_inc(made, 1)
            with pool.Fori(0, PAIRS) as p:
                for b in range(PB):
                    pool.wait_ge(head_var, p * PB + b + 1)
                    nc.gpsimd.tensor_tensor(out=hr[b][:], in0=hr[b][:], in1=neg_half[:], op=ALU.pow).then_inc(head_rstd, 1)
                for b in range(PB):
                    pool.wait_ge(gate_sig, p * (H // 2) + H // 2)
                    pool.wait_ge(affine, p * (PB * HEADS4) + (b + 1) * HEADS4)
                    nc.gpsimd.tensor_tensor(out=y[b][:], in0=y[b][:], in1=gate[:, :, b, :], op=ALU.mult).then_inc(gated, 1)
                pool.wait_ge(row_var, p + 1)
                nc.gpsimd.tensor_tensor(out=rr[:], in0=rr[:], in1=neg_half[:, 0:PB], op=ALU.pow).then_inc(row_rstd, 1)

        @block.tensor
        def _(pe):
            pe.wait_ge(consts, 5 * DMA)
            pe.wait_ge(made, 3)
            with pe.Fori(0, PAIRS) as p:
                for g in range(H // 2):
                    pe.wait_ge(gate_sig, p * (H // 2) + max(g - 1, 0))
                    for e in range(2):
                        for k in range(KT):
                            last = nc.tensor.matmul(ps_g[g % 2][:, e, :], wg[:, k, (2 * g + e) * DH:(2 * g + e + 1) * DH],
                                                    xT_sb[:, k, bass.ds(p * (PB * T), PB * T)],
                                                    start=(k == 0), stop=(k == KT - 1))
                    last.then_inc(gate_mm, 1)
                for b in range(PB):
                    pe.wait_ge(normed, p * PB + b + 1)
                    for q in range(HEADS4):
                        n = b * HEADS4 + q
                        pe.wait_ge(affine, p * (PB * HEADS4) + max(n - 1, 0))
                        for e in range(4):
                            last = nc.tensor.transpose(ps_t[n % 2][:, e, :], on[b][:, 4 * q + e, :], ident[:])
                        last.then_inc(turned, 1)
                for b in range(PB):
                    pe.wait_ge(gated, p * PB + b + 1)
                    for h in range(H):
                        last = nc.tensor.matmul(ps_o[b][:, 0:D], y[b][:, h, :], wo[:, h, :], start=(h == 0), stop=(h == H - 1))
                    last.then_inc(out_mm, 1)
                for b in range(PB):
                    pe.wait_ge(x1_ready, p * PB + b + 1)
                    for k in range(KT):
                        last = nc.tensor.transpose(ps_x[b][:, k, :], x1[b][:, k * P:(k + 1) * P], ident[:])
                    last.then_inc(x1_turned, 1)

        @block.scalar
        def _(act):
            act.wait_ge(consts, 5 * DMA)
            with act.Fori(0, PAIRS) as p:
                row = act.snap(p * PB)
                for g in range(H // 2):
                    act.wait_ge(gate_mm, p * (H // 2) + g + 1)
                    act.wait_ge(gated, p * PB)
                    nc.scalar.activation(gate[:, 2 * g:2 * g + 2, :, :].rearrange("c e b t -> c e (b t)"), ps_g[g % 2][:],
                                         ACT.Sigmoid).then_inc(gate_sig, 1)
                for b in range(PB):
                    act.wait_ge(out_mm, p * PB)
                    for q in range(HEADS4):
                        n = b * HEADS4 + q
                        act.wait_ge(turned, p * (PB * HEADS4) + n + 1)
                        nc.scalar.activation(y[b][:, 4 * q:4 * q + 4, :], ps_t[n % 2][:], ACT.Identity,
                                             bias=lb[:, 0:1], scale=lg[:, 0:1]).then_inc(affine, 1)
                for b in range(PB):
                    act.wait_ge(x1_ready, p * PB + b + 1)
                    act.dma_start(x1_dram[bass.ds(row + b, 1)].rearrange("a t n -> (a t) n"), x1[b][:]).then_inc(x1_out[b], DMA)
                    act.wait_ge(x1t_out[b], p * DMA)
                    act.wait_ge(x1_turned, p * PB + b + 1)
                    nc.scalar.copy(x1t[b][:], ps_x[b][:, 0:KT, :]).then_inc(x1t_cp, 1)
                    act.wait_ge(x1t_cp, p * PB + b + 1)
                    act.dma_start(x1T_dram[:, bass.ds(row * T + b * T, T)].rearrange("(k q) t -> q k t", q=P),
                                  x1t[b][:]).then_inc(x1t_out[b], DMA)

        @block.vector
        def _(dve):
            with dve.Fori(0, PAIRS) as p:
                st = Steps(dve, steps, p * STEPS)
                for b in range(PB):
                    dve.wait_ge(row_in[b], p * (2 * DMA) + 2 * DMA)
                    for h in range(H):
                        last = st.done(nc.vector.bn_stats(out=stats[b][:, h, :], in_=o[b][:, h, :]))
                    st.after(last)
                    moments(nc, st, stats[b][:], hm[b][:], hr[b][:], ht[b][:], DH)
                    dve.sem_inc(head_var, 1)
                for b in range(PB):
                    dve.wait_ge(head_rstd, p * PB + b + 1)
                    dve.wait_ge(turned, p * (PB * HEADS4))
                    for h in range(H):
                        ins = nc.vector.tensor_scalar(on[b][:, h, :], o[b][:, h, :], hm[b][:, h:h + 1], hr[b][:, h:h + 1],
                                                      ALU.subtract, ALU.mult)
                        if h < H - 1:
                            last = st.done(ins)
                    st.after(last)
                    ins.then_inc(normed, 1)
                for b in range(PB):
                    dve.wait_ge(out_mm, p * PB + b + 1)
                    last = st.done(nc.vector.tensor_tensor(out=res[b][:], in0=ps_o[b][:, 0:D], in1=xr[b][:], op=ALU.add))
                for b in range(PB):
                    st.after(last - PB + 1 + b)
                    done = st.done(nc.vector.bn_stats(out=rstats[:, b, :], in_=res[b][:]))
                st.after(done)
                moments(nc, st, rstats[:], rm[:], rr[:], rt[:], D)
                dve.sem_inc(row_var, 1)
                dve.wait_ge(row_rstd, p + 1)
                for b in range(PB):
                    dve.wait_ge(x1_out[b], p * DMA)
                    dve.wait_ge(x1_turned, p * PB)
                    nc.vector.tensor_scalar(x1[b][:], res[b][:], rm[:, b:b + 1], rr[:, b:b + 1], ALU.subtract,
                                            ALU.mult).then_inc(x1_ready, 1)
                assert st.n == STEPS, (st.n, STEPS)


def long_conv(nc, ctxR, kpad, dcol, x1_dram, x1T_dram, kz_dram, x2_dram, x2T_dram):
    HPAIR = HK // 2
    PAIRC = HD2 * HD2
    with ExitStack() as ctx:
        m = Pool(nc, ctx)
        c_sb = m.sb("p4_c", [P, KT, B, P])
        x1t = m.sb("p4_x1t", [P, KT, B, P])
        xa = m.sb("p4_xa", [P, KT, B, P])
        kz = m.sb("p4_kz", [HK, 3 * P])
        dk = m.sb("p4_dk", [HK, 1])
        toep = [m.sb(f"p4_toep{i}", [P, 2 * P]) for i in range(2)]
        prod = [m.sb(f"p4_prod{i}", [P, KT, B, PAIRC]) for i in range(2)]
        wy = [m.sb(f"p4_wy{i}", [P, B, PAIRC]) for i in range(2)]
        ident = m.sb("p4_ident", [P, P])
        neg_half = m.sb("p4_neg_half", [P, 2])
        x1 = [m.sb(f"p4_x1{b}", [T, D]) for b in range(2)]
        res = [m.sb(f"p4_res{b}", [T, D]) for b in range(2)]
        x2 = [m.sb(f"p4_x2{b}", [T, D]) for b in range(2)]
        x2t = [m.sb(f"p4_x2t{b}", [P, KT, T]) for b in range(2)]
        rstats = m.sb("p4_rstats", [T, 2, 6])
        rm, rr, rt = (m.sb(f"p4_r{n}", [T, 2]) for n in "mrt")
        ps_y = [m.ps(f"p4_ps_y{i}", [P, 2, 8 * PAIRC]) for i in range(4)]

        consts, k_in, kz_add, kz_out = m.sem("p4_consts"), m.sem("p4_k_in"), m.sem("p4_kz_add"), m.sem("p4_kz_out")
        made = m.sem("p4_made")
        toep_in = [m.sem(f"p4_toep_in{i}") for i in range(2)]
        head_free = m.sem("p4_head_free")
        bank_free = m.sem("p4_bank_free")
        prod_done, conv_done = m.sem("p4_prod_done"), m.sem("p4_conv_done")
        weighted, summed = m.sem("p4_weighted"), m.sem("p4_summed")
        x1_in = [m.sem(f"p4_x1_in{b}") for b in range(2)]
        xa_turned, x2_ready, x2_turned, x2t_cp = (m.sem(f"p4_{n}") for n in ("xa_turned", "x2_ready", "x2_turned", "x2t_cp"))
        steps = m.sem("p4_steps")
        res_ready = m.sem("p4_res_ready")
        row_var, row_rstd = m.sem("p4_row_var"), m.sem("p4_row_rstd")
        x2_out = [m.sem(f"p4_x2_out{b}") for b in range(2)]
        x2t_out = [m.sem(f"p4_x2t_out{b}") for b in range(2)]
        block = ctx.enter_context(nc.Block())
        ROW_STEPS = 2 + MOMENT_STEPS

        @block.sync
        def _(sp):
            sp.dma_start(kz[:], kpad).then_inc(k_in, DMA)
            sp.dma_start(dk[:], dcol).then_inc(k_in, DMA)
            sp.dma_start(c_sb[:], ctxR).then_inc(consts, DMA)
            sp.dma_start(x1t[:].rearrange("p k b t -> p k (b t)"), x1T_dram.rearrange("(k p) t -> p k t", p=P)).then_inc(consts, DMA)
            sp.wait_ge(kz_add, 1)
            sp.dma_start(kz_dram, kz[:]).then_inc(kz_out, DMA)
            sp.wait_ge(kz_out, DMA)
            with sp.Fori(0, HPAIR) as hp:
                for j in range(2):
                    sp.wait_ge(head_free, hp * 2 + j + 1)
                    sp.dma_start(toep[j][:], bass.AP(kz_dram.tensor, kz_dram.offset + (hp * 2 + j) * (3 * P),
                                                     [[1, P], [1, 2 * P]])).then_inc(toep_in[j], DMA)
            with sp.Fori(0, B // 2) as p:
                row = sp.snap(p * 2)
                for b in range(2):
                    sp.wait_ge(res_ready, p * 2)
                    sp.dma_start(x1[b][:], x1_dram[bass.ds(row + b, 1)].rearrange("a t n -> (a t) n")).then_inc(x1_in[b], DMA)
            for b in range(2):
                sp.wait_ge(x2_out[b], DMA * B // 2)
                sp.wait_ge(x2t_out[b], DMA * B // 2)

        @block.gpsimd
        def _(pool):
            nc.gpsimd.memset(ident[:], 0.0).then_inc(made, 1)
            nc.gpsimd.memset(neg_half[:], -0.5).then_inc(made, 1)
            pool.wait_ge(made, 2)
            nc.gpsimd.affine_select(out=ident[:], in_=ident[:], compare_op=ALU.not_equal, fill=1.0, base=0,
                                    pattern=[[-1, P]], channel_multiplier=1).then_inc(made, 1)
            pool.wait_ge(consts, 2 * DMA)
            with pool.Fori(0, HPAIR) as hp:
                for j in range(2):
                    pool.wait_ge(head_free, hp * 2 + j + 1)
                    c0 = (hp * 2 + j) * HD2
                    for k in range(KT):
                        ck = c_sb[:, k, :, bass.ds(c0, HD2)]
                        nc.gpsimd.tensor_tensor(
                            out=prod[j][:, k].rearrange("p b (i j) -> p b i j", i=HD2),
                            in0=ck.unsqueeze(3).broadcast_to([P, B, HD2, HD2]),
                            in1=ck.unsqueeze(2).broadcast_to([P, B, HD2, HD2]), op=ALU.mult).then_inc(prod_done, 1)
            with pool.Fori(0, B // 2) as p:
                pool.wait_ge(row_var, p + 1)
                nc.gpsimd.tensor_tensor(out=rr[:], in0=rr[:], in1=neg_half[:], op=ALU.pow).then_inc(row_rstd, 1)

        @block.tensor
        def _(pe):
            pe.sem_inc(head_free, 2)
            with pe.Fori(0, HPAIR) as hp:
                for j in range(2):
                    pe.wait_ge(toep_in[j], hp * DMA + DMA)
                    pe.wait_ge(prod_done, hp * (2 * KT) + (j + 1) * KT)
                    for c in range(KT):
                        for half in range(2):
                            n = j * 2 + c
                            if half == 0:
                                pe.wait_ge(bank_free, hp * 4 + n + 1)
                            for a in range(c + 1):
                                last = nc.tensor.matmul(ps_y[n][:, half, :], toep[j][:, (c - a) * P:(c - a + 1) * P],
                                                        prod[j][:, a, half * 8:(half + 1) * 8, :].rearrange("p b q -> p (b q)"),
                                                        start=(a == 0), stop=(a == c))
                        if c == 0:
                            last.then_inc(conv_done, 1)
                    last.then_inc(conv_done, 1)
                    pe.wait_ge(conv_done, hp * 4 + j * 2 + 2)
                    pe.sem_inc(head_free, 1)
            pe.wait_ge(summed, HK * KT)
            pe.wait_ge(made, 3)
            for row in range(B):
                b = row % 2
                pe.wait_ge(res_ready, max(row - 1, 0))
                for k in range(KT):
                    last = nc.tensor.transpose(ps_y[b][:, 0, k * P:(k + 1) * P], xa[:, k, row, :], ident[:])
                last.then_inc(xa_turned, 1)
                if b == 1:
                    for e in range(2):
                        pe.wait_ge(x2_ready, row + e)
                        pe.wait_ge(x2t_cp, max(row + e - 2, 0))
                        for k in range(KT):
                            last = nc.tensor.transpose(ps_y[2 + e][:, 0, k * P:(k + 1) * P], x2[e][:, k * P:(k + 1) * P], ident[:])
                        last.then_inc(x2_turned, 1)

        @block.vector
        def _(dve):
            dve.wait_ge(k_in, 2 * DMA)
            nc.vector.tensor_tensor(out=kz[:, P - 1:P], in0=kz[:, P - 1:P], in1=dk[:], op=ALU.add).then_inc(kz_add, 1)
            dve.sem_inc(bank_free, 4)
            dve.wait_ge(consts, 2 * DMA)
            with dve.Fori(0, HPAIR) as hp:
                for j in range(2):
                    for c in range(KT):
                        n = j * 2 + c
                        stream = x1t[:, c, :, bass.ds((hp * 2 + j) * HD2, HD2)]
                        dve.wait_ge(conv_done, hp * 4 + n + 1)
                        dve.wait_ge(summed, hp * 4 + max(n - 1, 0))
                        nc.vector.tensor_tensor(
                            out=wy[c][:].rearrange("p b (j i) -> p b j i", j=HD2),
                            in0=ps_y[n][:].rearrange("p a (b j i) -> p (a b) j i", j=HD2, i=HD2),
                            in1=stream.unsqueeze(2).broadcast_to([P, B, HD2, HD2]), op=ALU.mult).then_inc(bank_free, 1)
                        dve.wait_ge(bank_free, hp * 4 + n + 5)
                        nc.vector.tensor_reduce(out=xa[:, c, :, bass.ds((hp * 2 + j) * HD2, HD2)],
                                                in_=wy[c][:].rearrange("p b (j i) -> p b j i", j=HD2),
                                                axis=AXIS_X, op=ALU.add).then_inc(summed, 1)
            with dve.Fori(0, B // 2) as p:
                st = Steps(dve, steps, p * ROW_STEPS)
                for b in range(2):
                    dve.wait_ge(x1_in[b], p * DMA + DMA)
                    dve.wait_ge(xa_turned, p * 2 + b + 1)
                    nc.vector.tensor_tensor(out=res[b][:], in0=ps_y[b][:, 0, 0:D], in1=x1[b][:], op=ALU.add).then_inc(res_ready, 1)
                for b in range(2):
                    dve.wait_ge(res_ready, p * 2 + b + 1)
                    done = st.done(nc.vector.bn_stats(out=rstats[:, b, :], in_=res[b][:]))
                st.after(done)
                moments(nc, st, rstats[:], rm[:], rr[:], rt[:], D)
                dve.sem_inc(row_var, 1)
                dve.wait_ge(row_rstd, p + 1)
                for b in range(2):
                    dve.wait_ge(x2_out[b], p * DMA)
                    dve.wait_ge(x2_turned, p * 2)
                    nc.vector.tensor_scalar(x2[b][:], res[b][:], rm[:, b:b + 1], rr[:, b:b + 1], ALU.subtract,
                                            ALU.mult).then_inc(x2_ready, 1)
                assert st.n == ROW_STEPS

        @block.scalar
        def _(act):
            with act.Fori(0, B // 2) as p:
                row = act.snap(p * 2)
                for b in range(2):
                    act.wait_ge(x2_ready, p * 2 + b + 1)
                    act.dma_start(x2_dram[bass.ds(row + b, 1)].rearrange("a t n -> (a t) n"), x2[b][:]).then_inc(x2_out[b], DMA)
                for b in range(2):
                    act.wait_ge(x2t_out[b], p * DMA)
                    act.wait_ge(x2_turned, p * 2 + b + 1)
                    nc.scalar.copy(x2t[b][:].rearrange("p k t -> p (k t)"), ps_y[2 + b][:, 0, 0:D]).then_inc(x2t_cp, 1)
                    act.wait_ge(x2t_cp, p * 2 + b + 1)
                    act.dma_start(x2T_dram[:, bass.ds(row * T + b * T, T)].rearrange("(k q) t -> q k t", q=P),
                                  x2t[b][:]).then_inc(x2t_out[b], DMA)


def experts(nc, x2_dram, x2T_dram, gwT, sguT, sdT, wguT, wdT, buf_dram, eo_dram, out):
    NT = TOK // P
    MH = M // 2
    SM = MS // MH
    KEPT = 16384.0
    NE = NT * E
    with ExitStack() as outer:
        m = Pool(nc, outer)
        acc = m.sb("p5_acc", [P, NT, D])
        wk = m.sb("p5_wk", [P, TOPK, NT])
        slot_i = m.sb("p5_slot_i", [P, TOPK, NT], INT32)
        target_i = m.sb("p5_target_i", [P, TOPK, NT], INT32)
        shared = m.sb("p5_shared", [P, NT, D])

        with ExitStack() as ctx:
            m = Pool(nc, ctx)
            xT = m.sb("p5_xT", [P, KT, TOK])
            gw = m.sb("p5_gw", [P, KT, E])
            sgu = m.sb("p5_sgu", [P, KT, 2, MS])
            sd = m.sb("p5_sd", [MH, SM, D])
            zeros = m.sb("p5_zeros", [P, 8 * D])
            ones, tri = m.sb("p5_ones", [P, P]), m.sb("p5_tri", [P, P])
            reset = m.sb("p5_reset", [P, NT, E])
            below = m.sb("p5_below", [P, GROUPS, GROUPS])
            slot0_i = m.sb("p5_slot0_i", [P, E], INT32)
            slot0 = m.sb("p5_slot0", [P, E])
            score, a1, a2, a3, sel, rank, val = (m.sb(f"p5_{n}", [P, NT, E]) for n in
                                                 ("score", "a1", "a2", "a3", "sel", "rank", "val"))
            pre = m.sb("p5_pre", [P, NT + 1, E])
            top8 = m.sb("p5_top8", [P, NT, 8])
            gs, gr = m.sb("p5_gs", [P, NT, GROUPS]), m.sb("p5_gr", [P, NT, GROUPS])
            t1, t2 = m.sb("p5_t1", [P, NT]), m.sb("p5_t2", [P, NT])
            cnt = m.sb("p5_cnt", [P, E])
            vk, v2 = m.sb("p5_vk", [P, TOPK, NT]), m.sb("p5_v2", [P, TOPK, NT])
            sg = [m.sb(f"p5_sg{i}", [MH, 512]) for i in range(2)]
            gx = [m.sb(f"p5_gx{i}", [MH, 512]) for i in range(2)]
            ux = [m.sb(f"p5_ux{i}", [MH, 512]) for i in range(2)]
            hs = m.sb("p5_hs", [MH, SM, 512])
            ps_r = m.ps("p5_ps_r", [P, NT, E])
            ps_g = [m.ps(f"p5_ps_g{i}", [MH, 512]) for i in range(2)]
            ps_u = [m.ps(f"p5_ps_u{i}", [MH, 512]) for i in range(2)]
            ps_d = m.ps("p5_ps_d", [P, 2, D])
            ps_c = m.ps("p5_ps_c", [P, E])

            r_in, s_in, x_in = m.sem("p5_r_in"), m.sem("p5_s_in"), m.sem("p5_x_in")
            zero_made, zeroed = m.sem("p5_zero_made"), m.sem("p5_zeroed")
            made = m.sem("p5_made")
            logits, steps = m.sem("p5_logits"), m.sem("p5_steps")
            shifted, exped = m.sem("p5_shifted"), m.sem("p5_exped")
            chosen, ranked = m.sem("p5_chosen"), m.sem("p5_ranked")
            slots_ready = m.sem("p5_slots_ready")
            up_mm, sig_done, gx_done, ux_done = (m.sem(f"p5_{n}") for n in ("up_mm", "sig_done", "gx_done", "ux_done"))
            silu_done, h_done, down_mm, down_cp = (m.sem(f"p5_{n}") for n in ("silu_done", "h_done", "down_mm", "down_cp"))
            sent = m.sem("p5_sent")
            block = ctx.enter_context(nc.Block())

            @block.sync
            def _(sp):
                sp.dma_start(gw[:], gwT.rearrange("(k p) e -> p k e", p=P)).then_inc(r_in, DMA)
                sp.dma_start(xT[:], x2T_dram.rearrange("(k p) t -> p k t", p=P)).then_inc(r_in, DMA)
                sp.dma_start(sgu[:], sguT).then_inc(s_in, DMA)
                sp.dma_start(sd[:], sdT).then_inc(s_in, DMA)
                sp.dma_start(acc[:], x2_dram.rearrange("b t n -> t b n")).then_inc(x_in, DMA)
                sp.wait_ge(zero_made, 1)
                sp.dma_start(buf_dram.rearrange("(a p r) n -> p a (r n)", p=P, r=8),
                             zeros[:].unsqueeze(1).broadcast_to([P, SLOTS // (8 * P), 8 * D])).then_inc(zeroed, DMA)
                sp.wait_ge(zeroed, DMA)

            @block.gpsimd
            def _(pool):
                nc.gpsimd.memset(ones[:], 1.0).then_inc(made, 1)
                nc.gpsimd.memset(reset[:], 1.0).then_inc(made, 1)
                nc.gpsimd.memset(below[:], 1.0).then_inc(made, 1)
                nc.gpsimd.iota(slot0_i[:], pattern=[[CAP, E]], base=-1, channel_multiplier=0).then_inc(made, 1)
                pool.wait_ge(made, 4)
                nc.gpsimd.affine_select(out=tri[:], in_=ones[:], compare_op=ALU.is_ge, fill=0.0, base=0,
                                        pattern=[[1, P]], channel_multiplier=-1).then_inc(made, 1)
                nc.gpsimd.affine_select(out=reset[:], in_=reset[:], compare_op=ALU.not_equal, fill=0.0, base=0,
                                        pattern=[[0, NT], [1, E]], channel_multiplier=0).then_inc(made, 1)
                nc.gpsimd.affine_select(out=below[:], in_=below[:], compare_op=ALU.is_gt, fill=0.0, base=0,
                                        pattern=[[1, GROUPS], [-1, GROUPS]], channel_multiplier=0).then_inc(made, 1)
                with pool.Fori(0, 4) as q:
                    for s in range(SM):
                        i = s % 2
                        pool.wait_ge(sig_done, q * SM + s + 1)
                        pool.wait_ge(gx_done, q * SM + s + 1)
                        nc.gpsimd.tensor_tensor(out=gx[i][:], in0=gx[i][:], in1=sg[i][:], op=ALU.mult).then_inc(silu_done, 1)
                        pool.wait_ge(silu_done, q * SM + s + 1)
                        pool.wait_ge(ux_done, q * SM + s + 1)
                        pool.wait_ge(down_mm, q * 4)
                        nc.gpsimd.tensor_tensor(out=hs[:, s, :], in0=gx[i][:], in1=ux[i][:], op=ALU.mult).then_inc(h_done, 1)
                pool.wait_ge(slots_ready, 1)
                pool.wait_ge(x_in, DMA)
                pool.wait_ge(zeroed, DMA)
                for i in range(NT):
                    for k in range(TOPK):
                        nc.gpsimd.indirect_dma_start(
                            out=buf_dram, out_offset=bass.IndirectOffsetOnAxis(ap=target_i[:, k, i:i + 1], axis=0),
                            in_=acc[:, i, :], in_offset=None, bounds_check=SLOTS - 1, oob_is_err=False).then_inc(sent, DMA)
                pool.wait_ge(sent, DMA * NT * TOPK)

            @block.tensor
            def _(pe):
                pe.wait_ge(r_in, 2 * DMA)
                for i in range(NT):
                    for k in range(KT):
                        last = nc.tensor.matmul(ps_r[:, i, :], xT[:, k, i * P:(i + 1) * P], gw[:, k, :],
                                                start=(k == 0), stop=(k == KT - 1))
                last.then_inc(logits, 1)
                pe.wait_ge(s_in, 2 * DMA)
                with pe.Fori(0, 4) as q:
                    for s in range(SM):
                        i = s % 2
                        pe.wait_ge(gx_done, q * SM + max(s - 1, 0))
                        pe.wait_ge(ux_done, q * SM + max(s - 1, 0))
                        for half, ps in ((0, ps_g), (1, ps_u)):
                            for k in range(KT):
                                last = nc.tensor.matmul(ps[i][:], sgu[:, k, half, s * MH:(s + 1) * MH],
                                                        xT[:, k, bass.ds(q * 512, 512)], start=(k == 0), stop=(k == KT - 1))
                        last.then_inc(up_mm, 1)
                    pe.wait_ge(h_done, q * SM + SM)
                    for t in range(4):
                        pe.wait_ge(down_cp, q * 4 + t)
                        for s in range(SM):
                            last = nc.tensor.matmul(ps_d[:, t % 2, :], hs[:, s, t * P:(t + 1) * P], sd[:, s, :],
                                                    start=(s == 0), stop=(s == SM - 1))
                        last.then_inc(down_mm, 1)
                pe.wait_ge(chosen, 1)
                pe.wait_ge(made, 7)
                for i in range(NT):
                    nc.tensor.matmul(ps_r[:, i, :], tri[:], sel[:, i, :], start=True, stop=False)
                    nc.tensor.matmul(ps_r[:, i, :], ones[:], pre[:, i, :], start=False, stop=True)
                nc.tensor.matmul(ps_c[:], ones[:], pre[:, NT, :], start=True, stop=True).then_inc(ranked, 1)

            @block.scalar
            def _(act):
                act.wait_ge(shifted, 1)
                nc.scalar.activation(score[:], a1[:], ACT.Exp).then_inc(exped, 1)
                with act.Fori(0, 4) as q:
                    for s in range(SM):
                        i = s % 2
                        act.wait_ge(up_mm, q * SM + s + 1)
                        act.wait_ge(h_done, q * SM + max(s - 1, 0))
                        nc.scalar.activation(sg[i][:], ps_g[i][:], ACT.Sigmoid).then_inc(sig_done, 1)
                        nc.scalar.copy(gx[i][:], ps_g[i][:]).then_inc(gx_done, 1)
                        nc.scalar.copy(ux[i][:], ps_u[i][:]).then_inc(ux_done, 1)
                    for t in range(4):
                        act.wait_ge(down_mm, q * 4 + t + 1)
                        nc.scalar.copy(shared[:, bass.ds(q * 4 + t, 1), :].rearrange("p a n -> p (a n)"),
                                       ps_d[:, t % 2, :]).then_inc(down_cp, 1)

            @block.vector
            def _(dve):
                st = Steps(dve, steps, 0)
                tt, ts, stt = nc.vector.tensor_tensor, nc.vector.tensor_scalar, nc.vector.scalar_tensor_tensor

                def then(ins):
                    st.after(st.done(ins))

                def by_tile(ap):
                    return ap.unsqueeze(2).broadcast_to([P, NT, E])

                nc.vector.memset(zeros[:], 0.0).then_inc(zero_made, 1)
                then(nc.vector.memset(pre[:, 0, :], 0.0))
                dve.wait_ge(made, 7)
                then(nc.vector.tensor_copy(slot0[:], slot0_i[:]))
                dve.wait_ge(logits, 1)
                then(nc.vector.tensor_reduce(out=t1[:], in_=ps_r[:], axis=AXIS_X, op=ALU.max))
                tt(out=a1[:], in0=ps_r[:], in1=by_tile(t1[:]), op=ALU.subtract).then_inc(shifted, 1)
                dve.wait_ge(exped, 1)
                then(nc.vector.tensor_reduce(out=t1[:], in_=score[:], axis=AXIS_X, op=ALU.add))
                then(nc.vector.reciprocal(t2[:], t1[:]))
                then(tt(out=score[:], in0=score[:], in1=by_tile(t2[:]), op=ALU.mult))
                then(nc.vector.tensor_reduce(out=gs[:].rearrange("p t g -> p (t g)"),
                                             in_=score[:].rearrange("p t (g e) -> p (t g) e", g=GROUPS), axis=AXIS_X, op=ALU.max))
                pair = [P, NT, GROUPS, GROUPS]
                other, own = gs[:].unsqueeze(2).broadcast_to(pair), gs[:].unsqueeze(3).broadcast_to(pair)
                a1v, a2v = (a[:].rearrange("p t (g h) -> p t g h", g=GROUPS) for a in (a1, a2))
                st.done(tt(out=a1v, in0=other, in1=own, op=ALU.is_gt))
                then(tt(out=a2v, in0=other, in1=own, op=ALU.is_equal))
                then(tt(out=a2v, in0=a2v, in1=below[:].unsqueeze(1).broadcast_to(pair), op=ALU.mult))
                then(tt(out=a1[:], in0=a1[:], in1=a2[:], op=ALU.add))
                then(nc.vector.tensor_reduce(out=gr[:].rearrange("p t g -> p (t g)"),
                                             in_=a1[:].rearrange("p t (g h) -> p (t g) h", g=GROUPS), axis=AXIS_X, op=ALU.add))
                then(ts(gr[:], gr[:], float(TOPG), None, ALU.is_lt))
                then(tt(out=a1[:].rearrange("p t (g e) -> p (t g) e", g=GROUPS), in0=score[:].rearrange("p t (g e) -> p (t g) e", g=GROUPS),
                        in1=gr[:].rearrange("p t (g o) -> p (t g) o", o=1).broadcast_to([P, NT * GROUPS, E // GROUPS]), op=ALU.mult))
                for i in range(NT):
                    last = st.done(nc.vector.max(top8[:, i, :], a1[:, i, :]))
                st.after(last)
                kth = by_tile(top8[:, :, TOPK - 1])
                st.done(tt(out=a2[:], in0=a1[:], in1=kth, op=ALU.is_gt))
                then(tt(out=a3[:], in0=a1[:], in1=kth, op=ALU.is_equal))
                then(nc.vector.tensor_reduce(out=t1[:], in_=a2[:], axis=AXIS_X, op=ALU.add))
                flat = [a[:].rearrange("p t e -> p (t e)") for a in (reset, a3, rank, sel)]
                then(nc.vector.tensor_tensor_scan(flat[2], flat[0], flat[1], 0.0, ALU.mult, ALU.add))
                then(ts(t2[:], t1[:], -1.0, float(TOPK), ALU.mult, ALU.add))
                then(tt(out=rank[:], in0=rank[:], in1=by_tile(t2[:]), op=ALU.is_le))
                then(tt(out=a3[:], in0=a3[:], in1=rank[:], op=ALU.mult))
                then(tt(out=sel[:], in0=a3[:], in1=a2[:], op=ALU.add))
                for i in range(NT):
                    then(tt(out=pre[:, i + 1, :], in0=pre[:, i, :], in1=sel[:, i, :], op=ALU.add))
                dve.sem_inc(chosen, 1)
                then(nc.vector.tensor_tensor_scan(flat[2], flat[0], flat[3], 0.0, ALU.mult, ALU.add))
                dve.wait_ge(ranked, 1)
                then(nc.vector.tensor_copy(cnt[:], ps_c[:]))
                st.done(ts(a1[:], ps_r[:], float(CAP - 1), None, ALU.is_le))
                st.done(tt(out=a2[:], in0=ps_r[:], in1=cnt[:].unsqueeze(1).broadcast_to([P, NT, E]), op=ALU.is_equal))
                then(stt(out=val[:], in0=ps_r[:], scalar=float(CAP), in1=slot0[:].unsqueeze(1).broadcast_to([P, NT, E]),
                         op0=ALU.min, op1=ALU.add))
                then(tt(out=a1[:], in0=a1[:], in1=a2[:], op=ALU.max))
                then(stt(out=val[:], in0=a1[:], scalar=KEPT, in1=val[:], op0=ALU.mult, op1=ALU.add))
                for k in range(TOPK):
                    then(stt(out=a1[:], in0=rank[:], scalar=float(k + 1), in1=sel[:], op0=ALU.is_equal, op1=ALU.mult))
                    first = st.done(tt(out=a2[:], in0=a1[:], in1=val[:], op=ALU.mult))
                    second = st.done(tt(out=a3[:], in0=a1[:], in1=score[:], op=ALU.mult))
                    st.after(first)
                    st.done(nc.vector.tensor_reduce(out=vk[:, k, :], in_=a2[:], axis=AXIS_X, op=ALU.add))
                    st.after(second)
                    then(nc.vector.tensor_reduce(out=wk[:, k, :], in_=a3[:], axis=AXIS_X, op=ALU.add))
                then(ts(v2[:], vk[:], KEPT, KEPT, ALU.is_ge, ALU.mult))
                then(tt(out=vk[:], in0=vk[:], in1=v2[:], op=ALU.subtract))
                st.done(nc.vector.tensor_copy(slot_i[:], vk[:]))
                then(stt(out=v2[:], in0=v2[:], scalar=-1.0, in1=vk[:], op0=ALU.mult, op1=ALU.add))
                then(ts(v2[:], v2[:], KEPT, None, ALU.add))
                nc.vector.tensor_copy(target_i[:], v2[:]).then_inc(slots_ready, 1)

        with ExitStack() as ctx:
            m = Pool(nc, ctx)
            NB = 4
            ident = m.sb("p5_ident", [P, P])
            wgu = [m.sb(f"p5_wgu{i}", [P, KT, 2, M]) for i in range(NB)]
            wd = [m.sb(f"p5_wd{i}", [MH, 2, D]) for i in range(NB)]
            xe = [m.sb(f"p5_xe{i}", [CAP, D]) for i in range(NB)]
            xt = [m.sb(f"p5_xt{i}", [P, KT, CAP]) for i in range(NB)]
            sg = [m.sb(f"p5_esg{i}", [MH, 2, CAP]) for i in range(NB)]
            hh = [m.sb(f"p5_eh{i}", [MH, 2, CAP]) for i in range(NB)]
            yo = [m.sb(f"p5_yo{i}", [CAP, D]) for i in range(NB)]
            ps_x = [m.ps(f"p5_ps_x{i}", [P, 2, D]) for i in range(2)]
            ps_e = [m.ps(f"p5_ps_e{i}", [MH, 2, D]) for i in range(4)]
            ps_y = [m.ps(f"p5_ps_y{i}", [P, 2, D]) for i in range(2)]

            made = m.sem("p5_made2")
            w_in = [m.sem(f"p5_w_in{i}") for i in range(NB)]
            x_in = [m.sem(f"p5_xe_in{i}") for i in range(NB)]
            x_turned, xt_cp, up_mm, sig_done, silu_done, h_done, down_mm, y_cp = (
                m.sem(f"p5_e_{n}") for n in ("x_turned", "xt_cp", "up_mm", "sig_done", "silu_done", "h_done", "down_mm", "y_cp"))
            y_out = [m.sem(f"p5_y_out{i}") for i in range(NB)]
            block = ctx.enter_context(nc.Block())

            @block.sync
            def _(sp):
                with sp.Fori(0, E // NB) as q:
                    e0 = sp.snap(q * NB)
                    for i in range(NB):
                        sp.wait_ge(down_mm, q * NB)
                        sp.dma_start(wgu[i][:].rearrange("p k h m -> p (k h m)"), wguT[bass.ds(e0 + i, 1)]
                                     .rearrange("a p x -> (a p) x")).then_inc(w_in[i], DMA)
                        sp.dma_start(wd[i][:].rearrange("p h n -> p (h n)"), wdT[bass.ds(e0 + i, 1)]
                                     .rearrange("a p x -> (a p) x")).then_inc(w_in[i], DMA)

            @block.gpsimd
            def _(pool):
                nc.gpsimd.memset(ident[:], 0.0).then_inc(made, 1)
                pool.wait_ge(made, 1)
                nc.gpsimd.affine_select(out=ident[:], in_=ident[:], compare_op=ALU.not_equal, fill=1.0, base=0,
                                        pattern=[[-1, P]], channel_multiplier=1).then_inc(made, 1)
                with pool.Fori(0, E // NB) as q:
                    r0 = pool.snap(q * (NB * CAP))
                    for i in range(NB):
                        pool.wait_ge(x_turned, q * NB)
                        pool.dma_start(xe[i][:], buf_dram[bass.ds(r0 + i * CAP, CAP), :]).then_inc(x_in[i], DMA)

            @block.tensor
            def _(pe):
                pe.wait_ge(made, 2)

                def turn(q, i):
                    pe.wait_ge(x_in[i], q * DMA + DMA)
                    pe.wait_ge(xt_cp, q * NB)
                    for k in range(KT):
                        last = nc.tensor.transpose(ps_x[i // 2][:, i % 2, k * CAP:(k + 1) * CAP], xe[i][:, k * P:(k + 1) * P],
                                                   ident[0:CAP, 0:CAP])
                    last.then_inc(x_turned, 1)

                def up(q, i):
                    pe.wait_ge(w_in[i], q * (2 * DMA) + 2 * DMA)
                    pe.wait_ge(xt_cp, q * NB + i + 1)
                    pe.wait_ge(h_done, q * NB)
                    for g in range(2):
                        for half in range(2):
                            for k in range(KT):
                                last = nc.tensor.matmul(ps_e[i][:, g, half * CAP:(half + 1) * CAP],
                                                        wgu[i][:, k, g, half * MH:(half + 1) * MH], xt[i][:, k, :],
                                                        start=(k == 0), stop=(k == KT - 1))
                    last.then_inc(up_mm, 1)

                def down(q, i):
                    pe.wait_ge(h_done, q * NB + i + 1)
                    pe.wait_ge(y_cp, q * NB + max(i - 1, 0))
                    for half in range(2):
                        last = nc.tensor.matmul(ps_y[i % 2][0:CAP, 0, :], hh[i][:, half, :], wd[i][:, half, :],
                                                start=(half == 0), stop=(half == 1))
                    last.then_inc(down_mm, 1)

                with pe.Fori(0, E // NB) as q:
                    for i in range(NB):
                        turn(q, i)
                    up(q, 0)
                    for i in range(1, NB):
                        up(q, i)
                        down(q, i - 1)
                    down(q, NB - 1)

            @block.scalar
            def _(act):
                with act.Fori(0, E // NB) as q:
                    r0 = act.snap(q * (NB * CAP))

                    def store(i):
                        act.wait_ge(y_out[i], q * DMA)
                        act.wait_ge(down_mm, q * NB + i + 1)
                        nc.scalar.copy(yo[i][:], ps_y[i % 2][0:CAP, 0, :]).then_inc(y_cp, 1)
                        act.wait_ge(y_cp, q * NB + i + 1)
                        act.dma_start(eo_dram[bass.ds(r0 + i * CAP, CAP), :], yo[i][:]).then_inc(y_out[i], DMA)

                    for i in range(NB):
                        act.wait_ge(up_mm, q * NB + i + 1)
                        nc.scalar.activation(sg[i][:].rearrange("p h c -> p (h c)"), ps_e[i][:, 0, 0:2 * CAP],
                                             ACT.Sigmoid).then_inc(sig_done, 1)
                        if i >= 1:
                            store(i - 1)
                    store(NB - 1)
                for i in range(NB):
                    act.wait_ge(y_out[i], DMA * E // NB)

            @block.vector
            def _(dve):
                with dve.Fori(0, E // NB) as q:
                    for i in range(NB):
                        dve.wait_ge(x_turned, q * NB + i // 2 * 2 + 2)
                        nc.vector.tensor_copy(xt[i][:].rearrange("p k c -> p (k c)"),
                                              ps_x[i // 2][:, i % 2, 0:KT * CAP]).then_inc(xt_cp, 1)
                    for i in range(NB):
                        h = hh[i][:].rearrange("p h c -> p (h c)")
                        dve.wait_ge(down_mm, q * NB)
                        dve.wait_ge(sig_done, q * NB + i + 1)
                        nc.vector.tensor_tensor(out=h, in0=sg[i][:].rearrange("p h c -> p (h c)"), in1=ps_e[i][:, 0, 0:2 * CAP],
                                                op=ALU.mult).then_inc(silu_done, 1)
                        dve.wait_ge(silu_done, q * NB + i + 1)
                        nc.vector.tensor_tensor(out=h, in0=h, in1=ps_e[i][:, 1, 0:2 * CAP], op=ALU.mult).then_inc(h_done, 1)

        with ExitStack() as ctx:
            m = Pool(nc, ctx)
            NG = 4
            got = [m.sb(f"p5_got{i}", [P, TOPK, D]) for i in range(NG)]
            ysum = [m.sb(f"p5_ysum{i}", [P, D]) for i in range(2)]
            yf = [m.sb(f"p5_yf{i}", [P, D]) for i in range(2)]
            neg_half = m.sb("p5_neg_half", [P, 2])
            rstats = m.sb("p5_rstats", [P, 2, 6])
            rm, rr, rt = (m.sb(f"p5_r{n}", [P, 2]) for n in "mrt")
            made, steps = m.sem("p5_made3"), m.sem("p5_steps3")
            fetched = [m.sem(f"p5_fetched{i}") for i in range(NG)]
            summed = m.sem("p5_summed")
            row_var, row_rstd, y_ready = m.sem("p5_row_var"), m.sem("p5_row_rstd"), m.sem("p5_y_ready")
            y_out = [m.sem(f"p5_f_out{i}") for i in range(2)]
            block = ctx.enter_context(nc.Block())

            @block.gpsimd
            def _(pool):
                nc.gpsimd.memset(neg_half[:], -0.5).then_inc(made, 1)
                pool.wait_ge(made, 1)

                def rstd(p):
                    pool.wait_ge(row_var, p + 1)
                    nc.gpsimd.tensor_tensor(out=rr[:], in0=rr[:], in1=neg_half[:], op=ALU.pow).then_inc(row_rstd, 1)

                for i in range(NT):
                    if i >= NG:
                        pool.wait_ge(summed, i - NG + 1)
                    for k in range(TOPK):
                        nc.gpsimd.indirect_dma_start(
                            out=got[i % NG][:, k, :], out_offset=None, in_=eo_dram,
                            in_offset=bass.IndirectOffsetOnAxis(ap=slot_i[:, k, i:i + 1], axis=0)).then_inc(fetched[i % NG], DMA)
                    if i % 2 and i >= 3:
                        rstd(i // 2 - 1)
                rstd(NT // 2 - 1)

            @block.vector
            def _(dve):
                n_row = 2 * (1 + TOPK) + MOMENT_STEPS
                with dve.Fori(0, NT // NG) as q:
                    st = Steps(dve, steps, q * (2 * n_row))
                    for p in range(NG // 2):
                        pair = []
                        for b in range(2):
                            g = 2 * p + b
                            dve.wait_ge(fetched[g], q * (TOPK * DMA) + TOPK * DMA)
                            y = acc[:, bass.ds(q * NG + g, 1), :].rearrange("p a n -> p (a n)")
                            sh = shared[:, bass.ds(q * NG + g, 1), :].rearrange("p a n -> p (a n)")
                            pair.append([y, sh, g])
                        last = [0, 0]
                        for k in range(TOPK):
                            for b, (y, sh, g) in enumerate(pair):
                                if k:
                                    st.after(last[b])
                                ins = nc.vector.scalar_tensor_tensor(
                                    out=sh, in0=got[g][:, k, :], scalar=wk[:, k, bass.ds(q * NG + g, 1)],
                                    in1=sh, op0=ALU.mult, op1=ALU.add)
                                last[b] = st.done(ins)
                        for b, (y, sh, g) in enumerate(pair):
                            st.after(last[b])
                            dve.wait_ge(y_ready, q * NG + 2 * p)
                            nc.vector.tensor_tensor(out=ysum[b][:], in0=y, in1=sh, op=ALU.add).then_inc(summed, 1)
                        for b, (y, sh, g) in enumerate(pair):
                            dve.wait_ge(summed, q * NG + g + 1)
                            done = st.done(nc.vector.bn_stats(out=rstats[:, b, :], in_=ysum[b][:]))
                        st.after(done)
                        moments(nc, st, rstats[:], rm[:], rr[:], rt[:], D)
                        dve.sem_inc(row_var, 1)
                        dve.wait_ge(row_rstd, q * (NG // 2) + p + 1)
                        for b, (y, sh, g) in enumerate(pair):
                            dve.wait_ge(y_out[b], q * (NG // 2 * DMA) + p * DMA)
                            nc.vector.tensor_scalar(yf[b][:], ysum[b][:], rm[:, b:b + 1], rr[:, b:b + 1], ALU.subtract,
                                                    ALU.mult).then_inc(y_ready, 1)
                    assert st.n == 2 * n_row, (st.n, n_row)

            @block.sync
            def _(sp):
                with sp.Fori(0, NT // 2) as p:
                    row = sp.snap(p * 2)
                    for b in range(2):
                        sp.wait_ge(y_ready, p * 2 + b + 1)
                        sp.dma_start(out[bass.ds(row + b, 1)].rearrange("a t n -> (a t) n"), yf[b][:]).then_inc(y_out[b], DMA)
                for b in range(2):
                    sp.wait_ge(y_out[b], DMA * NT // 2)


INPUTS = ("x", "xT", "w_heads", "ba", "wbT", "bb_col", "bb_row", "wgT", "woT", "ln_g", "ln_b", "ctxR", "kpad", "dcol",
          "gwT", "sguT", "sdT", "wguT", "wdT")


def decoder_layer(nc, i, out):
    def scratch(name, *shape):
        return nc.dram_tensor(name, list(shape), FP32).ap()

    a, bv = scratch("decays", B, H, T, DH), scratch("beta_v", B, H, T, DH)
    gram, beta = scratch("gram", B, H, T, 2 * T), scratch("beta", B, H, T)
    hist = scratch("history", 2, P, T - C, DH)
    o = scratch("heads_out", B, H, T, DH + 32)
    x1, x1T = scratch("x1", B, T, D), scratch("x1T", D, TOK)
    x2, x2T = scratch("x2", B, T, D), scratch("x2T", D, TOK)
    projections(nc, i["xT"], i["w_heads"], i["ba"], i["wbT"], i["bb_col"], i["bb_row"], a, bv, gram, beta)
    recurrence(nc, a, bv, gram, beta, hist, o)
    attention_out(nc, i["x"], i["xT"], o, i["wgT"], i["woT"], i["ln_g"], i["ln_b"], x1, x1T)
    long_conv(nc, i["ctxR"], i["kpad"], i["dcol"], x1, x1T, scratch("filters", HK, 3 * P), x2, x2T)
    experts(nc, x2, x2T, i["gwT"], i["sguT"], i["sdT"], i["wguT"], i["wdT"],
            scratch("expert_in", SLOTS, D), scratch("expert_out", SLOTS, D), out)


def host_layout(i):
    def c(a):
        return np.ascontiguousarray(a)
    x = np.asarray(i["x"])
    g = {k[len("L0_attn_"):]: np.asarray(v) for k, v in i.items() if k.startswith("L0_attn_")}
    w = np.stack([g[n].reshape(H, P, KT, P) for n in ("Wk", "Wq", "Wv", "Wa")])
    par = np.stack([np.concatenate([g[n + "_w"][:, 0, :], g[n + "_b"][:, None]], 1).reshape(H, P, TAPS + 1)
                    for n in ("kc", "qc", "vc")])
    ctx = np.asarray(i["ctx_2048"]).reshape(B, P, KT, P)[:, :, :, ::-1].transpose(3, 2, 0, 1)
    kpad = np.zeros((HK, 3 * P), np.float32)
    kpad[:, P - 1:P - 1 + D] = np.asarray(i["L0_xattn_ssm_kernel"])
    f = {k[len("L0_ffn_"):]: np.asarray(v) for k, v in i.items() if k.startswith("L0_ffn_")}
    wgu = np.stack([f["Wg"], f["Wu"]]).reshape(2, E, M, KT, P).transpose(1, 4, 3, 0, 2).reshape(E, P, -1)
    wd = f["Wd"].reshape(E, D, 2, M // 2).transpose(0, 3, 2, 1).reshape(E, M // 2, -1)
    sgu = np.stack([f["Sg"], f["Su"]]).reshape(2, MS, KT, P).transpose(3, 2, 0, 1)
    sd = f["Sd"].reshape(D, MS // (M // 2), M // 2).transpose(2, 1, 0)
    return dict(
        gwT=c(f["gate_weight"].T), sguT=c(sgu), sdT=c(sd), wguT=c(wgu), wdT=c(wd),
        ctxR=c(ctx), kpad=kpad, dcol=c(np.asarray(i["L0_xattn_D"])[:, None]),
        xT=c(x.reshape(TOK, D).T), w_heads=c(np.concatenate([w.transpose(1, 4, 3, 0, 2).reshape(H, P, -1), par.transpose(1, 2, 0, 3).reshape(H, P, -1)], 2)),
        ba=c(g["ba"][None, :]), wbT=c(g["Wb"].T), bb_col=c(g["bb"][:, None]), bb_row=c(g["bb"][None, :]),
        x=c(x), wgT=c(g["Wg"].T), woT=c(g["Wo"].T), ln_g=c(g["ln_g"][:, None]), ln_b=c(g["ln_b"][:, None]),
    )


def kernel(**inputs):
    import concourse.bacc as bacc
    from concourse.bass_utils import run_bass_kernel_spmd

    laid = host_layout(inputs)
    nc = bacc.Bacc("TRN2", target_bir_lowering=False, num_devices=1)
    handles = {n: nc.dram_tensor(f"in_{n}", laid[n].shape, mybir.dt.from_np(laid[n].dtype), kind="ExternalInput").ap()
               for n in INPUTS}
    out = nc.dram_tensor("out_0", (B, T, D), FP32, kind="ExternalOutput").ap()
    decoder_layer(nc, handles, out)
    r = run_bass_kernel_spmd(nc, [{f"in_{n}": laid[n] for n in INPUTS}], core_ids=[0])
    return r.results[0]["out_0"]
```

```python
from contextlib import ExitStack

import concourse.bass as bass
import numpy as np
from concourse import mybir

FP32 = mybir.dt.float32
BF16 = mybir.dt.bfloat16
INT32 = mybir.dt.int32
UINT32 = mybir.dt.uint32
ALU = mybir.AluOpType
ACT = mybir.ActivationFunctionType
AXIS_X = mybir.AxisListType.X

P = 128
B, T, D = 16, 128, 256
H, DH = 16, 128
KT = D // P
TOK = B * T
TAPS = 4
EPS = 1e-5
DMA = 16
C = 16
NCHUNK = T // C
HK, HD2 = 16, 8
E, M, TOPK, GROUPS, TOPG, CAP = 64, 176, 6, 8, 3, 96
MS = 352
SLOTS = E * CAP


class Pool:

    def __init__(self, nc, ctx):
        self.nc, self.ctx, self.sems = nc, ctx, []

    def sb(self, name, shape, dt=FP32):
        return self.ctx.enter_context(self.nc.sbuf_tensor(name, shape, dt))

    def ps(self, name, shape):
        return self.ctx.enter_context(self.nc.psum_tensor(name, shape, FP32))

    def sem(self, name):
        self.sems.append(self.ctx.enter_context(self.nc.semaphore(name)))
        return self.sems[-1]


def clear(nc, sems):
    numbers = sorted(s.num for s in sems)
    assert numbers == list(range(numbers[0], numbers[-1] + 1))
    with nc.Block() as block:
        @block.sync
        def _(sp):
            sp.sem_clear(range(numbers[0], numbers[-1] + 1))


def projections(nc, xT, w_heads, ba, wbT, bb_col, bb_row, a_dram, bv_dram, gram_dram, beta_dram):
    QB = 4
    NQ = B // QB
    KINDS = 3
    UNITS = NQ * KINDS
    K_SCALE, Q_SCALE = 1.0 / DH, float(DH) ** -0.5
    with ExitStack() as ctx:
        m = Pool(nc, ctx)
        x_sb = m.sb("p1_x", [P, KT, TOK])
        head_sb = [m.sb(f"p1_w{i}", [P, KT * 4 * P + KINDS * (TAPS + 1)]) for i in range(2)]
        w_sb = [t[:, 0:KT * 4 * P].rearrange("p (k s c) -> p k s c", k=KT, s=4) for t in head_sb]
        par = [t[:, KT * 4 * P:].rearrange("p (s x) -> p s x", s=KINDS) for t in head_sb]
        ba_sb, ba_part, ba_sel = (m.sb(f"p1_ba{n}", [3, H * P]) for n in ("", "_part", "_sel"))
        ba_low, ba_parts = (m.sb(f"p1_ba_{n}", [3, H * P], BF16) for n in ("low", "parts"))
        ones3 = m.sb("p1_ones3", [3, P], BF16)
        wb_sb = m.sb("p1_wb", [P, KT, H])
        bbc_sb = m.sb("p1_bbc", [H, 1])
        bbr_sb = m.sb("p1_bbr", [1, H])
        ones = m.sb("p1_ones", [1, P])
        ident = m.sb("p1_ident", [P, P])
        beta_t = m.sb("p1_beta_t", [P, B, H])
        beta_h = m.sb("p1_beta_h", [H, TOK])
        y = [m.sb(f"p1_y{i}", [P, QB * T]) for i in range(4)]
        sig = [m.sb(f"p1_sig{i}", [P, QB * T]) for i in range(2)]
        kq = [m.sb(f"p1_kq{i}", [P, QB, 2, T]) for i in range(2)]
        v = [m.sb(f"p1_v{i}", [P, QB, T]) for i in range(2)]
        gram = [m.sb(f"p1_gram{i}", [P, QB, NCHUNK, 2, C]) for i in range(2)]
        bv = [m.sb(f"p1_bv{i}", [P, QB, P]) for i in range(2)]
        dec = [m.sb(f"p1_dec{i}", [P, QB, P]) for i in range(2)]
        ps_proj = [m.ps(f"p1_ps_proj{i}", [P, QB * T]) for i in range(4)]
        ps_gram = m.ps("p1_ps_gram", [P, QB, 2 * T])
        ps_v = m.ps("p1_ps_v", [P, QB, P])
        ps_a = m.ps("p1_ps_a", [P, QB, P])

        w_loaded = [m.sem(f"p1_w_loaded{i}") for i in range(2)]
        consts = m.sem("p1_consts")
        made = m.sem("p1_made")
        split = m.sem("p1_split")
        SPLIT = 10
        beta_mm = m.sem("p1_beta_mm")
        beta_sig = m.sem("p1_beta_sig")
        beta_out = m.sem("p1_beta_out")
        proj_done = m.sem("p1_proj_done")
        y_init = m.sem("p1_y_init")
        tap = m.sem("p1_tap")
        conv_done = m.sem("p1_conv_done")
        sig_done = m.sem("p1_sig_done")
        silu_done = m.sem("p1_silu_done")
        gram_done = m.sem("p1_gram_done")
        a_done = m.sem("p1_a_done")
        gram_k_cp, gram_q_cp = m.sem("p1_gram_k_cp"), m.sem("p1_gram_q_cp")
        bv_cp = m.sem("p1_bv_cp")
        a_cp = m.sem("p1_a_cp")
        gram_out, bv_out, a_out = ([m.sem(f"p1_{n}_out{i}") for i in range(2)] for n in ("gram", "bv", "a"))
        block = ctx.enter_context(nc.Block())

        def last_head(hp, j):
            return isinstance(hp, int) and (hp, j) == (H // 2 - 1, 1)

        def first_units(hp, j, u):
            return isinstance(hp, int) and hp * 2 + j == 0 and u < 4

        def next_head(hp, j):
            return (hp, 1) if j == 0 else (hp + 1, 0)

        @block.sync
        def _(sp):
            sp.dma_start(x_sb[:], xT.rearrange("(k p) t -> p k t", p=P)).then_inc(consts, DMA)
            sp.dma_start(wb_sb[:], wbT.rearrange("(k p) h -> p k h", p=P)).then_inc(consts, DMA)
            sp.dma_start(bbc_sb[:], bb_col).then_inc(consts, DMA)
            sp.dma_start(bbr_sb[:], bb_row).then_inc(consts, DMA)
            sp.dma_start(ba_sb[:], ba.broadcast_to([3, H * P])).then_inc(consts, DMA)
            sp.wait_ge(beta_sig, 2)
            sp.dma_start(beta_dram.rearrange("b h t -> h b t"),
                         beta_h[:].rearrange("h (b t) -> h b t", b=B)).then_inc(beta_out, DMA)
            with sp.Fori(0, H // 2) as hp:
                for j in range(2):
                    h = hp * 2 + j
                    for n in range(NQ):
                        i = n % 2
                        at = hp * (2 * NQ) + j * NQ + n + 1
                        b0 = n * QB
                        sp.wait_ge(a_cp, at)
                        sp.dma_start(a_dram[b0:b0 + QB, bass.ds(h, 1), :, :].rearrange("b h t i -> t (b h) i"),
                                     dec[i][:]).then_inc(a_out[i], DMA)
                        sp.wait_ge(bv_cp, at)
                        sp.dma_start(bv_dram[b0:b0 + QB, bass.ds(h, 1), :, :].rearrange("b h t i -> t (b h) i"),
                                     bv[i][:]).then_inc(bv_out[i], DMA)
                        sp.wait_ge(gram_k_cp, at)
                        sp.wait_ge(gram_q_cp, at)
                        sp.dma_start(gram_dram[b0:b0 + QB, bass.ds(h, 1), :, :].rearrange("b h t i -> t (b h) i"),
                                     gram[i][:].rearrange("p b c s e -> p b (c s e)")).then_inc(gram_out[i], DMA)
            sp.wait_ge(beta_out, DMA)
            for i in range(2):
                sp.wait_ge(a_out[i], DMA * H * NQ // 2)
            for i in range(2):
                sp.wait_ge(bv_out[i], DMA * H * NQ // 2)
            for i in range(2):
                sp.wait_ge(gram_out[i], DMA * H * NQ // 2)

        @block.gpsimd
        def _(pool):
            nc.gpsimd.memset(ones[:], 1.0).then_inc(made, 1)
            nc.gpsimd.memset(ones3[:], 1.0).then_inc(made, 1)
            nc.gpsimd.memset(ident[:], 0.0).then_inc(made, 1)
            pool.wait_ge(made, 3)
            nc.gpsimd.affine_select(out=ident[:], in_=ident[:], compare_op=ALU.not_equal, fill=1.0, base=0,
                                    pattern=[[-1, P]], channel_multiplier=1).then_inc(made, 1)
            for j in range(2):
                pool.dma_start(head_sb[j][:], w_heads[j]).then_inc(w_loaded[j], DMA)
            with pool.Fori(0, H // 2) as hp:
                for j in range(2):
                    for u in range(UNITS):
                        n, kind = divmod(u, KINDS)
                        at = hp * (2 * UNITS) + j * UNITS + u + 1
                        pool.wait_ge(sig_done, at)
                        if j == 1 or n >= 2:
                            pool.wait_ge(gram_done, hp * (2 * NQ) + j * NQ + n - 1)
                        dst = v[n % 2][:].rearrange("p b t -> p b t") if kind == 2 else kq[n % 2][:, :, kind, :]
                        nc.gpsimd.tensor_tensor(out=dst, in0=y[u % 4][:].rearrange("p (b t) -> p b t", b=QB),
                                                in1=sig[u % 2][:].rearrange("p (b t) -> p b t", b=QB),
                                                op=ALU.mult).then_inc(silu_done, 1)
                    pool.wait_ge(a_done, hp * (2 * NQ) + (j + 1) * NQ)
                    pool.wait_ge(conv_done, hp * (2 * UNITS) + (j + 1) * UNITS)
                    pool.dma_start(head_sb[j][:], w_heads[bass.ds((hp * 2 + (j + 2)) % H, 1)]
                                   .rearrange("a p x -> p (a x)")).then_inc(w_loaded[j], DMA)
            for j in range(2):
                pool.wait_ge(w_loaded[j], DMA * (H // 2 + 1))

        @block.tensor
        def _(pe):
            pe.wait_ge(consts, DMA * 5)
            pe.wait_ge(made, 4)
            for q in range(NQ):
                for k in range(KT):
                    nc.tensor.matmul(ps_proj[q][0:H, :], wb_sb[:, k, :], x_sb[:, k, q * 512:(q + 1) * 512],
                                     start=(k == 0), stop=(k == KT - 1))
            for b in range(B):
                for k in range(KT):
                    nc.tensor.matmul(ps_gram[:, 0, b * H:(b + 1) * H],
                                     x_sb[:, k, b * T:(b + 1) * T], wb_sb[:, k, :], start=(k == 0), stop=False)
                last = nc.tensor.matmul(ps_gram[:, 0, b * H:(b + 1) * H], ones[:], bbr_sb[:], start=False, stop=True)
            last.then_inc(beta_mm, 1)
            pe.wait_ge(beta_sig, 2)
            pe.wait_ge(split, SPLIT)

            def project(hp, j, n):
                for kind in range(KINDS):
                    u = n * KINDS + kind
                    if not first_units(hp, j, u):
                        pe.wait_ge(conv_done, hp * (2 * UNITS) + j * UNITS + u - 3)
                    for k in range(KT):
                        last = nc.tensor.matmul(ps_proj[u % 4][:], w_sb[j][:, k, kind, :],
                                                x_sb[:, k, n * 512:(n + 1) * 512], start=(k == 0), stop=(k == KT - 1))
                    last.then_inc(proj_done, 1)

            def decays(hp, j, n):
                h = hp * 2 + j
                pe.wait_ge(a_cp, hp * (2 * NQ) + j * NQ + n)
                for b in range(QB):
                    t0 = (n * QB + b) * T
                    for k in range(KT):
                        nc.tensor.matmul(ps_a[:, b, :], x_sb[:, k, t0:t0 + T], w_sb[j][:, k, 3, :],
                                         start=(k == 0), stop=False)
                    last = nc.tensor.matmul(ps_a[:, b, :], ones3[:], ba_parts[:, bass.ds(h * P, P)], start=False, stop=True)
                last.then_inc(a_done, 1)

            def grams(hp, j, n):
                at = hp * (2 * NQ) + j * NQ + n
                pe.wait_ge(silu_done, hp * (2 * UNITS) + j * UNITS + (n + 1) * KINDS)
                pe.wait_ge(gram_k_cp, at)
                pe.wait_ge(gram_q_cp, at)
                pe.wait_ge(bv_cp, at)
                for b in range(QB):
                    nc.tensor.matmul(ps_gram[:, b, :], kq[n % 2][:, b, 0, :],
                                     kq[n % 2][:, b, :, :].rearrange("p s t -> p (s t)"), start=True, stop=True)
                for b in range(QB):
                    last = nc.tensor.transpose(ps_v[:, b, :], v[n % 2][:, b, :], ident[:])
                last.then_inc(gram_done, 1)

            def head(hp, j):
                for n in range(NQ):
                    if n + 1 < NQ:
                        project(hp, j, n + 1)
                    elif not last_head(hp, j):
                        nhp, nj = next_head(hp, j)
                        pe.wait_ge(w_loaded[nj], nhp * DMA + DMA)
                        project(nhp, nj, 0)
                    decays(hp, j, n)
                    grams(hp, j, n)

            pe.wait_ge(w_loaded[0], DMA)
            project(0, 0, 0)
            with pe.Fori(0, H // 2 - 1) as hp:
                for j in range(2):
                    head(hp, j)
            for j in range(2):
                head(H // 2 - 1, j)

        @block.scalar
        def _(act):
            act.wait_ge(beta_mm, 1)
            for q in range(NQ):
                last = nc.scalar.activation(beta_h[:, q * 512:(q + 1) * 512], ps_proj[q][0:H, :], ACT.Sigmoid,
                                            bias=bbc_sb[:, 0:1])
            last.then_inc(beta_sig, 1)
            nc.scalar.activation(beta_t[:].rearrange("p b h -> p (b h)"), ps_gram[:, 0, :], ACT.Sigmoid).then_inc(beta_sig, 1)

            def first_tap(hp, j, u):
                h = hp * 2 + j
                kind = u % KINDS
                at = hp * (2 * UNITS) + j * UNITS + u
                act.wait_ge(proj_done, at + 1)
                if not first_units(hp, j, u):
                    act.wait_ge(silu_done, at - 3)
                nc.scalar.activation(y[u % 4][:], ps_proj[u % 4][:], ACT.Identity,
                                     bias=par[j][:, kind, TAPS:TAPS + 1],
                                     scale=par[j][:, kind, TAPS - 1:TAPS]).then_inc(y_init, 1)

            def sigmoid(hp, j, u):
                at = hp * (2 * UNITS) + j * UNITS + u
                act.wait_ge(conv_done, at + 1)
                if j == 1 or u >= 2:
                    act.wait_ge(silu_done, at - 1)
                else:
                    act.wait_ge(silu_done, hp * (2 * UNITS))
                nc.scalar.activation(sig[u % 2][:], y[u % 4][:], ACT.Sigmoid).then_inc(sig_done, 1)

            def copies(hp, j, n):
                at = hp * (2 * NQ) + j * NQ + n
                i = n % 2
                act.wait_ge(a_out[i], hp * (NQ * DMA) + (j * NQ + n) // 2 * DMA)
                act.wait_ge(a_done, at + 1)
                nc.scalar.activation(dec[i][:], ps_a[:], ACT.Sigmoid).then_inc(a_cp, 1)
                act.wait_ge(gram_out[i], hp * (NQ * DMA) + (j * NQ + n) // 2 * DMA)
                act.wait_ge(gram_done, at + 1)
                for half, scale, done in ((0, K_SCALE, gram_k_cp), (1, Q_SCALE, gram_q_cp)):
                    nc.scalar.activation(gram[i][:, :, :, half, :],
                                         ps_gram[:, :, half * T:(half + 1) * T].rearrange("p b (c s) -> p b c s", c=NCHUNK),
                                         ACT.Copy, scale=scale).then_inc(done, 1)

            def head(hp, j):
                for n in range(NQ):
                    for kind in range(KINDS):
                        sigmoid(hp, j, n * KINDS + kind)
                        if n + 1 < NQ:
                            first_tap(hp, j, (n + 1) * KINDS + kind)
                        elif not last_head(hp, j):
                            first_tap(*next_head(hp, j), kind)
                    copies(hp, j, n)

            for kind in range(KINDS):
                first_tap(0, 0, kind)
            with act.Fori(0, H // 2 - 1) as hp:
                for j in range(2):
                    head(hp, j)
            for j in range(2):
                head(H // 2 - 1, j)

        @block.vector
        def _(dve):
            dve.wait_ge(consts, DMA * 5)
            dve.wait_ge(made, 4)
            at = 0

            def then(ins):
                nonlocal at
                at += 1
                ins.then_inc(split, 1)
                dve.wait_ge(split, at)

            for part in range(3):
                if part < 2:
                    then(nc.vector.tensor_copy(ba_low[:], ba_sb[:]))
                    then(nc.vector.tensor_copy(ba_part[:], ba_low[:]))
                    piece = ba_part
                else:
                    piece = ba_sb
                mine = ident[0:3, part:part + 1]
                if part == 0:
                    then(nc.vector.tensor_scalar(ba_sel[:], piece[:], mine, None, ALU.mult))
                else:
                    then(nc.vector.scalar_tensor_tensor(out=ba_sel[:], in0=piece[:], scalar=mine, in1=ba_sel[:],
                                                        op0=ALU.mult, op1=ALU.add))
                if part < 2:
                    then(nc.vector.tensor_tensor(out=ba_sb[:], in0=ba_sb[:], in1=ba_part[:], op=ALU.subtract))
            then(nc.vector.tensor_copy(ba_parts[:], ba_sel[:]))
            assert at == SPLIT, at
            dve.wait_ge(beta_sig, 2)

            def conv(hp, j, u):
                kind = u % KINDS
                at = hp * (2 * UNITS) + j * UNITS + u
                dve.wait_ge(y_init, at + 1)
                yv = y[u % 4][:].rearrange("p (b t) -> p b t", b=QB)
                pv = ps_proj[u % 4][:].rearrange("p (b t) -> p b t", b=QB)
                for s in range(1, TAPS):
                    if s > 1:
                        dve.wait_ge(tap, at * 2 + s - 1)
                    nc.vector.scalar_tensor_tensor(
                        out=yv[:, :, s:], in0=pv[:, :, 0:T - s],
                        scalar=par[j][:, kind, TAPS - 1 - s:TAPS - s],
                        in1=yv[:, :, s:], op0=ALU.mult, op1=ALU.add).then_inc(
                            tap if s < TAPS - 1 else conv_done, 1)

            def head(hp, j):
                for n in range(NQ):
                    for kind in range(KINDS):
                        if n + 1 < NQ:
                            conv(hp, j, (n + 1) * KINDS + kind)
                        elif not last_head(hp, j):
                            conv(*next_head(hp, j), kind)
                    at = hp * (2 * NQ) + j * NQ + n
                    dve.wait_ge(gram_done, at + 1)
                    dve.wait_ge(bv_out[n % 2], hp * (NQ * DMA) + (j * NQ + n) // 2 * DMA)
                    for b in range(QB):
                        last = nc.vector.tensor_scalar(
                            bv[n % 2][:, b, :], ps_v[:, b, :],
                            beta_t[:, n * QB + b, bass.ds(hp * 2 + j, 1)], None, ALU.mult)
                    last.then_inc(bv_cp, 1)

            for kind in range(KINDS):
                conv(0, 0, kind)
            with dve.Fori(0, H // 2 - 1) as hp:
                for j in range(2):
                    head(hp, j)
            for j in range(2):
                head(H // 2 - 1, j)
        used = m.sems
    clear(nc, used)


def recurrence(nc, a_dram, bv_dram, gram_dram, beta_dram, hist_dram, o_dram):
    GR = 2
    BG = B // GR
    HU = H // 4
    UB = H // HU
    UNITS = BG * UB
    NTURN = 8
    HALF = C // 2
    OLD = T - 2 * C
    ROUNDS = NCHUNK - 1
    DROWS = 2 * C
    PIECE = 2 * C
    RZ = 6
    RO = 8
    LEAVES = GR * NCHUNK
    ORDER = ((0, 3, 12, 10, 4), (3, ROUNDS, 14, 8, 5))
    with ExitStack() as ctx:
        m = Pool(nc, ctx)
        hist = [m.sb(f"p2_hist{g}", [P, OLD, DH]) for g in range(GR)]
        zo = [m.sb(f"p2_zo{g}", [P, 2, C, DH]) for g in range(GR)]
        dec = [m.sb(f"p2_dec{half}", [P, HALF, DH]) for half in range(2)]
        gd = [m.sb(f"p2_gd{g}", [P, C, 2 * C]) for g in range(GR)]
        beta = [m.sb(f"p2_beta{g}", [P, C]) for g in range(GR)]
        w = [m.sb(f"p2_w{g}", [P, C + 1, DH]) for g in range(GR)]
        pp = m.sb("p2_pp", [P, HALF, DH])
        turned = [m.sb(f"p2_turned{i}", [C + OLD, HU, DH]) for i in range(NTURN)]
        gcol = [m.sb(f"p2_gcol{i}", [C + OLD, HU, 2 * C]) for i in range(NTURN)]
        z_turn = m.sb("p2_z_turn", [DH, P, 2 * C])
        x_o = m.sb("p2_x_o", [P, 4, DH])
        ident = m.sb("p2_ident", [P, P])
        NDZ, NDO = 2, 2
        DZ, DO = RZ // 2, RO // 2
        diag_z = [m.sb(f"p2_diag_z{i}", [P, DZ, P]) for i in range(NDZ)]
        diag_o = [m.sb(f"p2_diag_o{i}", [P, DO, P]) for i in range(NDO)]
        ps_z = [m.ps(f"p2_ps_z{i}", [DH, H, 2 * C]) for i in range(2)]
        ps_t = [m.ps(f"p2_ps_t{i}", [P, 4, DH]) for i in range(2)]
        ps_x = [m.ps(f"p2_ps_x{i}", [P, 4, DH]) for i in range(4)]
        Z_FILLS = ((0, 1), (1, 2), (2, 4), (4, 6), (6, 8))
        O_FILLS = ((0, 4), (4, 8))
        FILLS = len(Z_FILLS) + len(O_FILLS)
        O_BANK = 1
        DUNITS = HALF * 2

        zo_zero = m.sem("p2_zo_zero")
        cleared = m.sem("p2_cleared")
        lo_in = m.sem("p2_lo_in")
        hi_in = m.sem("p2_hi_in")
        bv_in = [m.sem(f"p2_bv_in{g}") for g in range(GR)]
        gd_in = [m.sem(f"p2_gd_in{g}") for g in range(GR)]
        step_done = m.sem("p2_step_done")
        half_done = m.sem("p2_half_done")
        leaf_done = m.sem("p2_leaf_done")
        diag_z_made = m.sem("p2_diag_z_made")
        diag_o_made = m.sem("p2_diag_o_made")
        diag_z_used = m.sem("p2_diag_z_used")
        diag_o_used = m.sem("p2_diag_o_used")
        x_done = m.sem("p2_x_done")
        x_z_read = m.sem("p2_x_z_read")
        o_copied = m.sem("p2_o_copied")
        o_scaled = m.sem("p2_o_scaled")
        o_final = m.sem("p2_o_final")
        o_out = [m.sem(f"p2_o_out{g}") for g in range(GR)]
        hist_done = [m.sem(f"p2_hist_done{g}") for g in range(GR)]
        first_rows = [m.sem(f"p2_first_rows{g}") for g in range(GR)]
        kept = [m.sem(f"p2_kept{g}") for g in range(GR)]
        turned_in = [m.sem(f"p2_turned_in{i}") for i in range(NTURN)]
        mm_done = m.sem("p2_mm_done")
        u_saved = [m.sem(f"p2_u_saved{g}") for g in range(GR)]
        hist_saved = [m.sem(f"p2_hist_saved{g}") for g in range(GR)]
        z_cp = m.sem("p2_z_cp")
        t_done = m.sem("p2_t_done")
        t_cp = m.sem("p2_t_cp")
        zo_ready = [m.sem(f"p2_zo_ready{g}") for g in range(GR)]
        TD = 2
        TB = 2 * C // 4
        FREE = 1
        with nc.Block() as start:
            @start.sync
            def _(sp):
                for sem in (*zo_ready, o_final, mm_done, z_cp, t_done, t_cp):
                    sp.sem_inc(sem, FREE)
                sp.sem_inc(diag_o_used, NDO)
        block = ctx.enter_context(nc.Block())
        TRI = HALF * (HALF + 1) // 2
        STEPS = ((HALF - 1) + (TRI - HALF) + HALF + TRI + 2 * HALF
                 + 2 + HALF * (2 * HALF - RZ - RO) + len(Z_FILLS)
                 + (HALF - 1) + (TRI - HALF) + HALF + TRI + 3 * HALF - 1 + 1)

        def pieces(c):
            return [(r, min(PIECE, c * C - r)) for r in range(DROWS, c * C, PIECE)]

        def carried(c):
            return sum(len(pieces(before)) for before in range(c))

        def seq_rows(dram, g, t0, n):
            return dram[g * BG:(g + 1) * BG, :, bass.ds(t0, n), :].rearrange("b h t i -> (b h) t i")

        def o_share(g):
            return zo[g][:, 0, 1 + HALF:5 + HALF, :], x_o[:]

        def following(c, g):
            return (c, g + 1) if g + 1 < GR else (c + 1, 0)

        @block.vector
        def _(dve):
            for g in range(GR):
                nc.vector.memset(zo[g][:], 0.0).then_inc(zo_zero, 1)
                nc.vector.memset(hist[g][:, 0:DROWS], 0.0).then_inc(zo_zero, 1)

            def leaf(c, g):
                at = c * GR + g
                base = c * (GR * STEPS) + g * STEPS
                count = [0]

                def done(ins):
                    count[0] += 1
                    ins.then_inc(step_done, 1)
                    return count[0]

                def after(n):
                    if n:
                        dve.wait_ge(step_done, base + n)

                def mul(out, in0, in1):
                    return done(nc.vector.tensor_tensor(out=out, in0=in0, in1=in1, op=ALU.mult))

                def add_scaled(acc, row, scalar):
                    return done(nc.vector.scalar_tensor_tensor(out=acc, in0=row, scalar=scalar, in1=acc,
                                                               op0=ALU.mult, op1=ALU.add))

                def take_u(s):
                    return done(nc.vector.scalar_tensor_tensor(
                        out=w[g][:, 1 + s, :], in0=zo[g][:, 0, s, :], scalar=beta[g][:, s:s + 1],
                        in1=w[g][:, 1 + s, :], op0=ALU.mult, op1=ALU.subtract, reverse1=True))

                dve.wait_ge(lo_in, c * (GR * DMA) + (g + 1) * DMA)
                dve.wait_ge(bv_in[g], c * DMA + DMA)
                dve.wait_ge(gd_in[g], c * (2 * DMA) + 2 * DMA)
                dve.wait_ge(zo_ready[g], c + FREE)
                dve.wait_ge(zo_zero, 2 * GR)
                w_at = z_at = o_at = u_at = 0
                for s in range(HALF + 1):
                    if s == HALF:
                        after(w_at)
                        dve.sem_inc(half_done, 1)
                    for r in range(-1, s):
                        if 0 < s < HALF:
                            after(max(z_at, w_at))
                            if r < 0:
                                z_at = mul(zo[g][:, 0, s, :], zo[g][:, 0, s, :], w[g][:, 0, :])
                            else:
                                z_at = add_scaled(zo[g][:, 0, s, :], w[g][:, 1 + r, :], gd[g][:, r, s:s + 1])
                        if s > 0:
                            after(max(o_at, w_at, u_at))
                            if r < 0:
                                o_at = mul(zo[g][:, 1, s - 1, :], zo[g][:, 1, s - 1, :], w[g][:, 0, :])
                            else:
                                o_at = add_scaled(zo[g][:, 1, s - 1, :], w[g][:, 1 + r, :], gd[g][:, r, C + s - 1:C + s])
                    if s < HALF:
                        after(z_at)
                        u_at = take_u(s)
                        after(max(z_at, o_at, u_at if s == HALF - 1 else 0))
                        if s == 0:
                            w_at = done(nc.vector.tensor_copy(w[g][:, 0, :], dec[0][:, 0, :]))
                        else:
                            w_at = mul(w[g][:, 0:1 + s, :], w[g][:, 0:1 + s, :],
                                       dec[0][:, s:s + 1, :].broadcast_to([P, 1 + s, DH]))
                for f in range(2):
                    h_at = mul(zo[g][:, f, HALF:, :], zo[g][:, f, HALF:, :], w[g][:, 0:1, :].broadcast_to([P, HALF, DH]))
                dve.wait_ge(hi_in, c * (GR * DMA) + (g + 1) * DMA)
                dve.wait_ge(o_final, c * (GR * len(O_FILLS)) + g * len(O_FILLS) + FREE)
                for f, rows in ((0, range(RZ, HALF)), (1, range(RO, HALF))):
                    for r in rows:
                        after(h_at)
                        for k in range(HALF):
                            h_at = add_scaled(zo[g][:, f, HALF + k, :], w[g][:, 1 + r, :],
                                              gd[g][:, r, f * C + HALF + k:f * C + HALF + k + 1])
                z_at = o_at = h_at
                w_at = u_at = p_at = 0
                fill = 0
                for k in range(HALF + 1):
                    s = HALF + k
                    if fill < len(Z_FILLS) and Z_FILLS[fill][0] == k:
                        k0, k1 = Z_FILLS[fill]
                        fill += 1
                        dve.wait_ge(x_done, c * (GR * FILLS) + g * FILLS + fill)
                        after(h_at)
                        z_at = count[0] + 1
                        count[0] += 1
                        nc.vector.tensor_tensor(out=zo[g][:, 0, HALF + k0:HALF + k1, :],
                                                in0=zo[g][:, 0, HALF + k0:HALF + k1, :],
                                                in1=ps_x[(fill - 1) % 4][:, 0:k1 - k0, :], op=ALU.add).then_inc(step_done, 1)
                        after(z_at)
                        dve.sem_inc(x_z_read, 1)
                    for r in range(-1, k):
                        if 0 < k < HALF:
                            after(max(z_at, w_at, p_at))
                            if r < 0:
                                z_at = mul(zo[g][:, 0, s, :], zo[g][:, 0, s, :], pp[:, k - 1, :])
                            else:
                                z_at = add_scaled(zo[g][:, 0, s, :], w[g][:, 1 + HALF + r, :], gd[g][:, HALF + r, s:s + 1])
                        if k > 0:
                            after(max(o_at, w_at, u_at, p_at))
                            if r < 0:
                                o_at = mul(zo[g][:, 1, s - 1, :], zo[g][:, 1, s - 1, :], pp[:, k - 1, :])
                            else:
                                o_at = add_scaled(zo[g][:, 1, s - 1, :], w[g][:, 1 + HALF + r, :],
                                                  gd[g][:, HALF + r, C + s - 1:C + s])
                    if k < HALF:
                        after(z_at)
                        u_at = take_u(s)
                        if k == 0:
                            p_at = done(nc.vector.tensor_copy(pp[:, 0, :], dec[1][:, 0, :]))
                        else:
                            p_at = mul(pp[:, k, :], pp[:, k - 1, :], dec[1][:, k, :])
                            after(max(z_at, o_at))
                            w_at = mul(w[g][:, 1 + HALF:1 + s, :], w[g][:, 1 + HALF:1 + s, :],
                                       dec[1][:, k:k + 1, :].broadcast_to([P, k, DH]))
                mul(zo[g][:, 0, 0:1 + HALF, :], w[g][:, 0:1 + HALF, :], pp[:, HALF - 1:HALF, :].broadcast_to([P, 1 + HALF, DH]))
                assert count[0] == STEPS, (count[0], STEPS)
                after(count[0])
                dve.sem_inc(leaf_done, 1)
                nc.vector.tensor_tensor(out=hist[g][:, 0:DROWS], in0=hist[g][:, 0:DROWS],
                                        in1=zo[g][:, 0, 0:1, :].broadcast_to([P, DROWS, DH]),
                                        op=ALU.mult).then_inc(first_rows[g], 1)

            with dve.Fori(0, NCHUNK) as c:
                for g in range(GR):
                    leaf(c, g)

        @block.gpsimd
        def _(pool):
            def load_half(c, g, half):
                pool.dma_start(dec[half][:], seq_rows(a_dram, g, c * C + half * HALF, HALF)).then_inc((lo_in, hi_in)[half], DMA)

            def load_gram(c, g):
                pool.dma_start(w[g][:, 1:, :], seq_rows(bv_dram, g, c * C, C)).then_inc(bv_in[g], DMA)
                pool.dma_start(gd[g][:], gram_dram[g * BG:(g + 1) * BG, :, bass.ds(c * C, C), bass.ds(c * (2 * C), 2 * C)]
                               .rearrange("b h t e -> (b h) t e")).then_inc(gd_in[g], DMA)
                pool.dma_start(beta[g][:], beta_dram[g * BG:(g + 1) * BG, :, bass.ds(c * C, C)]
                               .rearrange("b h t -> (b h) t")).then_inc(gd_in[g], DMA)

            def diagonals(c, g, load_next=True):
                at = c * (GR * DUNITS) + g * DUNITS
                pool.wait_ge(gd_in[g], c * (2 * DMA) + 2 * DMA)
                for u in range(DUNITS):
                    if u == NDZ and load_next:
                        pool.wait_ge(half_done, c * GR + g + 1)
                        load_half(*following(c, g), 0)
                    k, r0 = u // 2, u % 2 * DZ
                    if not (u < NDZ and isinstance(c, int) and c == 0 and g == 0):
                        pool.wait_ge(diag_z_used, at + u + 1 - NDZ)
                    nc.gpsimd.tensor_tensor(out=diag_z[u % NDZ][:], in0=ident[:].unsqueeze(1).broadcast_to([P, DZ, P]),
                                            in1=gd[g][:, r0:r0 + DZ, HALF + k:HALF + k + 1].broadcast_to([P, DZ, P]),
                                            op=ALU.mult).then_inc(diag_z_made, 1)

            def outputs(c, g):
                n = len(O_FILLS)
                for j, (k0, k1) in enumerate(O_FILLS):
                    pool.wait_ge(o_copied, c * (GR * n) + g * n + j + 1)
                    nc.gpsimd.tensor_tensor(out=pp[:, k0:k1, :], in0=o_share(g)[j], in1=pp[:, k0:k1, :],
                                            op=ALU.mult).then_inc(o_scaled, 1)
                    pool.wait_ge(o_scaled, c * (GR * n) + g * n + j + 1)
                    nc.gpsimd.tensor_tensor(out=zo[g][:, 1, HALF + k0:HALF + k1, :], in0=zo[g][:, 1, HALF + k0:HALF + k1, :],
                                            in1=pp[:, k0:k1, :], op=ALU.add).then_inc(o_final, 1)
                pool.wait_ge(o_final, c * (GR * n) + (g + 1) * n + FREE)
                pool.dma_start(seq_rows(o_dram, g, c * C, C)[:, :, 0:DH], zo[g][:, 1]).then_inc(o_out[g], DMA)

            load_half(0, 0, 0)
            load_gram(0, 0)
            load_half(0, 0, 1)
            load_gram(0, 1)
            for i in range(NTURN):
                nc.gpsimd.memset(turned[i][:], 0.0).then_inc(cleared, 1)
                nc.gpsimd.memset(gcol[i][:], 0.0).then_inc(cleared, 1)
            nc.gpsimd.memset(ident[:], 0.0).then_inc(cleared, 1)
            pool.wait_ge(cleared, 2 * NTURN + 1)
            nc.gpsimd.affine_select(out=ident[:], in_=ident[:], compare_op=ALU.not_equal, fill=1.0, base=0,
                                    pattern=[[-1, P]], channel_multiplier=1).then_inc(cleared, 1)
            pool.wait_ge(cleared, 2 * NTURN + 2)
            diagonals(0, 0)
            for c in range(ROUNDS):
                for g in range(GR):
                    pool.wait_ge(leaf_done, c * GR + g + 1)
                    if c:
                        pool.wait_ge(kept[g], c * 2)
                    for j, (r0, rows) in enumerate(pieces(c)):
                        if j == 1:
                            load_half(*following(c, g), 1)
                        nc.gpsimd.tensor_tensor(out=hist[g][:, r0:r0 + rows], in0=hist[g][:, r0:r0 + rows],
                                                in1=zo[g][:, 0, 0:1, :].broadcast_to([P, rows, DH]),
                                                op=ALU.mult).then_inc(hist_done[g], 1)
                    if len(pieces(c)) < 2:
                        load_half(*following(c, g), 1)
                    pool.wait_ge(first_rows[g], c + 1)
                    if c + 1 < ROUNDS:
                        nc.gpsimd.tensor_copy(hist[g][:, c * C:c * C + HALF, :], zo[g][:, 0, 1:1 + HALF, :]).then_inc(kept[g], 1)
                        nc.gpsimd.tensor_copy(hist[g][:, c * C + HALF:(c + 1) * C, :], w[g][:, 1 + HALF:, :]).then_inc(kept[g], 1)
                        pool.wait_ge(kept[g], (c + 1) * 2)
                    outputs(c, g)
                    pool.wait_ge(u_saved[g], (c + 1) * 2 * DMA)
                    load_gram(c + 1, g)
                    diagonals(*following(c, g))
            last = NCHUNK - 1
            pool.wait_ge(leaf_done, last * GR + 1)
            load_half(last, 1, 1)
            outputs(last, 0)
            diagonals(last, 1, load_next=False)
            pool.wait_ge(leaf_done, LEAVES)
            outputs(last, 1)
            for g in range(GR):
                pool.wait_ge(o_out[g], DMA * NCHUNK)

        @block.sync
        def _(sp):
            def by_seq(g, r0, n):
                return hist_dram[g, r0:r0 + n].rearrange("r p i -> p r i")

            for c in range(ROUNDS):
                rows, t1 = (c + 1) * C, (c + 1) * 2 * C
                for g in range(GR):
                    sp.wait_ge(leaf_done, c * GR + g + 1)
                    sp.dma_start(by_seq(g, c * C, HALF), zo[g][:, 0, 1:1 + HALF, :]).then_inc(u_saved[g], DMA)
                    sp.dma_start(by_seq(g, c * C + HALF, HALF), w[g][:, 1 + HALF:, :]).then_inc(u_saved[g], DMA)
                    if c:
                        sp.wait_ge(first_rows[g], c + 1)
                        n = min(DROWS, c * C)
                        sp.dma_start(by_seq(g, 0, n), hist[g][:, 0:n]).then_inc(hist_saved[g], DMA)
                    for j, (r0, n) in enumerate(pieces(c)):
                        sp.wait_ge(hist_done[g], carried(c) + j + 1)
                        sp.dma_start(by_seq(g, r0, n), hist[g][:, r0:r0 + n]).then_inc(hist_saved[g], DMA)
                    for u in range(UNITS):
                        n = g * UNITS + u
                        i = n % NTURN
                        b, h0 = u // UB, u % UB * HU
                        if c or n >= NTURN:
                            sp.wait_ge(mm_done, c * (GR * UNITS) + n - NTURN + 1 + FREE)
                        sp.dma_start(gcol[i][0:rows], gram_dram[g * BG + b, h0:h0 + HU, 0:rows, t1:t1 + 2 * C]
                                     .rearrange("h r e -> r h e")).then_inc(turned_in[i], DMA)
                        if u == 0:
                            sp.wait_ge(u_saved[g], (c + 1) * 2 * DMA)
                            if c:
                                sp.wait_ge(hist_saved[g], (carried(c + 1) + c) * DMA)
                        sp.dma_start(turned[i][0:rows], hist_dram[g, 0:rows, u * HU:(u + 1) * HU]).then_inc(turned_in[i], DMA)

        @block.tensor
        def _(pe):
            pe.wait_ge(cleared, 2 * NTURN + 2)

            def cross_z(c, g, between=lambda u: None):
                at = c * (GR * DUNITS) + g * DUNITS
                pe.wait_ge(half_done, c * GR + g + 1)
                if not (isinstance(c, int) and c == 0 and g == 0):
                    pe.wait_ge(o_copied, c * (GR * len(O_FILLS)) + g * len(O_FILLS))
                u = 0
                for j, (k0, k1) in enumerate(Z_FILLS):
                    if j == 4:
                        pe.wait_ge(x_z_read, c * (GR * len(Z_FILLS)) + g * len(Z_FILLS) + 1)
                    for k in range(k0, k1):
                        for q in range(2):
                            pe.wait_ge(diag_z_made, at + u + 1)
                            for e in range(DZ):
                                r = q * DZ + e
                                last = nc.tensor.matmul(ps_x[j % 4][:, k - k0, :], diag_z[u % NDZ][:, e, :], w[g][:, 1 + r, :],
                                                        start=(r == 0), stop=(r == RZ - 1))
                            last.then_inc(diag_z_used, 1)
                            u += 1
                            if not (k == k1 - 1 and q == 1):
                                between(u)
                    pe.wait_ge(diag_z_used, at + u)
                    pe.sem_inc(x_done, 1)
                    between(u)

            def cross_o(c, g, between=lambda u: None):
                at = c * (GR * DUNITS) + g * DUNITS
                pe.wait_ge(x_z_read, c * (GR * len(Z_FILLS)) + g * len(Z_FILLS) + 3)
                u = 0
                for j, (k0, k1) in enumerate(O_FILLS):
                    for k in range(k0, k1):
                        for q in range(2):
                            pe.wait_ge(diag_o_made, at + u + 1)
                            for e in range(DO):
                                r = q * DO + e
                                last = nc.tensor.matmul(ps_x[O_BANK + j][:, k - k0, :], diag_o[u % NDO][:, e, :],
                                                        w[g][:, 1 + r, :], start=(r == 0), stop=(r == RO - 1))
                            last.then_inc(diag_o_used, 1)
                            u += 1
                            between(u)
                    pe.wait_ge(diag_o_used, at + u + NDO)
                    pe.sem_inc(x_done, 1)

            cross_z(0, 0)
            for c0, c1, o_units, first, z_units in ORDER:
                with pe.Fori(c0, c1) as c:
                    for g in range(GR):
                        def history(u):
                            n = g * UNITS + u
                            i = n % NTURN
                            k = g * BG + u // UB
                            pe.wait_ge(turned_in[i], c * (GR * UNITS // NTURN * TD * DMA) + (n // NTURN + 1) * TD * DMA)
                            pe.wait_ge(z_cp, (c * (GR * BG) + k - 1 if k >= 2 else c * (GR * BG)) + FREE)
                            for h in range(HU):
                                last = nc.tensor.matmul(ps_z[k % 2][:, u % UB * HU + h, :], turned[i][:, h, :],
                                                        gcol[i][:, h, :], start=True, stop=True)
                            last.then_inc(mm_done, 1)

                        todo = list(range(UNITS))

                        def history_past(units):
                            def between(u):
                                if todo and u > units:
                                    history(todo.pop(0))
                            return between

                        cross_o(c, g, history_past(o_units))
                        for _ in range(min(first, len(todo))):
                            history(todo.pop(0))
                        cross_z(*following(c, g), history_past(z_units))
                        for u in todo:
                            history(u)
                        pe.wait_ge(z_cp, c * (GR * BG) + (g + 1) * BG + FREE)
                        for t in range(TB):
                            k = g * TB + t
                            pe.wait_ge(t_cp, (c * (GR * TB) + k - 1 if k >= 2 else c * (GR * TB)) + FREE)
                            for e in range(4):
                                last = nc.tensor.transpose(ps_t[t % 2][:, e, :], z_turn[:, :, t * 4 + e], ident[:])
                            last.then_inc(t_done, 1)
            cross_o(NCHUNK - 1, 0)
            cross_z(NCHUNK - 1, 1)
            cross_o(NCHUNK - 1, 1)

        @block.scalar
        def _(act):
            act.wait_ge(cleared, 2 * NTURN + 2)

            def diagonals(c, g, between=lambda u: None):
                at = c * (GR * DUNITS) + g * DUNITS
                act.wait_ge(half_done, c * GR + g + 1)
                for u in range(DUNITS):
                    k, r0 = u // 2, u % 2 * DO
                    act.wait_ge(diag_o_used, at + u + 1)
                    for e in range(DO):
                        last = nc.scalar.activation(diag_o[u % NDO][:, e, :], ident[:], ACT.Copy,
                                                    scale=gd[g][:, r0 + e, C + HALF + k:C + HALF + k + 1])
                    last.then_inc(diag_o_made, 1)
                    between(u + 1)
                act.wait_ge(leaf_done, c * GR + g + 1)
                for j, dst in enumerate(o_share(g)):
                    act.wait_ge(x_done, c * (GR * FILLS) + g * FILLS + len(Z_FILLS) + j + 1)
                    nc.scalar.copy(dst, ps_x[O_BANK + j][:]).then_inc(o_copied, 1)

            for c0, c1, o_units, _, _ in ORDER:
                with act.Fori(c0, c1) as c:
                    for g in range(GR):
                        todo = list(range(BG))

                        def batch_row(b):
                            k = g * BG + b
                            act.wait_ge(mm_done, c * (GR * UNITS) + (k + 1) * UB + FREE)
                            if b == 0:
                                act.wait_ge(t_done, c * (GR * TB) + g * TB + FREE)
                            nc.scalar.copy(z_turn[:, b * H:(b + 1) * H, :], ps_z[k % 2][:]).then_inc(z_cp, 1)

                        def between(u):
                            if todo and u > o_units + (todo[0] + 1) * UB:
                                batch_row(todo.pop(0))

                        diagonals(c, g, between)
                        for b in todo:
                            batch_row(b)
                        act.wait_ge(o_out[g], c * DMA + DMA)
                        act.wait_ge(u_saved[g], c * (2 * DMA) + 2 * DMA)
                        for t in range(TB):
                            act.wait_ge(t_done, c * (GR * TB) + g * TB + t + 1 + FREE)
                            nc.scalar.copy(zo[g][:].rearrange("p f s i -> p (f s) i")[:, 4 * t:4 * t + 4, :],
                                           ps_t[t % 2][:]).then_inc(t_cp, 1)
                        act.wait_ge(t_cp, c * (GR * TB) + (g + 1) * TB + FREE)
                        act.sem_inc(zo_ready[g], 1)
            for g in range(GR):
                diagonals(NCHUNK - 1, g)
                act.wait_ge(o_scaled, LEAVES * len(O_FILLS) - (GR - 1 - g) * len(O_FILLS))
        used = m.sems
    clear(nc, used)


class Steps:

    def __init__(self, eng, sem, base):
        self.eng, self.sem, self.base, self.n = eng, sem, base, 0

    def done(self, ins):
        ins.then_inc(self.sem, 1)
        self.n += 1
        return self.n

    def after(self, n):
        self.eng.wait_ge(self.sem, self.base + n)


def moments(nc, st, stats, mean, var, tmp, width):
    me, ce, mo, co = (stats[:, :, i] for i in (1, 2, 4, 5))
    diff = st.done(nc.vector.tensor_tensor(out=tmp, in0=me, in1=mo, op=ALU.subtract))
    total = st.done(nc.vector.tensor_tensor(out=mean, in0=me, in1=mo, op=ALU.add))
    m2 = st.done(nc.vector.tensor_tensor(out=var, in0=ce, in1=co, op=ALU.add))
    st.after(diff)
    square = st.done(nc.vector.scalar_tensor_tensor(out=tmp, in0=tmp, scalar=0.25, in1=tmp, op0=ALU.mult, op1=ALU.mult))
    st.after(total)
    half = st.done(nc.vector.tensor_scalar(mean, mean, 0.5, None, ALU.mult))
    st.after(m2)
    scaled = st.done(nc.vector.tensor_scalar(var, var, 1.0 / width, EPS, ALU.mult, ALU.add))
    st.after(max(square, half, scaled))
    st.after(st.done(nc.vector.tensor_tensor(out=var, in0=var, in1=tmp, op=ALU.add)))


MOMENT_STEPS = 7


def attention_out(nc, x, xT, o_dram, wgT, woT, ln_g, ln_b, x1_dram, x1T_dram):
    PB = 2
    PAIRS = B // PB
    HEADS4 = H // 4
    with ExitStack() as ctx:
        m = Pool(nc, ctx)
        xT_sb = m.sb("p3_xT", [P, KT, TOK])
        wg = m.sb("p3_wg", [P, KT, H * DH])
        wo = m.sb("p3_wo", [DH, H, D])
        lg, lb = m.sb("p3_lg", [DH, 1]), m.sb("p3_lb", [DH, 1])
        ident = m.sb("p3_ident", [P, P])
        neg_half = m.sb("p3_neg_half", [P, H])
        o = [m.sb(f"p3_o{b}", [T, H, DH]) for b in range(PB)]
        xr = [m.sb(f"p3_x{b}", [T, D]) for b in range(PB)]
        on = [m.sb(f"p3_on{b}", [T, H, DH]) for b in range(PB)]
        stats = [m.sb(f"p3_stats{b}", [T, H, 6]) for b in range(PB)]
        hm = [m.sb(f"p3_hm{b}", [T, H]) for b in range(PB)]
        hr = [m.sb(f"p3_hr{b}", [T, H]) for b in range(PB)]
        ht = [m.sb(f"p3_ht{b}", [T, H]) for b in range(PB)]
        gate = [m.sb(f"p3_gate{j}", [DH, H, PB, T]) for j in range(2)]
        y = [m.sb(f"p3_y{b}", [DH, H, T]) for b in range(PB)]
        res = [m.sb(f"p3_res{b}", [T, D]) for b in range(PB)]
        x1 = [m.sb(f"p3_x1{b}", [T, D]) for b in range(PB)]
        x1t = [m.sb(f"p3_x1t{b}", [P, KT, T]) for b in range(PB)]
        rstats = m.sb("p3_rstats", [T, PB, 6])
        rm, rr, rt = (m.sb(f"p3_r{n}", [T, PB]) for n in "mrt")
        ps_g = [m.ps(f"p3_ps_g{i}", [DH, 2, PB * T]) for i in range(2)]
        ps_t = [m.ps(f"p3_ps_t{i}", [DH, 4, T]) for i in range(2)]
        ps_o = [m.ps(f"p3_ps_o{b}", [T, 2 * D]) for b in range(PB)]
        ps_x = [m.ps(f"p3_ps_x{b}", [P, 4, T]) for b in range(PB)]

        gate_in = m.sem("p3_gate_in")
        consts = m.sem("p3_consts")
        made = m.sem("p3_made")
        o_in = [m.sem(f"p3_o_in{b}") for b in range(PB)]
        x_in = [m.sem(f"p3_x_in{b}") for b in range(PB)]
        gate_mm, gate_sig = m.sem("p3_gate_mm"), m.sem("p3_gate_sig")
        steps = m.sem("p3_steps")
        head_var, head_rstd = m.sem("p3_head_var"), m.sem("p3_head_rstd")
        row_var, row_rstd = m.sem("p3_row_var"), m.sem("p3_row_rstd")
        normed = m.sem("p3_normed")
        turned, affine = m.sem("p3_turned"), m.sem("p3_affine")
        gated = m.sem("p3_gated")
        out_mm = m.sem("p3_out_mm")
        x1_ready = m.sem("p3_x1_ready")
        x1_turned, x1t_cp = m.sem("p3_x1_turned"), m.sem("p3_x1t_cp")
        x1_out = [m.sem(f"p3_x1_out{b}") for b in range(PB)]
        x1t_out = [m.sem(f"p3_x1t_out{b}") for b in range(PB)]
        block = ctx.enter_context(nc.Block())
        NORM_STEPS = PB * (H + MOMENT_STEPS + H - 1)
        STEPS = NORM_STEPS + PB * 2 + MOMENT_STEPS

        @block.sync
        def _(sp):
            sp.dma_start(xT_sb[:], xT.rearrange("(k p) t -> p k t", p=P)).then_inc(gate_in, DMA)
            sp.dma_start(wg[:], wgT.rearrange("(k p) c -> p k c", p=P)).then_inc(gate_in, DMA)
            for b in range(PB):
                sp.dma_start(o[b][:], o_dram[b, :, :, 0:DH].rearrange("h t i -> t h i")).then_inc(o_in[b], DMA)
            sp.dma_start(lg[:], ln_g).then_inc(consts, DMA)
            sp.dma_start(lb[:], ln_b).then_inc(consts, DMA)
            sp.dma_start(wo[:], woT.rearrange("(h i) n -> i h n", i=DH)).then_inc(consts, DMA)
            for b in range(PB):
                sp.dma_start(xr[b][:], x[b]).then_inc(x_in[b], DMA)
            with sp.Fori(1, PAIRS) as p:
                row = sp.snap(p * PB)
                for b in range(PB):
                    sp.wait_ge(normed, (p - 1) * PB + b + 1)
                    sp.dma_start(o[b][:], o_dram[bass.ds(row + b, 1), :, :, 0:DH].rearrange("a h t i -> t (a h) i")).then_inc(o_in[b], DMA)
                for b in range(PB):
                    sp.wait_ge(x1_ready, p * PB)
                    sp.dma_start(xr[b][:], x[bass.ds(row + b, 1)].rearrange("a t n -> (a t) n")).then_inc(x_in[b], DMA)
            for b in range(PB):
                sp.wait_ge(x1_out[b], DMA * PAIRS)
                sp.wait_ge(x1t_out[b], DMA * PAIRS)

        @block.gpsimd
        def _(pool):
            nc.gpsimd.memset(ident[:], 0.0).then_inc(made, 1)
            nc.gpsimd.memset(neg_half[:], -0.5).then_inc(made, 1)
            pool.wait_ge(made, 2)
            nc.gpsimd.affine_select(out=ident[:], in_=ident[:], compare_op=ALU.not_equal, fill=1.0, base=0,
                                    pattern=[[-1, P]], channel_multiplier=1).then_inc(made, 1)
            def head_std(p):
                for b in range(PB):
                    pool.wait_ge(head_var, p * PB + b + 1)
                    nc.gpsimd.tensor_tensor(out=hr[b][:], in0=hr[b][:], in1=neg_half[:], op=ALU.pow).then_inc(head_rstd, 1)

            def apply_gates(p, j):
                for b in range(PB):
                    pool.wait_ge(gate_sig, p * (H // 2) + H // 2)
                    pool.wait_ge(affine, p * (PB * HEADS4) + (b + 1) * HEADS4)
                    nc.gpsimd.tensor_tensor(out=y[b][:], in0=y[b][:], in1=gate[j][:, :, b, :], op=ALU.mult).then_inc(gated, 1)

            def row_std(p):
                pool.wait_ge(row_var, p + 1)
                nc.gpsimd.tensor_tensor(out=rr[:], in0=rr[:], in1=neg_half[:, 0:PB], op=ALU.pow).then_inc(row_rstd, 1)

            head_std(0)
            apply_gates(0, 0)
            head_std(1)
            row_std(0)
            with pool.Fori(0, PAIRS // 2 - 1) as pp:
                for j in range(2):
                    p = pp * 2 + j + 1
                    apply_gates(p, (j + 1) % 2)
                    head_std(p + 1)
                    row_std(p)
            apply_gates(PAIRS - 1, (PAIRS - 1) % 2)
            row_std(PAIRS - 1)

        @block.tensor
        def _(pe):
            pe.wait_ge(gate_in, 2 * DMA)
            pe.wait_ge(made, 3)

            def gates(p):
                for g in range(H // 2):
                    if not isinstance(p, int) or p * (H // 2) + g >= 2:
                        pe.wait_ge(gate_sig, p * (H // 2) + g - 1)
                    for e in range(2):
                        for k in range(KT):
                            last = nc.tensor.matmul(ps_g[g % 2][:, e, :], wg[:, k, (2 * g + e) * DH:(2 * g + e + 1) * DH],
                                                    xT_sb[:, k, bass.ds(p * (PB * T), PB * T)],
                                                    start=(k == 0), stop=(k == KT - 1))
                    last.then_inc(gate_mm, 1)

            def heads(p):
                for b in range(PB):
                    pe.wait_ge(normed, p * PB + b + 1)
                    for q in range(HEADS4):
                        n = b * HEADS4 + q
                        pe.wait_ge(affine, p * (PB * HEADS4) + max(n - 1, 0))
                        for e in range(4):
                            last = nc.tensor.transpose(ps_t[n % 2][:, e, :], on[b][:, 4 * q + e, :], ident[:])
                        last.then_inc(turned, 1)

            def project(p):
                for b in range(PB):
                    pe.wait_ge(gated, p * PB + b + 1)
                    for h in range(H):
                        last = nc.tensor.matmul(ps_o[b][:, 0:D], y[b][:, h, :], wo[:, h, :], start=(h == 0), stop=(h == H - 1))
                    last.then_inc(out_mm, 1)

            def turn_x1(p):
                pe.wait_ge(x1t_cp, p * PB)
                for b in range(PB):
                    pe.wait_ge(x1_ready, p * PB + b + 1)
                    for k in range(KT):
                        last = nc.tensor.transpose(ps_x[b][:, k, :], x1[b][:, k * P:(k + 1) * P], ident[:])
                    last.then_inc(x1_turned, 1)

            gates(0)
            heads(0)
            gates(1)
            pe.wait_ge(consts, 3 * DMA)
            project(0)
            with pe.Fori(1, PAIRS - 1) as p:
                heads(p)
                turn_x1(p - 1)
                gates(p + 1)
                project(p)
            heads(PAIRS - 1)
            turn_x1(PAIRS - 2)
            project(PAIRS - 1)
            turn_x1(PAIRS - 1)

        @block.scalar
        def _(act):

            def gates(p, j):
                for g in range(H // 2):
                    act.wait_ge(gate_mm, p * (H // 2) + g + 1)
                    if g == 0 and not (isinstance(p, int) and p < 2):
                        act.wait_ge(gated, p * PB - PB)
                    nc.scalar.activation(gate[j][:, 2 * g:2 * g + 2, :, :].rearrange("c e b t -> c e (b t)"), ps_g[g % 2][:],
                                         ACT.Sigmoid).then_inc(gate_sig, 1)

            def affine_heads(p):
                for b in range(PB):
                    if b == 0 and not (isinstance(p, int) and p == 0):
                        act.wait_ge(out_mm, p * PB)
                    for q in range(HEADS4):
                        n = b * HEADS4 + q
                        act.wait_ge(turned, p * (PB * HEADS4) + n + 1)
                        nc.scalar.activation(y[b][:, 4 * q:4 * q + 4, :], ps_t[n % 2][:], ACT.Identity,
                                             bias=lb[:, 0:1], scale=lg[:, 0:1]).then_inc(affine, 1)

            def store(p):
                row = p * PB if isinstance(p, int) else act.snap(p * PB)
                for b in range(PB):
                    act.wait_ge(x1_ready, p * PB + b + 1)
                    act.dma_start(x1_dram[bass.ds(row + b, 1)].rearrange("a t n -> (a t) n"), x1[b][:]).then_inc(x1_out[b], DMA)
                    if not (isinstance(p, int) and p == 0):
                        act.wait_ge(x1t_out[b], p * DMA)
                    act.wait_ge(x1_turned, p * PB + b + 1)
                    nc.scalar.copy(x1t[b][:], ps_x[b][:, 0:KT, :]).then_inc(x1t_cp, 1)
                    act.wait_ge(x1t_cp, p * PB + b + 1)
                    act.dma_start(x1T_dram[:, bass.ds(row * T + b * T, T)].rearrange("(k q) t -> q k t", q=P),
                                  x1t[b][:]).then_inc(x1t_out[b], DMA)

            gates(0, 0)
            act.wait_ge(consts, 3 * DMA)
            affine_heads(0)
            gates(1, 1)
            with act.Fori(0, PAIRS // 2 - 1) as pp:
                for j in range(2):
                    p = pp * 2 + j + 1
                    affine_heads(p)
                    store(p - 1)
                    gates(p + 1, j)
            affine_heads(PAIRS - 1)
            store(PAIRS - 2)
            store(PAIRS - 1)

        @block.vector
        def _(dve):
            def normalize(p, st):
                for b in range(PB):
                    dve.wait_ge(o_in[b], p * DMA + DMA)
                    for h in range(H):
                        last = st.done(nc.vector.bn_stats(out=stats[b][:, h, :], in_=o[b][:, h, :]))
                    st.after(last)
                    moments(nc, st, stats[b][:], hm[b][:], hr[b][:], ht[b][:], DH)
                    dve.sem_inc(head_var, 1)
                for b in range(PB):
                    dve.wait_ge(head_rstd, p * PB + b + 1)
                    if not isinstance(p, int):
                        dve.wait_ge(turned, p * (PB * HEADS4))
                    for h in range(H):
                        ins = nc.vector.tensor_scalar(on[b][:, h, :], o[b][:, h, :], hm[b][:, h:h + 1], hr[b][:, h:h + 1],
                                                      ALU.subtract, ALU.mult)
                        if h < H - 1:
                            last = st.done(ins)
                    st.after(last)
                    ins.then_inc(normed, 1)

            def residual(p, st):
                for b in range(PB):
                    dve.wait_ge(x_in[b], p * DMA + DMA)
                    dve.wait_ge(out_mm, p * PB + b + 1)
                    last = st.done(nc.vector.tensor_tensor(out=res[b][:], in0=ps_o[b][:, 0:D], in1=xr[b][:], op=ALU.add))
                for b in range(PB):
                    st.after(last - PB + 1 + b)
                    done = st.done(nc.vector.bn_stats(out=rstats[:, b, :], in_=res[b][:]))
                st.after(done)
                moments(nc, st, rstats[:], rm[:], rr[:], rt[:], D)
                dve.sem_inc(row_var, 1)
                dve.wait_ge(row_rstd, p + 1)
                for b in range(PB):
                    if b == 0 and not (isinstance(p, int) and p == 0):
                        dve.wait_ge(x1_turned, p * PB)
                    if not (isinstance(p, int) and p == 0):
                        dve.wait_ge(x1_out[b], p * DMA)
                    nc.vector.tensor_scalar(x1[b][:], res[b][:], rm[:, b:b + 1], rr[:, b:b + 1], ALU.subtract,
                                            ALU.mult).then_inc(x1_ready, 1)

            normalize(0, Steps(dve, steps, 0))
            st = Steps(dve, steps, NORM_STEPS)
            dve.wait_ge(turned, PB * HEADS4)
            normalize(1, st)
            residual(0, st)
            assert st.n == STEPS, (st.n, STEPS)
            with dve.Fori(1, PAIRS - 1) as p:
                st = Steps(dve, steps, p * STEPS + NORM_STEPS)
                normalize(p + 1, st)
                residual(p, st)
            residual(PAIRS - 1, Steps(dve, steps, (PAIRS - 1) * STEPS + NORM_STEPS))


def long_conv(nc, ctxR, kpad, dcol, x1_dram, x1T_dram, kz_dram, x2_dram, x2T_dram):
    HPAIR = HK // 2
    PAIRC = HD2 * HD2
    with ExitStack() as ctx:
        m = Pool(nc, ctx)
        c_sb = m.sb("p4_c", [P, KT, B, P])
        x1t = m.sb("p4_x1t", [P, KT, B, P])
        xa = m.sb("p4_xa", [P, KT, B, P])
        kz = m.sb("p4_kz", [HK, 3 * P])
        dk = m.sb("p4_dk", [HK, 1])
        toep = [m.sb(f"p4_toep{i}", [P, 2 * P]) for i in range(2)]
        prod = [m.sb(f"p4_prod{i}", [P, KT, B, PAIRC]) for i in range(2)]
        wy = [m.sb(f"p4_wy{i}", [P, B, PAIRC]) for i in range(2)]
        ident = m.sb("p4_ident", [P, P])
        neg_half = m.sb("p4_neg_half", [P, 2])
        x1 = [m.sb(f"p4_x1{b}", [T, D]) for b in range(2)]
        res = [m.sb(f"p4_res{b}", [T, D]) for b in range(2)]
        x2 = [m.sb(f"p4_x2{b}", [T, D]) for b in range(2)]
        x2t = [m.sb(f"p4_x2t{b}", [P, KT, T]) for b in range(2)]
        rstats = m.sb("p4_rstats", [T, 2, 6])
        rm, rr, rt = (m.sb(f"p4_r{n}", [T, 2]) for n in "mrt")
        ps_y = [m.ps(f"p4_ps_y{i}", [P, 2, 8 * PAIRC]) for i in range(4)]

        ctx_in, x1t_in = m.sem("p4_ctx_in"), m.sem("p4_x1t_in")
        k_in, kz_add, kz_out = m.sem("p4_k_in"), m.sem("p4_kz_add"), m.sem("p4_kz_out")
        made = m.sem("p4_made")
        toep_in = [m.sem(f"p4_toep_in{i}") for i in range(2)]
        head_free = m.sem("p4_head_free")
        bank_free = m.sem("p4_bank_free")
        prod_done, conv_done = m.sem("p4_prod_done"), m.sem("p4_conv_done")
        weighted, summed = m.sem("p4_weighted"), m.sem("p4_summed")
        x1_in = [m.sem(f"p4_x1_in{b}") for b in range(2)]
        xa_turned, x2_ready, x2_turned, x2t_cp = (m.sem(f"p4_{n}") for n in ("xa_turned", "x2_ready", "x2_turned", "x2t_cp"))
        steps = m.sem("p4_steps")
        res_ready = m.sem("p4_res_ready")
        row_var, row_rstd = m.sem("p4_row_var"), m.sem("p4_row_rstd")
        x2_out = [m.sem(f"p4_x2_out{b}") for b in range(2)]
        x2t_out = [m.sem(f"p4_x2t_out{b}") for b in range(2)]
        block = ctx.enter_context(nc.Block())
        ROW_STEPS = 2 + MOMENT_STEPS

        @block.sync
        def _(sp):
            sp.dma_start(kz[:], kpad).then_inc(k_in, DMA)
            sp.dma_start(dk[:], dcol).then_inc(k_in, DMA)
            sp.dma_start(c_sb[:], ctxR).then_inc(ctx_in, DMA)
            sp.dma_start(x1t[:].rearrange("p k b t -> p k (b t)"), x1T_dram.rearrange("(k p) t -> p k t", p=P)).then_inc(x1t_in, DMA)
            sp.wait_ge(kz_add, 1)
            sp.dma_start(kz_dram, kz[:]).then_inc(kz_out, DMA)
            sp.wait_ge(kz_out, DMA)
            with sp.Fori(0, HPAIR) as hp:
                for j in range(2):
                    sp.wait_ge(head_free, hp * 2 + j + 1)
                    sp.dma_start(toep[j][:], bass.AP(kz_dram.tensor, kz_dram.offset + (hp * 2 + j) * (3 * P),
                                                     [[1, P], [1, 2 * P]])).then_inc(toep_in[j], DMA)
            with sp.Fori(0, B // 2) as p:
                row = sp.snap(p * 2)
                for b in range(2):
                    sp.wait_ge(res_ready, p * 2)
                    sp.dma_start(x1[b][:], x1_dram[bass.ds(row + b, 1)].rearrange("a t n -> (a t) n")).then_inc(x1_in[b], DMA)
            for b in range(2):
                sp.wait_ge(x2_out[b], DMA * B // 2)
                sp.wait_ge(x2t_out[b], DMA * B // 2)

        @block.gpsimd
        def _(pool):
            nc.gpsimd.memset(ident[:], 0.0).then_inc(made, 1)
            nc.gpsimd.memset(neg_half[:], -0.5).then_inc(made, 1)
            pool.wait_ge(made, 2)
            nc.gpsimd.affine_select(out=ident[:], in_=ident[:], compare_op=ALU.not_equal, fill=1.0, base=0,
                                    pattern=[[-1, P]], channel_multiplier=1).then_inc(made, 1)
            pool.wait_ge(ctx_in, DMA)
            with pool.Fori(0, HPAIR) as hp:
                for j in range(2):
                    pool.wait_ge(head_free, hp * 2 + j + 1)
                    c0 = (hp * 2 + j) * HD2
                    for k in range(KT):
                        ck = c_sb[:, k, :, bass.ds(c0, HD2)]
                        nc.gpsimd.tensor_tensor(
                            out=prod[j][:, k].rearrange("p b (i j) -> p b i j", i=HD2),
                            in0=ck.unsqueeze(3).broadcast_to([P, B, HD2, HD2]),
                            in1=ck.unsqueeze(2).broadcast_to([P, B, HD2, HD2]), op=ALU.mult).then_inc(prod_done, 1)
            with pool.Fori(0, B // 2) as p:
                pool.wait_ge(row_var, p + 1)
                nc.gpsimd.tensor_tensor(out=rr[:], in0=rr[:], in1=neg_half[:], op=ALU.pow).then_inc(row_rstd, 1)

        @block.tensor
        def _(pe):
            pe.sem_inc(head_free, 2)
            with pe.Fori(0, HPAIR) as hp:
                for j in range(2):
                    pe.wait_ge(toep_in[j], hp * DMA + DMA)
                    pe.wait_ge(prod_done, hp * (2 * KT) + (j + 1) * KT)
                    for c in range(KT):
                        for half in range(2):
                            n = j * 2 + c
                            if half == 0:
                                pe.wait_ge(bank_free, hp * 4 + n + 1)
                            for a in range(c + 1):
                                last = nc.tensor.matmul(ps_y[n][:, half, :], toep[j][:, (c - a) * P:(c - a + 1) * P],
                                                        prod[j][:, a, half * 8:(half + 1) * 8, :].rearrange("p b q -> p (b q)"),
                                                        start=(a == 0), stop=(a == c))
                        if c == 0:
                            last.then_inc(conv_done, 1)
                    last.then_inc(conv_done, 1)
                    pe.wait_ge(conv_done, hp * 4 + j * 2 + 2)
                    pe.sem_inc(head_free, 1)
            pe.wait_ge(summed, HK * KT)
            pe.wait_ge(made, 3)
            for row in range(B):
                b = row % 2
                pe.wait_ge(res_ready, max(row - 1, 0))
                for k in range(KT):
                    last = nc.tensor.transpose(ps_y[b][:, 0, k * P:(k + 1) * P], xa[:, k, row, :], ident[:])
                last.then_inc(xa_turned, 1)
                if b == 1:
                    for e in range(2):
                        pe.wait_ge(x2_ready, row + e)
                        pe.wait_ge(x2t_cp, max(row + e - 2, 0))
                        for k in range(KT):
                            last = nc.tensor.transpose(ps_y[2 + e][:, 0, k * P:(k + 1) * P], x2[e][:, k * P:(k + 1) * P], ident[:])
                        last.then_inc(x2_turned, 1)

        @block.vector
        def _(dve):
            dve.wait_ge(k_in, 2 * DMA)
            nc.vector.tensor_tensor(out=kz[:, P - 1:P], in0=kz[:, P - 1:P], in1=dk[:], op=ALU.add).then_inc(kz_add, 1)
            dve.sem_inc(bank_free, 4)
            dve.wait_ge(x1t_in, DMA)
            with dve.Fori(0, HPAIR) as hp:
                for j in range(2):
                    for c in range(KT):
                        n = j * 2 + c
                        stream = x1t[:, c, :, bass.ds((hp * 2 + j) * HD2, HD2)]
                        dve.wait_ge(conv_done, hp * 4 + n + 1)
                        dve.wait_ge(summed, hp * 4 + max(n - 1, 0))
                        nc.vector.tensor_tensor(
                            out=wy[c][:].rearrange("p b (j i) -> p b j i", j=HD2),
                            in0=ps_y[n][:].rearrange("p a (b j i) -> p (a b) j i", j=HD2, i=HD2),
                            in1=stream.unsqueeze(2).broadcast_to([P, B, HD2, HD2]), op=ALU.mult).then_inc(bank_free, 1)
                        dve.wait_ge(bank_free, hp * 4 + n + 5)
                        nc.vector.tensor_reduce(out=xa[:, c, :, bass.ds((hp * 2 + j) * HD2, HD2)],
                                                in_=wy[c][:].rearrange("p b (j i) -> p b j i", j=HD2),
                                                axis=AXIS_X, op=ALU.add).then_inc(summed, 1)
            with dve.Fori(0, B // 2) as p:
                st = Steps(dve, steps, p * ROW_STEPS)
                for b in range(2):
                    dve.wait_ge(x1_in[b], p * DMA + DMA)
                    dve.wait_ge(xa_turned, p * 2 + b + 1)
                    nc.vector.tensor_tensor(out=res[b][:], in0=ps_y[b][:, 0, 0:D], in1=x1[b][:], op=ALU.add).then_inc(res_ready, 1)
                for b in range(2):
                    dve.wait_ge(res_ready, p * 2 + b + 1)
                    done = st.done(nc.vector.bn_stats(out=rstats[:, b, :], in_=res[b][:]))
                st.after(done)
                moments(nc, st, rstats[:], rm[:], rr[:], rt[:], D)
                dve.sem_inc(row_var, 1)
                dve.wait_ge(row_rstd, p + 1)
                for b in range(2):
                    dve.wait_ge(x2_out[b], p * DMA)
                    dve.wait_ge(x2_turned, p * 2)
                    nc.vector.tensor_scalar(x2[b][:], res[b][:], rm[:, b:b + 1], rr[:, b:b + 1], ALU.subtract,
                                            ALU.mult).then_inc(x2_ready, 1)
                assert st.n == ROW_STEPS

        @block.scalar
        def _(act):
            with act.Fori(0, B // 2) as p:
                row = act.snap(p * 2)
                for b in range(2):
                    act.wait_ge(x2_ready, p * 2 + b + 1)
                    act.dma_start(x2_dram[bass.ds(row + b, 1)].rearrange("a t n -> (a t) n"), x2[b][:]).then_inc(x2_out[b], DMA)
                for b in range(2):
                    act.wait_ge(x2t_out[b], p * DMA)
                    act.wait_ge(x2_turned, p * 2 + b + 1)
                    nc.scalar.copy(x2t[b][:].rearrange("p k t -> p (k t)"), ps_y[2 + b][:, 0, 0:D]).then_inc(x2t_cp, 1)
                    act.wait_ge(x2t_cp, p * 2 + b + 1)
                    act.dma_start(x2T_dram[:, bass.ds(row * T + b * T, T)].rearrange("(k q) t -> q k t", q=P),
                                  x2t[b][:]).then_inc(x2t_out[b], DMA)


def experts(nc, x2_dram, x2T_dram, gwT, sguT, sdT, wguT, wdT, buf_dram, eo_dram, out):
    NT = TOK // P
    MH = M // 2
    SM = MS // MH
    KEPT = 16384.0
    NE = NT * E
    with ExitStack() as outer:
        m = Pool(nc, outer)
        acc = m.sb("p5_acc", [P, NT, D])
        wk = m.sb("p5_wk", [P, TOPK, NT])
        slot_i = m.sb("p5_slot_i", [P, TOPK, NT], INT32)
        target_i = m.sb("p5_target_i", [P, TOPK, NT], INT32)
        shared = m.sb("p5_shared", [P, NT, D])

        with ExitStack() as ctx:
            m = Pool(nc, ctx)
            xT = m.sb("p5_xT", [P, KT, TOK])
            gw = m.sb("p5_gw", [P, KT, E])
            sgu = m.sb("p5_sgu", [P, KT, 2, MS])
            sd = m.sb("p5_sd", [MH, SM, D])
            zeros = m.sb("p5_zeros", [P, 8 * D])
            ones, tri = m.sb("p5_ones", [P, P]), m.sb("p5_tri", [P, P])
            reset = m.sb("p5_reset", [P, NT, E])
            below = m.sb("p5_below", [P, GROUPS, GROUPS])
            slot0_i = m.sb("p5_slot0_i", [P, E], INT32)
            slot0 = m.sb("p5_slot0", [P, E])
            score, a1, a2, a3, sel, rank, val = (m.sb(f"p5_{n}", [P, NT, E]) for n in
                                                 ("score", "a1", "a2", "a3", "sel", "rank", "val"))
            pre = m.sb("p5_pre", [P, NT + 1, E])
            top8 = m.sb("p5_top8", [P, NT, 8])
            gs, gr = m.sb("p5_gs", [P, NT, GROUPS]), m.sb("p5_gr", [P, NT, GROUPS])
            t1, t2 = m.sb("p5_t1", [P, NT]), m.sb("p5_t2", [P, NT])
            cnt = m.sb("p5_cnt", [P, E])
            vk, v2 = m.sb("p5_vk", [P, TOPK, NT]), m.sb("p5_v2", [P, TOPK, NT])
            sg = [m.sb(f"p5_sg{i}", [MH, 512]) for i in range(2)]
            gx = [m.sb(f"p5_gx{i}", [MH, 512]) for i in range(2)]
            ux = [m.sb(f"p5_ux{i}", [MH, 512]) for i in range(2)]
            hs = m.sb("p5_hs", [MH, SM, 512])
            ps_r = m.ps("p5_ps_r", [P, NT, E])
            ps_g = [m.ps(f"p5_ps_g{i}", [MH, 512]) for i in range(2)]
            ps_u = [m.ps(f"p5_ps_u{i}", [MH, 512]) for i in range(2)]
            ps_d = m.ps("p5_ps_d", [P, 2, D])
            ps_c = m.ps("p5_ps_c", [P, E])

            r_in, s_in, x_in = m.sem("p5_r_in"), m.sem("p5_s_in"), m.sem("p5_x_in")
            zero_made, zeroed = m.sem("p5_zero_made"), m.sem("p5_zeroed")
            made = m.sem("p5_made")
            logits, steps = m.sem("p5_logits"), m.sem("p5_steps")
            shifted, exped = m.sem("p5_shifted"), m.sem("p5_exped")
            chosen, ranked = m.sem("p5_chosen"), m.sem("p5_ranked")
            slots_ready = m.sem("p5_slots_ready")
            QP = 1
            up_mm, sig_done, gx_done, ux_done = (m.sem(f"p5_{n}") for n in ("up_mm", "sig_done", "gx_done", "ux_done"))
            silu_done, h_done, down_mm, down_cp = (m.sem(f"p5_{n}") for n in ("silu_done", "h_done", "down_mm", "down_cp"))
            sent = m.sem("p5_sent")
            block = ctx.enter_context(nc.Block())

            @block.sync
            def _(sp):
                sp.dma_start(gw[:], gwT.rearrange("(k p) e -> p k e", p=P)).then_inc(r_in, DMA)
                sp.dma_start(xT[:], x2T_dram.rearrange("(k p) t -> p k t", p=P)).then_inc(r_in, DMA)
                sp.dma_start(sgu[:], sguT).then_inc(s_in, DMA)
                sp.dma_start(sd[:], sdT).then_inc(s_in, DMA)
                sp.dma_start(acc[:], x2_dram.rearrange("b t n -> t b n")).then_inc(x_in, DMA)
                sp.wait_ge(zero_made, 1)
                sp.dma_start(buf_dram.rearrange("(a p r) n -> p a (r n)", p=P, r=8),
                             zeros[:].unsqueeze(1).broadcast_to([P, SLOTS // (8 * P), 8 * D])).then_inc(zeroed, DMA)
                sp.wait_ge(zeroed, DMA)

            @block.gpsimd
            def _(pool):
                nc.gpsimd.memset(ones[:], 1.0).then_inc(made, 1)
                nc.gpsimd.memset(reset[:], 1.0).then_inc(made, 1)
                nc.gpsimd.memset(below[:], 1.0).then_inc(made, 1)
                nc.gpsimd.iota(slot0_i[:], pattern=[[CAP, E]], base=-1, channel_multiplier=0).then_inc(made, 1)
                pool.wait_ge(made, 4)
                nc.gpsimd.affine_select(out=tri[:], in_=ones[:], compare_op=ALU.is_ge, fill=0.0, base=0,
                                        pattern=[[1, P]], channel_multiplier=-1).then_inc(made, 1)
                nc.gpsimd.affine_select(out=reset[:], in_=reset[:], compare_op=ALU.not_equal, fill=0.0, base=0,
                                        pattern=[[0, NT], [1, E]], channel_multiplier=0).then_inc(made, 1)
                nc.gpsimd.affine_select(out=below[:], in_=below[:], compare_op=ALU.is_gt, fill=0.0, base=0,
                                        pattern=[[1, GROUPS], [-1, GROUPS]], channel_multiplier=0).then_inc(made, 1)
                with pool.Fori(0, QP) as q:
                    for s in range(SM):
                        i = s % 2
                        pool.wait_ge(sig_done, q * SM + s + 1)
                        pool.wait_ge(gx_done, q * SM + s + 1)
                        nc.gpsimd.tensor_tensor(out=gx[i][:], in0=gx[i][:], in1=sg[i][:], op=ALU.mult).then_inc(silu_done, 1)
                        pool.wait_ge(silu_done, q * SM + s + 1)
                        pool.wait_ge(ux_done, q * SM + s + 1)
                        pool.wait_ge(down_mm, q * 4)
                        nc.gpsimd.tensor_tensor(out=hs[:, s, :], in0=gx[i][:], in1=ux[i][:], op=ALU.mult).then_inc(h_done, 1)
                pool.wait_ge(slots_ready, 1)
                pool.wait_ge(x_in, DMA)
                pool.wait_ge(zeroed, DMA)
                for i in range(NT):
                    for k in range(TOPK):
                        nc.gpsimd.indirect_dma_start(
                            out=buf_dram, out_offset=bass.IndirectOffsetOnAxis(ap=target_i[:, k, i:i + 1], axis=0),
                            in_=acc[:, i, :], in_offset=None, bounds_check=SLOTS - 1, oob_is_err=False).then_inc(sent, DMA)
                pool.wait_ge(sent, DMA * NT * TOPK)

            @block.tensor
            def _(pe):
                pe.wait_ge(r_in, 2 * DMA)
                for i in range(NT):
                    for k in range(KT):
                        last = nc.tensor.matmul(ps_r[:, i, :], xT[:, k, i * P:(i + 1) * P], gw[:, k, :],
                                                start=(k == 0), stop=(k == KT - 1))
                last.then_inc(logits, 1)
                pe.wait_ge(s_in, 2 * DMA)
                def shared_net(q):
                    for s in range(SM):
                        i = s % 2
                        pe.wait_ge(gx_done, q * SM + max(s - 1, 0))
                        pe.wait_ge(ux_done, q * SM + max(s - 1, 0))
                        for half, ps in ((0, ps_g), (1, ps_u)):
                            for k in range(KT):
                                last = nc.tensor.matmul(ps[i][:], sgu[:, k, half, s * MH:(s + 1) * MH],
                                                        xT[:, k, bass.ds(q * 512, 512)], start=(k == 0), stop=(k == KT - 1))
                        last.then_inc(up_mm, 1)
                    pe.wait_ge(h_done, q * SM + SM)
                    for t in range(4):
                        pe.wait_ge(down_cp, q * 4 + t)
                        for s in range(SM):
                            last = nc.tensor.matmul(ps_d[:, t % 2, :], hs[:, s, t * P:(t + 1) * P], sd[:, s, :],
                                                    start=(s == 0), stop=(s == SM - 1))
                        last.then_inc(down_mm, 1)

                with pe.Fori(0, QP) as q:
                    shared_net(q)
                pe.wait_ge(chosen, 1)
                pe.wait_ge(made, 7)
                for i in range(NT):
                    nc.tensor.matmul(ps_r[:, i, :], tri[:], sel[:, i, :], start=True, stop=False)
                    nc.tensor.matmul(ps_r[:, i, :], ones[:], pre[:, i, :], start=False, stop=True)
                nc.tensor.matmul(ps_c[:], ones[:], pre[:, NT, :], start=True, stop=True).then_inc(ranked, 1)
                with pe.Fori(QP, 4) as q:
                    shared_net(q)

            @block.scalar
            def _(act):
                act.wait_ge(shifted, 1)
                nc.scalar.activation(score[:], a1[:], ACT.Exp).then_inc(exped, 1)
                with act.Fori(0, 4) as q:
                    for s in range(SM):
                        i = s % 2
                        act.wait_ge(up_mm, q * SM + s + 1)
                        act.wait_ge(h_done, q * SM + max(s - 1, 0))
                        nc.scalar.activation(sg[i][:], ps_g[i][:], ACT.Sigmoid).then_inc(sig_done, 1)
                        nc.scalar.copy(gx[i][:], ps_g[i][:]).then_inc(gx_done, 1)
                        nc.scalar.copy(ux[i][:], ps_u[i][:]).then_inc(ux_done, 1)
                    for t in range(4):
                        act.wait_ge(down_mm, q * 4 + t + 1)
                        nc.scalar.copy(shared[:, bass.ds(q * 4 + t, 1), :].rearrange("p a n -> p (a n)"),
                                       ps_d[:, t % 2, :]).then_inc(down_cp, 1)

            @block.vector
            def _(dve):
                st = Steps(dve, steps, 0)
                tt, ts, stt = nc.vector.tensor_tensor, nc.vector.tensor_scalar, nc.vector.scalar_tensor_tensor

                def then(ins):
                    st.after(st.done(ins))

                def by_tile(ap):
                    return ap.unsqueeze(2).broadcast_to([P, NT, E])

                nc.vector.memset(zeros[:], 0.0).then_inc(zero_made, 1)
                then(nc.vector.memset(pre[:, 0, :], 0.0))
                dve.wait_ge(made, 7)
                then(nc.vector.tensor_copy(slot0[:], slot0_i[:]))
                dve.wait_ge(logits, 1)
                then(nc.vector.tensor_reduce(out=t1[:], in_=ps_r[:], axis=AXIS_X, op=ALU.max))
                tt(out=a1[:], in0=ps_r[:], in1=by_tile(t1[:]), op=ALU.subtract).then_inc(shifted, 1)
                dve.wait_ge(exped, 1)
                then(nc.vector.tensor_reduce(out=t1[:], in_=score[:], axis=AXIS_X, op=ALU.add))
                then(nc.vector.reciprocal(t2[:], t1[:]))
                then(tt(out=score[:], in0=score[:], in1=by_tile(t2[:]), op=ALU.mult))
                then(nc.vector.tensor_reduce(out=gs[:].rearrange("p t g -> p (t g)"),
                                             in_=score[:].rearrange("p t (g e) -> p (t g) e", g=GROUPS), axis=AXIS_X, op=ALU.max))
                pair = [P, NT, GROUPS, GROUPS]
                other, own = gs[:].unsqueeze(2).broadcast_to(pair), gs[:].unsqueeze(3).broadcast_to(pair)
                a1v, a2v = (a[:].rearrange("p t (g h) -> p t g h", g=GROUPS) for a in (a1, a2))
                st.done(tt(out=a1v, in0=other, in1=own, op=ALU.is_gt))
                then(tt(out=a2v, in0=other, in1=own, op=ALU.is_equal))
                then(tt(out=a2v, in0=a2v, in1=below[:].unsqueeze(1).broadcast_to(pair), op=ALU.mult))
                then(tt(out=a1[:], in0=a1[:], in1=a2[:], op=ALU.add))
                then(nc.vector.tensor_reduce(out=gr[:].rearrange("p t g -> p (t g)"),
                                             in_=a1[:].rearrange("p t (g h) -> p (t g) h", g=GROUPS), axis=AXIS_X, op=ALU.add))
                then(ts(gr[:], gr[:], float(TOPG), None, ALU.is_lt))
                then(tt(out=a1[:].rearrange("p t (g e) -> p (t g) e", g=GROUPS), in0=score[:].rearrange("p t (g e) -> p (t g) e", g=GROUPS),
                        in1=gr[:].rearrange("p t (g o) -> p (t g) o", o=1).broadcast_to([P, NT * GROUPS, E // GROUPS]), op=ALU.mult))
                for i in range(NT):
                    last = st.done(nc.vector.max(top8[:, i, :], a1[:, i, :]))
                st.after(last)
                kth = by_tile(top8[:, :, TOPK - 1])
                st.done(tt(out=a2[:], in0=a1[:], in1=kth, op=ALU.is_gt))
                then(tt(out=a3[:], in0=a1[:], in1=kth, op=ALU.is_equal))
                then(nc.vector.tensor_reduce(out=t1[:], in_=a2[:], axis=AXIS_X, op=ALU.add))
                flat = [a[:].rearrange("p t e -> p (t e)") for a in (reset, a3, rank, sel)]
                then(nc.vector.tensor_tensor_scan(flat[2], flat[0], flat[1], 0.0, ALU.mult, ALU.add))
                then(ts(t2[:], t1[:], -1.0, float(TOPK), ALU.mult, ALU.add))
                then(tt(out=rank[:], in0=rank[:], in1=by_tile(t2[:]), op=ALU.is_le))
                then(tt(out=a3[:], in0=a3[:], in1=rank[:], op=ALU.mult))
                then(tt(out=sel[:], in0=a3[:], in1=a2[:], op=ALU.add))
                for i in range(NT):
                    then(tt(out=pre[:, i + 1, :], in0=pre[:, i, :], in1=sel[:, i, :], op=ALU.add))
                dve.sem_inc(chosen, 1)
                then(nc.vector.tensor_tensor_scan(flat[2], flat[0], flat[3], 0.0, ALU.mult, ALU.add))
                dve.wait_ge(ranked, 1)
                then(nc.vector.tensor_copy(cnt[:], ps_c[:]))
                st.done(ts(a1[:], ps_r[:], float(CAP - 1), None, ALU.is_le))
                st.done(tt(out=a2[:], in0=ps_r[:], in1=cnt[:].unsqueeze(1).broadcast_to([P, NT, E]), op=ALU.is_equal))
                then(stt(out=val[:], in0=ps_r[:], scalar=float(CAP), in1=slot0[:].unsqueeze(1).broadcast_to([P, NT, E]),
                         op0=ALU.min, op1=ALU.add))
                then(tt(out=a1[:], in0=a1[:], in1=a2[:], op=ALU.max))
                then(stt(out=val[:], in0=a1[:], scalar=KEPT, in1=val[:], op0=ALU.mult, op1=ALU.add))
                for k in range(TOPK):
                    then(stt(out=a1[:], in0=rank[:], scalar=float(k + 1), in1=sel[:], op0=ALU.is_equal, op1=ALU.mult))
                    then(tt(out=a2[:], in0=a1[:], in1=val[:], op=ALU.mult))
                    then(nc.vector.tensor_reduce(out=vk[:, k, :], in_=a2[:], axis=AXIS_X, op=ALU.add))
                then(ts(v2[:], vk[:], KEPT, KEPT, ALU.is_ge, ALU.mult))
                then(tt(out=vk[:], in0=vk[:], in1=v2[:], op=ALU.subtract))
                st.done(nc.vector.tensor_copy(slot_i[:], vk[:]))
                then(stt(out=v2[:], in0=v2[:], scalar=-1.0, in1=vk[:], op0=ALU.mult, op1=ALU.add))
                then(ts(v2[:], v2[:], KEPT, None, ALU.add))
                nc.vector.tensor_copy(target_i[:], v2[:]).then_inc(slots_ready, 1)
                for k in range(TOPK):
                    then(stt(out=a1[:], in0=rank[:], scalar=float(k + 1), in1=sel[:], op0=ALU.is_equal, op1=ALU.mult))
                    then(tt(out=a3[:], in0=a1[:], in1=score[:], op=ALU.mult))
                    then(nc.vector.tensor_reduce(out=wk[:, k, :], in_=a3[:], axis=AXIS_X, op=ALU.add))
                with dve.Fori(QP, 4) as q:
                    for s in range(SM):
                        i = s % 2
                        dve.wait_ge(sig_done, q * SM + s + 1)
                        dve.wait_ge(gx_done, q * SM + s + 1)
                        tt(out=gx[i][:], in0=gx[i][:], in1=sg[i][:], op=ALU.mult).then_inc(silu_done, 1)
                        dve.wait_ge(silu_done, q * SM + s + 1)
                        dve.wait_ge(ux_done, q * SM + s + 1)
                        dve.wait_ge(down_mm, q * 4)
                        tt(out=hs[:, s, :], in0=gx[i][:], in1=ux[i][:], op=ALU.mult).then_inc(h_done, 1)

        with ExitStack() as ctx:
            m = Pool(nc, ctx)
            NB = 4
            ident = m.sb("p5_ident", [P, P])
            wgu = [m.sb(f"p5_wgu{i}", [P, KT, 2, M]) for i in range(NB)]
            wd = [m.sb(f"p5_wd{i}", [MH, 2, D]) for i in range(NB)]
            xe = [m.sb(f"p5_xe{i}", [CAP, D]) for i in range(NB)]
            xt = [m.sb(f"p5_xt{i}", [P, KT, CAP]) for i in range(NB)]
            sg = [m.sb(f"p5_esg{i}", [MH, 2, CAP]) for i in range(NB)]
            hh = [m.sb(f"p5_eh{i}", [MH, 2, CAP]) for i in range(NB)]
            yo = [m.sb(f"p5_yo{i}", [CAP, D]) for i in range(NB)]
            ps_x = [m.ps(f"p5_ps_x{i}", [P, 2, D]) for i in range(2)]
            ps_e = [m.ps(f"p5_ps_e{i}", [MH, 2, D]) for i in range(4)]
            ps_y = [m.ps(f"p5_ps_y{i}", [P, 2, D]) for i in range(2)]

            made = m.sem("p5_made2")
            w_in = [m.sem(f"p5_w_in{i}") for i in range(NB)]
            x_in = [m.sem(f"p5_xe_in{i}") for i in range(NB)]
            x_turned, xt_cp, up_mm, sig_done, silu_done, h_done, down_mm, y_cp = (
                m.sem(f"p5_e_{n}") for n in ("x_turned", "xt_cp", "up_mm", "sig_done", "silu_done", "h_done", "down_mm", "y_cp"))
            y_out = [m.sem(f"p5_y_out{i}") for i in range(NB)]
            block = ctx.enter_context(nc.Block())

            @block.sync
            def _(sp):
                for i in range(NB):
                    sp.dma_start(wgu[i][:].rearrange("p k h m -> p (k h m)"), wguT[i]).then_inc(w_in[i], DMA)
                    sp.dma_start(wd[i][:].rearrange("p h n -> p (h n)"), wdT[i]).then_inc(w_in[i], DMA)
                with sp.Fori(1, E // NB) as q:
                    e0 = sp.snap(q * NB)
                    for i in range(NB):
                        sp.wait_ge(down_mm, (q - 1) * NB + i + 1)
                        sp.dma_start(wgu[i][:].rearrange("p k h m -> p (k h m)"), wguT[bass.ds(e0 + i, 1)]
                                     .rearrange("a p x -> (a p) x")).then_inc(w_in[i], DMA)
                        sp.dma_start(wd[i][:].rearrange("p h n -> p (h n)"), wdT[bass.ds(e0 + i, 1)]
                                     .rearrange("a p x -> (a p) x")).then_inc(w_in[i], DMA)

            @block.gpsimd
            def _(pool):
                nc.gpsimd.memset(ident[:], 0.0).then_inc(made, 1)
                pool.wait_ge(made, 1)
                nc.gpsimd.affine_select(out=ident[:], in_=ident[:], compare_op=ALU.not_equal, fill=1.0, base=0,
                                        pattern=[[-1, P]], channel_multiplier=1).then_inc(made, 1)
                for i in range(NB):
                    pool.dma_start(xe[i][:], buf_dram[i * CAP:(i + 1) * CAP, :]).then_inc(x_in[i], DMA)
                with pool.Fori(1, E // NB) as q:
                    r0 = pool.snap(q * (NB * CAP))
                    for i in range(NB):
                        pool.wait_ge(x_turned, (q - 1) * NB + i + 1)
                        pool.dma_start(xe[i][:], buf_dram[bass.ds(r0 + i * CAP, CAP), :]).then_inc(x_in[i], DMA)

            @block.tensor
            def _(pe):
                pe.wait_ge(made, 2)

                def turn(q, i):
                    pe.wait_ge(x_in[i], q * DMA + DMA)
                    pe.wait_ge(xt_cp, q * NB)
                    for k in range(KT):
                        last = nc.tensor.transpose(ps_x[i // 2][:, i % 2, k * CAP:(k + 1) * CAP], xe[i][:, k * P:(k + 1) * P],
                                                   ident[0:CAP, 0:CAP])
                    last.then_inc(x_turned, 1)

                def up(q, i):
                    pe.wait_ge(w_in[i], q * (2 * DMA) + 2 * DMA)
                    pe.wait_ge(xt_cp, q * NB + i + 1)
                    pe.wait_ge(h_done, q * NB)
                    for g in range(2):
                        for half in range(2):
                            for k in range(KT):
                                last = nc.tensor.matmul(ps_e[i][:, g, half * CAP:(half + 1) * CAP],
                                                        wgu[i][:, k, g, half * MH:(half + 1) * MH], xt[i][:, k, :],
                                                        start=(k == 0), stop=(k == KT - 1))
                    last.then_inc(up_mm, 1)

                def down(q, i):
                    pe.wait_ge(h_done, q * NB + i + 1)
                    pe.wait_ge(y_cp, q * NB + max(i - 1, 0))
                    for half in range(2):
                        last = nc.tensor.matmul(ps_y[i % 2][0:CAP, 0, :], hh[i][:, half, :], wd[i][:, half, :],
                                                start=(half == 0), stop=(half == 1))
                    last.then_inc(down_mm, 1)

                with pe.Fori(0, E // NB) as q:
                    for i in range(NB):
                        turn(q, i)
                    up(q, 0)
                    for i in range(1, NB):
                        up(q, i)
                        down(q, i - 1)
                    down(q, NB - 1)

            @block.scalar
            def _(act):
                with act.Fori(0, E // NB) as q:
                    r0 = act.snap(q * (NB * CAP))

                    def store(i):
                        act.wait_ge(y_out[i], q * DMA)
                        act.wait_ge(down_mm, q * NB + i + 1)
                        nc.scalar.copy(yo[i][:], ps_y[i % 2][0:CAP, 0, :]).then_inc(y_cp, 1)
                        act.wait_ge(y_cp, q * NB + i + 1)
                        act.dma_start(eo_dram[bass.ds(r0 + i * CAP, CAP), :], yo[i][:]).then_inc(y_out[i], DMA)

                    for i in range(NB):
                        act.wait_ge(up_mm, q * NB + i + 1)
                        nc.scalar.activation(sg[i][:].rearrange("p h c -> p (h c)"), ps_e[i][:, 0, 0:2 * CAP],
                                             ACT.Sigmoid).then_inc(sig_done, 1)
                        if i >= 1:
                            store(i - 1)
                    store(NB - 1)
                for i in range(NB):
                    act.wait_ge(y_out[i], DMA * E // NB)

            @block.vector
            def _(dve):
                with dve.Fori(0, E // NB) as q:
                    for i in range(NB):
                        dve.wait_ge(x_turned, q * NB + i // 2 * 2 + 2)
                        nc.vector.tensor_copy(xt[i][:].rearrange("p k c -> p (k c)"),
                                              ps_x[i // 2][:, i % 2, 0:KT * CAP]).then_inc(xt_cp, 1)
                    for i in range(NB):
                        h = hh[i][:].rearrange("p h c -> p (h c)")
                        dve.wait_ge(down_mm, q * NB)
                        dve.wait_ge(sig_done, q * NB + i + 1)
                        nc.vector.tensor_tensor(out=h, in0=sg[i][:].rearrange("p h c -> p (h c)"), in1=ps_e[i][:, 0, 0:2 * CAP],
                                                op=ALU.mult).then_inc(silu_done, 1)
                        dve.wait_ge(silu_done, q * NB + i + 1)
                        nc.vector.tensor_tensor(out=h, in0=h, in1=ps_e[i][:, 1, 0:2 * CAP], op=ALU.mult).then_inc(h_done, 1)

        with ExitStack() as ctx:
            m = Pool(nc, ctx)
            NG = 4
            got = [m.sb(f"p5_got{i}", [P, TOPK, D]) for i in range(NG)]
            ysum = [m.sb(f"p5_ysum{i}", [P, D]) for i in range(2)]
            yf = [m.sb(f"p5_yf{i}", [P, D]) for i in range(2)]
            neg_half = m.sb("p5_neg_half", [P, 2])
            rstats = m.sb("p5_rstats", [P, 2, 6])
            rm, rr, rt = (m.sb(f"p5_r{n}", [P, 2]) for n in "mrt")
            made, steps = m.sem("p5_made3"), m.sem("p5_steps3")
            fetched = [m.sem(f"p5_fetched{i}") for i in range(NG)]
            summed = m.sem("p5_summed")
            row_var, row_rstd, y_ready = m.sem("p5_row_var"), m.sem("p5_row_rstd"), m.sem("p5_y_ready")
            y_out = [m.sem(f"p5_f_out{i}") for i in range(2)]
            block = ctx.enter_context(nc.Block())

            @block.gpsimd
            def _(pool):
                nc.gpsimd.memset(neg_half[:], -0.5).then_inc(made, 1)
                pool.wait_ge(made, 1)

                def rstd(p):
                    pool.wait_ge(row_var, p + 1)
                    nc.gpsimd.tensor_tensor(out=rr[:], in0=rr[:], in1=neg_half[:], op=ALU.pow).then_inc(row_rstd, 1)

                for i in range(NT):
                    if i >= NG:
                        pool.wait_ge(summed, i - NG + 1)
                    for k in range(TOPK):
                        nc.gpsimd.indirect_dma_start(
                            out=got[i % NG][:, k, :], out_offset=None, in_=eo_dram,
                            in_offset=bass.IndirectOffsetOnAxis(ap=slot_i[:, k, i:i + 1], axis=0)).then_inc(fetched[i % NG], DMA)
                    if i % 2 and i >= 3:
                        rstd(i // 2 - 1)
                rstd(NT // 2 - 1)

            @block.vector
            def _(dve):
                n_row = 2 * (1 + TOPK) + MOMENT_STEPS
                with dve.Fori(0, NT // NG) as q:
                    st = Steps(dve, steps, q * (2 * n_row))
                    for p in range(NG // 2):
                        pair = []
                        for b in range(2):
                            g = 2 * p + b
                            dve.wait_ge(fetched[g], q * (TOPK * DMA) + TOPK * DMA)
                            y = acc[:, bass.ds(q * NG + g, 1), :].rearrange("p a n -> p (a n)")
                            sh = shared[:, bass.ds(q * NG + g, 1), :].rearrange("p a n -> p (a n)")
                            pair.append([y, sh, g])
                        last = [0, 0]
                        for k in range(TOPK):
                            for b, (y, sh, g) in enumerate(pair):
                                if k:
                                    st.after(last[b])
                                ins = nc.vector.scalar_tensor_tensor(
                                    out=sh, in0=got[g][:, k, :], scalar=wk[:, k, bass.ds(q * NG + g, 1)],
                                    in1=sh, op0=ALU.mult, op1=ALU.add)
                                last[b] = st.done(ins)
                        for b, (y, sh, g) in enumerate(pair):
                            st.after(last[b])
                            dve.wait_ge(y_ready, q * NG + 2 * p)
                            nc.vector.tensor_tensor(out=ysum[b][:], in0=y, in1=sh, op=ALU.add).then_inc(summed, 1)
                        for b, (y, sh, g) in enumerate(pair):
                            dve.wait_ge(summed, q * NG + g + 1)
                            done = st.done(nc.vector.bn_stats(out=rstats[:, b, :], in_=ysum[b][:]))
                        st.after(done)
                        moments(nc, st, rstats[:], rm[:], rr[:], rt[:], D)
                        dve.sem_inc(row_var, 1)
                        dve.wait_ge(row_rstd, q * (NG // 2) + p + 1)
                        for b, (y, sh, g) in enumerate(pair):
                            dve.wait_ge(y_out[b], q * (NG // 2 * DMA) + p * DMA)
                            nc.vector.tensor_scalar(yf[b][:], ysum[b][:], rm[:, b:b + 1], rr[:, b:b + 1], ALU.subtract,
                                                    ALU.mult).then_inc(y_ready, 1)
                    assert st.n == 2 * n_row, (st.n, n_row)

            @block.sync
            def _(sp):
                with sp.Fori(0, NT // 2) as p:
                    row = sp.snap(p * 2)
                    for b in range(2):
                        sp.wait_ge(y_ready, p * 2 + b + 1)
                        sp.dma_start(out[bass.ds(row + b, 1)].rearrange("a t n -> (a t) n"), yf[b][:]).then_inc(y_out[b], DMA)
                for b in range(2):
                    sp.wait_ge(y_out[b], DMA * NT // 2)


INPUTS = ("x", "xT", "w_heads", "ba", "wbT", "bb_col", "bb_row", "wgT", "woT", "ln_g", "ln_b", "ctxR", "kpad", "dcol",
          "gwT", "sguT", "sdT", "wguT", "wdT")


def decoder_layer(nc, i, out):
    def scratch(name, *shape):
        return nc.dram_tensor(name, list(shape), FP32).ap()

    a, bv = scratch("decays", B, H, T, DH), scratch("beta_v", B, H, T, DH)
    gram, beta = scratch("gram", B, H, T, 2 * T), scratch("beta", B, H, T)
    hist = scratch("history", 2, T - C, P, DH)
    o = scratch("heads_out", B, H, T, DH + 32)
    x1, x1T = scratch("x1", B, T, D), scratch("x1T", D, TOK)
    x2, x2T = scratch("x2", B, T, D), scratch("x2T", D, TOK)
    projections(nc, i["xT"], i["w_heads"], i["ba"], i["wbT"], i["bb_col"], i["bb_row"], a, bv, gram, beta)
    recurrence(nc, a, bv, gram, beta, hist, o)
    attention_out(nc, i["x"], i["xT"], o, i["wgT"], i["woT"], i["ln_g"], i["ln_b"], x1, x1T)
    long_conv(nc, i["ctxR"], i["kpad"], i["dcol"], x1, x1T, scratch("filters", HK, 3 * P), x2, x2T)
    experts(nc, x2, x2T, i["gwT"], i["sguT"], i["sdT"], i["wguT"], i["wdT"],
            scratch("expert_in", SLOTS, D), scratch("expert_out", SLOTS, D), out)


def host_layout(i):
    def c(a):
        return np.ascontiguousarray(a)
    x = np.asarray(i["x"])
    g = {k[len("L0_attn_"):]: np.asarray(v) for k, v in i.items() if k.startswith("L0_attn_")}
    w = np.stack([g[n].reshape(H, P, KT, P) for n in ("Wk", "Wq", "Wv", "Wa")])
    par = np.stack([np.concatenate([g[n + "_w"][:, 0, :], g[n + "_b"][:, None]], 1).reshape(H, P, TAPS + 1)
                    for n in ("kc", "qc", "vc")])
    ctx = np.asarray(i["ctx_2048"]).reshape(B, P, KT, P)[:, :, :, ::-1].transpose(3, 2, 0, 1)
    kpad = np.zeros((HK, 3 * P), np.float32)
    kpad[:, P - 1:P - 1 + D] = np.asarray(i["L0_xattn_ssm_kernel"])
    f = {k[len("L0_ffn_"):]: np.asarray(v) for k, v in i.items() if k.startswith("L0_ffn_")}
    wgu = np.stack([f["Wg"], f["Wu"]]).reshape(2, E, M, KT, P).transpose(1, 4, 3, 0, 2).reshape(E, P, -1)
    wd = f["Wd"].reshape(E, D, 2, M // 2).transpose(0, 3, 2, 1).reshape(E, M // 2, -1)
    sgu = np.stack([f["Sg"], f["Su"]]).reshape(2, MS, KT, P).transpose(3, 2, 0, 1)
    sd = f["Sd"].reshape(D, MS // (M // 2), M // 2).transpose(2, 1, 0)
    return dict(
        gwT=c(f["gate_weight"].T), sguT=c(sgu), sdT=c(sd), wguT=c(wgu), wdT=c(wd),
        ctxR=c(ctx), kpad=kpad, dcol=c(np.asarray(i["L0_xattn_D"])[:, None]),
        xT=c(x.reshape(TOK, D).T), w_heads=c(np.concatenate([w.transpose(1, 4, 3, 0, 2).reshape(H, P, -1), par.transpose(1, 2, 0, 3).reshape(H, P, -1)], 2)),
        ba=c(g["ba"][None, :]), wbT=c(g["Wb"].T), bb_col=c(g["bb"][:, None]), bb_row=c(g["bb"][None, :]),
        x=c(x), wgT=c(g["Wg"].T), woT=c(g["Wo"].T), ln_g=c(g["ln_g"][:, None]), ln_b=c(g["ln_b"][:, None]),
    )


def kernel(**inputs):
    import concourse.bacc as bacc
    from concourse.bass_utils import run_bass_kernel_spmd

    laid = host_layout(inputs)
    nc = bacc.Bacc("TRN2", target_bir_lowering=False, num_devices=1)
    handles = {n: nc.dram_tensor(f"in_{n}", laid[n].shape, mybir.dt.from_np(laid[n].dtype), kind="ExternalInput").ap()
               for n in INPUTS}
    out = nc.dram_tensor("out_0", (B, T, D), FP32, kind="ExternalOutput").ap()
    decoder_layer(nc, handles, out)
    r = run_bass_kernel_spmd(nc, [{f"in_{n}": laid[n] for n in INPUTS}], core_ids=[0])
    return r.results[0]["out_0"]
```
